# Optimizing a Trainium2 kernel written in Bass

```python
import numpy as np
import jax
import jax.numpy as jnp

def _softmax(x, axis=-1):
    return jax.nn.softmax(x, axis=axis)

def _gelu(x):
    return jax.nn.gelu(x, approximate=True)

def _silu(x):
    return jax.nn.silu(x)

def _sigmoid(x):
    return jax.nn.sigmoid(x)

def _layernorm(x, axis=-1, eps=1e-05):
    m = jnp.mean(x, axis=axis, keepdims=True)
    v = jnp.var(x, axis=axis, keepdims=True)
    return (x - m) / jnp.sqrt(v + eps)

def _scatter_add(tgt, idx, src, axis=0):
    return tgt.at[idx].add(src)

def _segment_sum(src, seg, n):
    return jax.ops.segment_sum(src, seg, n)
kernel_name = 'mk_decoder_preln_d1_seqx_r4_385c3f'

def setup_inputs(seed: int=0):
    np.random.seed(seed)
    _w = jnp.asarray

    def _rec_inputs():
        import jax
        import jax.numpy as jnp
        _rk = jax.random.key(seed)
        x = 0.0003765 + 1 * jax.random.normal(jax.random.fold_in(_rk, 1), (8, 256, 512), jnp.float32)
        _lenS = 256 - jax.random.randint(jax.random.fold_in(_rk, 7), (8,), 0, max(1, 256 // 4) + 1, jnp.int32)
        _lenS2 = 256 - jax.random.randint(jax.random.fold_in(_rk, 8), (8,), 0, max(1, 256 // 4) + 1, jnp.int32)
        _ctx_2048P = jax.random.normal(jax.random.fold_in(_rk, 11), (8, 16, 512), jnp.float32)
        _ctx_2048c = jax.random.dirichlet(jax.random.fold_in(_rk, 511), 0.3 * jnp.ones((16,), jnp.float32), (8, 256))
        _ctx_2048t = jnp.einsum('bsk,bkd->bsd', _ctx_2048c, _ctx_2048P)
        _ctx_2048t = _ctx_2048t * jax.lax.rsqrt(jnp.mean(jnp.square(_ctx_2048t)) + 1e-12) * 0.953939
        ctx_2048 = -0.000292821 + 1.00034 * (_ctx_2048t + 0.3 * jax.random.normal(jax.random.fold_in(_rk, 611), (8, 256, 512), jnp.float32))
        return (x, ctx_2048)
    x, ctx_2048 = _rec_inputs()

    def _L0_attn_setup():
        import jax, jax.numpy as jnp
        import numpy as np
        import math
        E = 512
        H = 16
        D = E // H

        def _alibi_slopes(n):

            def pow2_slopes(n):
                start = 2 ** (-2 ** (-(math.log2(n) - 3)))
                return [start * start ** i for i in range(n)]
            if math.log2(n).is_integer():
                return pow2_slopes(n)
            c = 2 ** math.floor(math.log2(n))
            return pow2_slopes(c) + _alibi_slopes(2 * c)[::2][:n - c]

        def _alibi_bias(seq_len):
            slopes = jnp.asarray(_alibi_slopes(H), dtype=jnp.float32)
            pos = jnp.arange(seq_len)
            rel = jnp.abs(pos[None, :] - pos[:, None]).astype(jnp.float32)
            return -slopes[:, None, None] * rel[None, :, :]
        key = jax.random.key(seed)
        ks = jax.random.split(key, 5)
        B, S = (2, 512)
        scale = 1.0 / math.sqrt(E)
        x = jax.random.normal(ks[0], (B, S, E), dtype=jnp.float32)
        Wq = jax.random.normal(ks[1], (E, E), dtype=jnp.float32) * scale
        Wk = jax.random.normal(ks[2], (E, E), dtype=jnp.float32) * scale
        Wv = jax.random.normal(ks[3], (E, E), dtype=jnp.float32) * scale
        Wo = jax.random.normal(ks[4], (E, E), dtype=jnp.float32) * scale
        z = jnp.zeros((E,), dtype=jnp.float32)
        return {'x': x, 'Wq': Wq, 'bq': z, 'Wk': Wk, 'bk': z, 'Wv': Wv, 'bv': z, 'Wo': Wo, 'bo': z}
    _L0_attn_all = _L0_attn_setup()
    _L0_attn_in = {k: v for k, v in _L0_attn_all.items() if k in ('Wq', 'bq', 'Wk', 'bk', 'Wv', 'bv', 'Wo', 'bo')}
    del _L0_attn_all

    def _L0_xattn_setup():
        import jax, jax.numpy as jnp
        import numpy as np
        key = jax.random.key(seed)
        k1, k2, k3, k4, k5 = jax.random.split(key, 5)
        B, D_MODEL, L = (2, 256, 512)
        HEAD_DIM = 8
        H = D_MODEL // HEAD_DIM
        return {'k': jax.random.normal(k1, (B, D_MODEL, L), dtype=jnp.float32), 'v': jax.random.normal(k2, (B, D_MODEL, L), dtype=jnp.float32), 'q': jax.random.normal(k3, (B, D_MODEL, L), dtype=jnp.float32), 'ssm_kernel': jax.random.normal(k4, (H, L), dtype=jnp.float32), 'D': jax.random.normal(k5, (H,), dtype=jnp.float32), 'head_dim': HEAD_DIM}
    _L0_xattn_all = _L0_xattn_setup()
    _L0_xattn_in = {k: v for k, v in _L0_xattn_all.items() if k in ('ssm_kernel', 'D')}
    del _L0_xattn_all

    def _L0_ffn_setup():
        import jax, jax.numpy as jnp
        import numpy as np
        B, S, H = (1, 512, 512)
        E, FE, K = (8, 352, 2)
        key = jax.random.key(seed)
        k0, k1, k2, k3, k4 = jax.random.split(key, 5)
        s = 0.02
        return {'x': jax.random.normal(k0, (B, S, H), jnp.float32), 'w_router': jax.random.normal(k1, (E, H), jnp.float32) * s, 'w1': jax.random.normal(k2, (E, FE, H), jnp.float32) * s, 'w2': jax.random.normal(k3, (E, H, FE), jnp.float32) * s, 'w3': jax.random.normal(k4, (E, FE, H), jnp.float32) * s}
    _L0_ffn_all = _L0_ffn_setup()
    _L0_ffn_in = {k: v for k, v in _L0_ffn_all.items() if k in ('w_router', 'w1', 'w2', 'w3')}
    del _L0_ffn_all
    return {'x': x, 'ctx_2048': ctx_2048, 'L0_attn_Wq': _L0_attn_in['Wq'], 'L0_attn_bq': _L0_attn_in['bq'], 'L0_attn_Wk': _L0_attn_in['Wk'], 'L0_attn_bk': _L0_attn_in['bk'], 'L0_attn_Wv': _L0_attn_in['Wv'], 'L0_attn_bv': _L0_attn_in['bv'], 'L0_attn_Wo': _L0_attn_in['Wo'], 'L0_attn_bo': _L0_attn_in['bo'], 'L0_xattn_ssm_kernel': _L0_xattn_in['ssm_kernel'], 'L0_xattn_D': _L0_xattn_in['D'], 'L0_ffn_w_router': _L0_ffn_in['w_router'], 'L0_ffn_w1': _L0_ffn_in['w1'], 'L0_ffn_w2': _L0_ffn_in['w2'], 'L0_ffn_w3': _L0_ffn_in['w3']}

def reference(x, ctx_2048, L0_attn_Wq, L0_attn_bq, L0_attn_Wk, L0_attn_bk, L0_attn_Wv, L0_attn_bv, L0_attn_Wo, L0_attn_bo, L0_xattn_ssm_kernel, L0_xattn_D, L0_ffn_w_router, L0_ffn_w1, L0_ffn_w2, L0_ffn_w3):
    import jax
    import jax.numpy as jnp

    def _L0_attn_ref(x, Wq, bq, Wk, bk, Wv, bv, Wo, bo):
        import jax, jax.numpy as jnp
        import numpy as np
        import math
        E = 512
        H = 16
        D = E // H

        def _alibi_slopes(n):

            def pow2_slopes(n):
                start = 2 ** (-2 ** (-(math.log2(n) - 3)))
                return [start * start ** i for i in range(n)]
            if math.log2(n).is_integer():
                return pow2_slopes(n)
            c = 2 ** math.floor(math.log2(n))
            return pow2_slopes(c) + _alibi_slopes(2 * c)[::2][:n - c]

        def _alibi_bias(seq_len):
            slopes = jnp.asarray(_alibi_slopes(H), dtype=jnp.float32)
            pos = jnp.arange(seq_len)
            rel = jnp.abs(pos[None, :] - pos[:, None]).astype(jnp.float32)
            return -slopes[:, None, None] * rel[None, :, :]
        B, S, _ = x.shape

        def proj(W, b):
            return (x @ W.T + b).reshape(B, S, H, D).transpose(0, 2, 1, 3)
        q = proj(Wq, bq)
        k = proj(Wk, bk)
        v = proj(Wv, bv)
        scores = jnp.einsum('bhqd,bhkd->bhqk', q, k) / math.sqrt(D)
        causal = jnp.triu(jnp.ones((S, S), dtype=bool), k=1)
        scores = jnp.where(causal[None, None], -jnp.inf, scores)
        scores = scores + _alibi_bias(S)[None]
        probs = jax.nn.softmax(scores, axis=-1)
        out = jnp.einsum('bhqk,bhkd->bhqd', probs, v)
        out = out.transpose(0, 2, 1, 3).reshape(B, S, E)
        return out @ Wo.T + bo

    def _L0_xattn_ref(k, v, q, ssm_kernel, D, head_dim):
        import jax, jax.numpy as jnp
        import numpy as np
        B, HD, L = k.shape
        H = HD // head_dim
        fft_size = 2 * L
        k_ = k.reshape(B, H, head_dim, L)
        v_ = v.reshape(B, H, head_dim, L)
        q_ = q.reshape(B, H, head_dim, L)
        kv = jnp.einsum('bhil,bhjl->bijhl', k_, v_)
        kv_f = jnp.fft.rfft(kv, n=fft_size)
        kernel_f = jnp.fft.rfft(ssm_kernel, n=fft_size)
        y = jnp.fft.irfft(kv_f * kernel_f, n=fft_size)[..., :L]
        out = y + kv * D[None, None, None, :, None]
        out = jnp.einsum('bijhl,bhil->bjhl', out, q_)
        out = jnp.transpose(out, (0, 2, 1, 3)).reshape(B, H * head_dim, L)
        return out.astype(k.dtype)

    def _L0_ffn_ref(x, w_router, w1, w2, w3):
        import jax, jax.numpy as jnp
        import numpy as np
        B, S, H = (1, 512, 512)
        E, FE, K = (8, 352, 2)
        top_k = K
        batch = x.shape[0]
        hidden = x.shape[-1]
        num_experts = w1.shape[0]
        xf = x.reshape(-1, hidden)
        logits = xf @ w_router.T
        probs = jax.nn.softmax(logits, axis=-1)
        scores, idx = jax.lax.top_k(probs, top_k)
        scores = scores / jnp.sum(scores, axis=-1, keepdims=True)
        oh = jax.nn.one_hot(idx, num_experts, dtype=xf.dtype)
        cw = jnp.einsum('tk,tke->te', scores, oh)
        out = jnp.zeros_like(xf)
        for e in range(num_experts):
            y = jax.nn.silu(xf @ w1[e].T) * (xf @ w3[e].T) @ w2[e].T
            out = out + cw[:, e:e + 1] * y
        return out.reshape(batch, -1, hidden)
    x = x + _L0_attn_ref(_layernorm(x, axis=-1), L0_attn_Wq, L0_attn_bq, L0_attn_Wk, L0_attn_bk, L0_attn_Wv, L0_attn_bv, L0_attn_Wo, L0_attn_bo)
    x = x + _L0_xattn_ref(ctx_2048, ctx_2048, _layernorm(x, axis=-1), L0_xattn_ssm_kernel, L0_xattn_D, 8)
    x = x + _L0_ffn_ref(_layernorm(x, axis=-1), L0_ffn_w_router, L0_ffn_w1, L0_ffn_w2, L0_ffn_w3)
    return x

_drawn_inputs = setup_inputs


def setup_inputs(seed=0):
    import zlib

    import numpy as np

    out = dict(_drawn_inputs(seed))
    spreads = {'L0_attn_bq': (0.0, 0.1),
     'L0_attn_bk': (0.0, 0.8),
     'L0_attn_bv': (0.0, 0.1),
     'L0_attn_bo': (0.0, 0.1)}
    factors = {'L0_ffn_w_router': 8.0, 'L0_ffn_w1': 8.0, 'L0_ffn_w2': 8.0, 'L0_ffn_w3': 8.0}
    for name, (base, spread) in spreads.items():
        noise = np.random.default_rng([zlib.crc32(name.encode()), seed]).standard_normal(out[name].shape)
        drawn = base * np.exp(spread * noise) if base else spread * noise
        out[name] = jnp.asarray(drawn.astype(out[name].dtype))
    for name, factor in factors.items():
        out[name] = (out[name] * factor).astype(out[name].dtype)
    return out
```

```python
from contextlib import ExitStack

import concourse.bass as bass
from concourse import mybir

P = 128
B, S, E = 8, 256, 512
TILES = B * S // P
TB = S // P
EC = E // P
H, HD = 16, 32
HG = P // HD
MH, MD = 32, 8
DIAGS = MD // 2 + 1
PAIRS = DIAGS * MD
MW = MD + DIAGS - 1
MIRROR = DIAGS - 2
SKEW = MD + MIRROR
TERMS = MD * SKEW + MIRROR + 1
NX, F = 8, 352
FC = (F + P - 1) // P
FLAST = F - (FC - 1) * P
TOPK = 2
SLOT_TILES = 40
SLOTS = SLOT_TILES * P
EPS = 1e-5
KPAD = P - 1 + E
MASKED = -1e30

F32 = mybir.dt.float32
F32R = mybir.dt.float32r
I32 = mybir.dt.int32
U32 = mybir.dt.uint32
ALU = mybir.AluOpType
ACT = mybir.ActivationFunctionType
AX = mybir.AxisListType
KB = 1024

assert SLOT_TILES >= TILES * TOPK + NX - 1 and SLOT_TILES % 4 == 0


def decoder_block(nc, x, w_attn, b_qk, b_v, b_o, ctx_rev, kern_pad, skip_d, w_router, w_up, w_gate,
                  w_down, out):
    ctx = ExitStack()
    with ctx:
        arena = (nc.sbuf_base + 63) // 64 * 64

        def at(name, shape, kb, dt=F32):
            return nc.alloc_sbuf_tensor_at(name, shape, dt, offset=arena + int(kb * KB))

        def sem(name):
            return ctx.enter_context(nc.semaphore(name))

        X = at("X", [P, TILES, E], 0)
        QX = at("QX", [P, EC, B * S], 32)
        ident = at("ident", [P, P], 200)
        mhalf = at("mhalf", [P, TB], 200.5)
        carrier = at("carrier", [P, 64], 200.75)
        carried = [0, 0]
        wraw = at("wraw", [P, 4, EC, E], 32)
        whi = at("whi", [P, 4, EC, E], 64, F32R)
        wlo = at("wlo", [P, 4, EC, E], 96, F32R)
        HI_AT = (1, 2, 3, 0)
        bias_tab = at("bias_tab", [P, H, S], 128)
        hn = at("hn", [P, TB, E], 144)
        hn2 = at("hn2", [P, TB, E], 148)
        hTh = at("hTh", [P, EC, S], 152, F32R)
        hTl = at("hTl", [P, EC, S], 156, F32R)
        qT = at("qT", [P, H // HG, S], 160)
        kT = at("kT", [P, H // HG, S], 164)
        v = at("v", [P, TB, E], 168)
        NE = 4
        sc = at("sc", [P, NE, 3 * P], 172)
        pr = at("pr", [P, NE, 3 * P], 178)
        pT = at("pT", [P, NE, 3 * P], 184)
        bo_b = at("bo_b", [P, E], 190)
        bv_b = at("bv_b", [P, E], 192)
        dist = at("dist", [P, S], 194)
        dist_i = at("dist_i", [P, S], 195, I32)
        bqk_c = at("bqk_c", [P, 2, H // HG], 196)
        mx = at("mx", [P, H, TB], 196.25)
        nm = at("nm", [P, H, TB], 196.5)
        sums = at("sums", [P, H, TB], 196.75)
        rsum = at("rsum", [P, H, TB], 197)
        st1 = at("st1", [P, TB, 6], 197.25)
        mv1 = at("mv1", [P, TB, 2], 197.375)
        ve1 = at("ve1", [P, TB], 197.5)
        rs1 = at("rs1", [P, TB], 197.625)
        st2 = at("st2", [P, TB, 6], 197.75)
        mv2 = at("mv2", [P, TB, 2], 197.875)
        ve2 = at("ve2", [P, TB], 198)
        rs2 = at("rs2", [P, TB], 198.125)
        cx = at("cx", [P, EC * B, MH, MW], 72)
        NS = 4
        strip = at("strip", [P, NS, E], 120)
        KV = 4
        kv = at("kv", [P, KV, EC * B, PAIRS], 128)
        qe = at("qe", [P, 2, EC * B, MW], 64)
        terms = at("terms", [P, EC * B, TERMS], 148)
        anti = at("anti", [P, P], 201)
        d_b = at("d_b", [P, MH], 201.5)
        wd = at("wd", [P, NX, FC, E], 64)
        wg = at("wg", [P, NX, EC, F], 112)
        wu = at("wu", [P, NX, EC, F], 156)
        CB = 64
        h3 = at("h3", [P, 2, E], CB)
        h3T = at("h3T", [P, 2, EC, P], CB + 4)
        logits = at("logits", [P, TILES, NX], CB + 8)
        top = at("top", [P, TILES, 8], CB + 8.5)
        topi = at("topi", [P, TILES, 8], CB + 9, U32)
        topx = at("topx", [P, TILES, 8], CB + 9.5)
        padded = at("padded", [P, 2 * TILES, NX], CB + 10)
        picked = padded[:, TILES:2 * TILES, :]
        hot = at("hot", [P, TOPK, TILES, NX], CB + 11)
        zsum = at("zsum", [P, TILES], 202)
        zrec = at("zrec", [P, TILES], 202.0625)
        psum2 = at("psum2", [P, TILES], 202.125)
        prec2 = at("prec2", [P, TILES], 202.1875)
        gate = at("gate", [P, TILES, TOPK], 202.25)
        idxf = at("idxf", [P, TOPK, TILES], 202.375)
        slotf = at("slotf", [P, TOPK, TILES], 202.5)
        slot = at("slot", [P, TOPK, TILES], 202.625, I32)
        sdiv = at("sdiv", [P, TOPK, TILES], 202.75, I32)
        smod = at("smod", [P, TOPK, TILES], 202.875, I32)
        sdivf = at("sdivf", [P, TOPK, TILES], 203)
        smodf = at("smodf", [P, TOPK, TILES], 203.125)
        cnt = at("cnt", [P, NX], 203.25)
        count = at("count", [P, NX], 203.28125)
        ntile = at("ntile", [P, NX], 203.3125)
        cumt = at("cumt", [P, NX], 203.34375)
        base = at("base", [P, NX], 203.375)
        eidf = at("eidf", [P, SLOT_TILES], 203.5)
        eid = at("eid", [P, SLOT_TILES], 203.75, I32)
        idx = at("idx", [P, SLOT_TILES], 204, I32)
        tok = at("tok", [P, TILES], 204.25)
        iota8 = at("iota8", [P, NX], 204.3125)
        iota16 = at("iota16", [P, TILES], 204.34375)
        iota40 = at("iota40", [P, SLOT_TILES], 204.5)
        le8 = at("le8", [P, NX, NX], 204.75)
        st3 = at("st3", [P, 2, 6], 205)
        mv3 = at("mv3", [P, 2, 2], 205.0625)
        ve3 = at("ve3", [P, 2], 205.125)
        rs3 = at("rs3", [P, 2], 205.15625)
        gcol = at("gcol", [P, 4], 205.1875, U32)
        fcol = at("fcol", [P, 4, TOPK], 205.25, U32)
        tok_i = at("tok_i", [P, TILES], 205.3125, I32)
        i40_i = at("i40_i", [P, SLOT_TILES], 205.5, I32)
        wr = at("wr", [P, EC, NX], 205.75)
        iota128 = at("iota128", [P, P], 206.25)
        ranks = at("ranks", [P, TILES, NX], 206.75)
        ones = at("ones", [P, P], 32)
        upper = at("upper", [P, P], 32.5)
        cmp = at("cmp", [P, SLOT_TILES * NX], 33)
        hot_p = at("hot_p", [P, TOPK * TILES, P], 35)
        hot_j = at("hot_j", [P, TOPK * TILES, SLOT_TILES], 51)
        NG = 4
        xg = at("xg", [P, NG, E], 32)
        xgT = at("xgT", [P, 2, EC, P], 40)
        act = at("act", [P, 2, F], 44)
        gu = at("gu", [P, 2, F], 47)
        guT = at("guT", [P, 2, FC, P], 50)
        yo = at("yo", [P, 4, E], 53)
        ga = at("ga", [P, 4, TOPK, E], 64)
        res = at("res", [P, 4, E], 80)

        ps = ctx.enter_context(nc.psum_tensor("ps", [P, 8, 512], F32))

        h3_d = nc.dram_tensor("h3_rows", [B * S, E], F32, kind="Internal").ap()
        y_d = nc.dram_tensor("expert_rows", [SLOTS, E], F32, kind="Internal").ap()

        x_t = x.rearrange("b (t p) e -> p (b t) e", p=P)
        out_t = out.rearrange("b (t p) e -> p (b t) e", p=P)
        h3_t = h3_d.rearrange("(t p) e -> p t e", p=P)
        y_t = y_d.rearrange("(t p) e -> p t e", p=P)

        x_in0, x_in = sem("x_in0"), sem("x_in")
        w_in = [sem(f"w_in{m}") for m in range(4)]
        small_in = sem("small_in")
        wsplit_hi, wsplit_lo = sem("wsplit_hi"), sem("wsplit_lo")
        consts = sem("consts")
        tab_scaled, tab_ready = sem("tab_scaled"), sem("tab_ready")
        ln1 = {k: sem(f"ln1_{k}") for k in ("stats", "aggr", "var", "rstd", "out")}
        ln2 = {k: sem(f"ln2_{k}") for k in ("stats", "aggr", "var", "rstd", "out")}
        misc_full = sem("misc_full")
        ht_hi, ht_lo = sem("ht_hi"), sem("ht_lo")
        q_ready, k_ready, v_ready = sem("q_ready"), sem("k_ready"), sem("v_ready")
        s_full, s_read = sem("s_full"), sem("s_read")
        nm_ready, p_ready = sem("nm_ready"), sem("p_ready")
        pt_full, pt_dve, pt_act = sem("pt_full"), sem("pt_dve"), sem("pt_act")
        av_done, rsum_ready, o_ready = sem("av_done"), sem("rsum_ready"), sem("o_ready")
        xb_ready, x1_ready, qx_ready = sem("xb_ready"), sem("x1_ready"), sem("qx_ready")
        cx_in = sem("cx_in")
        strip_in = [sem(f"strip_in{r}") for r in range(NS)]
        strip_fixed, kv_ready, qe_ready = sem("strip_fixed"), sem("kv_ready"), sem("qe_ready")
        wrapped = sem("wrapped")
        y_full, y_read, mixed = sem("y_full"), sem("y_read"), sem("mixed")
        x2T_full, x2_ready = sem("x2T_full"), sem("x2_ready")
        ln3 = {k: sem(f"ln3_{k}") for k in ("stats", "aggr", "var", "rstd", "out")}
        h3_stored = [sem("h3_stored0"), sem("h3_stored1")]
        h3T_full, h3T_ready, logits_full = sem("h3T_full"), sem("h3T_ready"), sem("logits_full")
        tables = sem("tables")
        route, shifted, numer = sem("route"), sem("shifted"), sem("numer")
        picked_ready, ranks_full = sem("picked_ready"), sem("ranks_full")
        hot_ready, idx_full, idx_ready = sem("hot_ready"), sem("idx_full"), sem("idx_ready")
        wx_in, wx_late = sem("wx_in"), sem("wx_late")
        gcol_ready = sem("gcol_ready")
        gathered = [sem(f"gathered{r}") for r in range(4)]
        xT_full, xT_ready = sem("xT_full"), sem("xT_ready")
        up_full, gate_full = sem("up_full"), sem("gate_full")
        act_ready, gu_ready = sem("act_ready"), sem("gu_ready")
        guT_full, guT_ready = sem("guT_full"), sem("guT_ready")
        down_full, yo_ready = sem("down_full"), sem("yo_ready")
        y_stored = [sem(f"y_stored{r}") for r in range(4)]
        fcol_ready = sem("fcol_ready")
        fetched = [sem(f"fetched{r}") for r in range(4)]
        half_done, res_ready = sem("half_done"), sem("res_ready")
        sent = [sem(f"sent{r}") for r in range(4)]
        block = ctx.enter_context(nc.Block())

        MISC = (0, 1)
        SB = (2, 3)
        PB = (4, 5)
        OB = (6, 7)
        Q0, K0, V0 = 0, H // HG, 2 * (H // HG)
        FIRST_UNITS, TURN_UNITS = 2 * (H // HG) + TB + TB, 2 * (H // HG) + 4 * TB + TB

        def units_before(b, first):
            return TB if first else TB + FIRST_UNITS + (b - 1) * TURN_UNITS

        UNITS_END = TB + FIRST_UNITS + (B - 1) * TURN_UNITS - TB

        def positions(first, last):
            n = V0 + TB
            pos = {}
            if not first:
                pos["oT"], pos["wo"] = n, n + TB
                n += 2 * TB
            if not last:
                pos["hT"] = n
                n += TB
            if not first:
                pos["x1T"] = n
            return pos

        def bank(n):
            return MISC[n % 2]

        def pt_on_act(h):
            return h % 4 == 3

        def pt_count(b, h, act_engine):
            n = (h + 1) // 4 if act_engine else h + 1 - (h + 1) // 4
            return (H // 4 if act_engine else H - H // 4) * b + n

        def windows(a, dims, start=0):
            return bass.AP(tensor=a.tensor, offset=a.offset + start, ap=[list(a.ap[0])] + dims)

        def mixer_rows(h):
            q = QX[:, :, :].rearrange("p c (b h i) -> p (c b) h i", b=B, h=MH)
            return q[:, :, bass.ds(h, 1), :].squeeze(2)

        def convolved(r):
            return ps[:, 4 * (r % 2):4 * (r % 2) + 4, :].rearrange("p c (b k) -> p (c b) k", b=B)

        @block.sync
        def _(sp):
            sp.dma_start(X[:, 0:TB, :], x_t[:, 0:TB, :]).then_inc(x_in0, 16)
            for m in range(4):
                sp.dma_start(wraw[:, m, :, :], w_attn[m]).then_inc(w_in[m], 16)
                if m == 0:
                    sp.dma_start(bqk_c[:, :, :], b_qk).then_inc(small_in, 16)
                    sp.dma_start(bv_b[:, :], b_v.partition_broadcast(P)).then_inc(small_in, 16)
                    sp.dma_start(bo_b[:, :], b_o.partition_broadcast(P)).then_inc(small_in, 16)
                    sp.dma_start(d_b[:, :], skip_d.partition_broadcast(P)).then_inc(small_in, 16)
                    sp.dma_start(wr[:, :, :], w_router).then_inc(small_in, 16)
            sp.dma_start(X[:, TB:TILES, :], x_t[:, TB:TILES, :]).then_inc(x_in, 16)

            sp.wait_ge(q_ready, 4 * B)
            sp.wait_ge(k_ready, 4 * B)
            sp.wait_ge(v_ready, TB * B)
            sp.dma_start(cx[:, :, :, :], ctx_rev).then_inc(cx_in, 16)

            def load_strip(h, r, first=False):
                if not first:
                    sp.wait_ge(y_full, h - NS + 1)
                src = kern_pad[bass.ds(h, 1), :]
                src = bass.AP(tensor=src.tensor, offset=src.offset, ap=[[1, P], [1, E]])
                sp.dma_start(strip[:, r, :], src).then_inc(strip_in[r], 16)

            sp.wait_ge(x1_ready, TB * B)
            for h in range(NS):
                load_strip(h, h, first=True)
            sp.wait_ge(qx_ready, TILES)
            with sp.Fori(1, MH // NS) as i:
                for r in range(NS):
                    load_strip(NS * i + r, r)
                sp.dma_start(wu[:, bass.ds(i, 1), :, :], w_up[:, bass.ds(i, 1), :, :]).then_inc(wx_in, 16)

            LATE = 2
            sp.wait_ge(mixed, MH)
            sp.dma_start(wu[:, 0, :, :], w_up[:, 0, :, :]).then_inc(wx_in, 16)
            for t in range(TILES):
                if t % 2:
                    sp.dma_start(wg[:, t // 2, :, :], w_gate[:, t // 2, :, :]).then_inc(wx_in, 16)
                elif t // 2 >= LATE:
                    sp.dma_start(wd[:, t // 2, :, :], w_down[:, t // 2, :, :]).then_inc(wx_in, 16)
                sp.wait_ge(ln3["out"], t + 1)
                sp.dma_start(h3_t[:, t, :], h3[:, t % 2, :]).then_inc(h3_stored[t % 2], 16)
            sp.wait_ge(idx_ready, 1)
            sp.dma_start(wd[:, 0:LATE, :, :], w_down[:, 0:LATE, :, :]).then_inc(wx_late, 16)
            with sp.Fori(0, SLOT_TILES // 4) as i:
                for r in range(4):
                    sp.wait_ge(yo_ready, 4 * i + r + 1)
                    sp.dma_start(y_t[:, bass.ds(4 * i + r, 1), :], yo[:, r:r + 1, :])\
                        .then_inc(y_stored[r], 16)
            with sp.Fori(0, TILES // 4) as i:
                for r in range(4):
                    sp.wait_ge(res_ready, 4 * i + r + 1)
                    sp.dma_start(out_t[:, bass.ds(4 * i + r, 1), :], res[:, r:r + 1, :])\
                        .then_inc(sent[r], 16)
            for r in range(4):
                sp.wait_ge(sent[r], 16 * (TILES // 4))

        @block.gpsimd
        def _(pool):
            pool.memset(ident[:, :], 0.0).then_inc(consts, 1)
            pool.memset(mhalf[:, :], -0.5).then_inc(consts, 1)
            pool.iota(dist_i[:, :], pattern=[[1, S]], base=-P, channel_multiplier=-1).then_inc(consts, 1)
            pool.wait_ge(consts, 3)
            pool.affine_select(out=ident[:, :], in_=ident[:, :], compare_op=ALU.not_equal, fill=1.0,
                               base=0, pattern=[[-1, P]], channel_multiplier=1).then_inc(consts, 1)
            pool.tensor_copy(dist[:, :], dist_i[:, :]).then_inc(consts, 1)

            def carry():
                carried[1] = (carried[1] + 1) % 16
                pool.tensor_tensor(carrier[:, 48 + carried[1]:49 + carried[1]], mhalf[:, 0:1], mhalf[:, 0:1], ALU.add)

            def rstd(ln, var, dst, n):
                pool.wait_ge(ln["var"], n + 1)
                pool.tensor_tensor(dst[:, :], var[:, :], mhalf[:, :], ALU.pow).then_inc(ln["rstd"], 1)

            def add_bo(b):
                pool.wait_ge(ln1["out"], TB * b + TB)
                xs = X[:, bass.ds(TB * b, TB), :]
                pool.tensor_tensor(xs, xs, bo_b[:, :].unsqueeze(1).to_broadcast([P, TB, E]),
                                   ALU.add).then_inc(xb_ready, 1)

            rstd(ln1, ve1, rs1, 0)
            pool.iota(tok_i[:, :], pattern=[[P, TILES]], base=0, channel_multiplier=1).then_inc(tables, 1)
            pool.iota(i40_i[:, :], pattern=[[1, SLOT_TILES]], base=0, channel_multiplier=0)\
                .then_inc(tables, 1)
            pool.iota(iota128[:, :], pattern=[[1, P]], base=0, channel_multiplier=0,
                      allow_small_or_imprecise_dtypes=True).then_inc(tables, 1)
            pool.memset(le8[:, :, :], 1.0).then_inc(tables, 1)
            pool.wait_ge(tables, 4)
            pool.tensor_copy(tok[:, :], tok_i[:, :]).then_inc(tables, 1)
            pool.tensor_copy(iota40[:, :], i40_i[:, :]).then_inc(tables, 1)
            pool.tensor_copy(iota8[:, :], i40_i[:, 0:NX]).then_inc(tables, 1)
            pool.affine_select(out=le8[:, :, :], in_=le8[:, :, :], compare_op=ALU.is_ge, fill=0.0,
                               base=0, pattern=[[1, NX], [-1, NX]], channel_multiplier=0)\
                .then_inc(tables, 1)
            pool.wait_ge(tab_scaled, H)
            pool.affine_select(out=bias_tab[:, :, :], in_=bias_tab[:, :, :], compare_op=ALU.is_ge,
                               fill=MASKED, base=P, pattern=[[0, H], [-1, S]],
                               channel_multiplier=1).then_inc(tab_ready, 1)
            pool.wait_ge(small_in, 16 * 5)
            add_bo(0)

            def turn(b, first=False, last=False):
                if not last:
                    rstd(ln1, ve1, rs1, b + 1)
                    add_bo(b + 1)
                if not first:
                    rstd(ln2, ve2, rs2, b - 1)

            turn(0, first=True)
            with pool.Fori(1, B - 1) as b:
                turn(b)
            turn(B - 1, last=True)
            rstd(ln2, ve2, rs2, B - 1)


            pool.wait_ge(x1_ready, TB * B)
            pool.wait_ge(av_done, H * B)
            pool.memset(anti[:, :], 0.0).then_inc(consts, 1)
            pool.wait_ge(consts, 6)
            pool.affine_select(out=anti[:, :], in_=anti[:, :], compare_op=ALU.not_equal, fill=1.0,
                               base=-(P - 1), pattern=[[1, P]], channel_multiplier=1).then_inc(consts, 1)
            pool.wait_ge(cx_in, 16)

            def products(h, r, free):
                if free:
                    pool.wait_ge(y_full, h - KV + 1)
                c = cx[:, :, bass.ds(h, 1), :].squeeze(2)
                pool.tensor_tensor(kv[:, r, :, :].rearrange("p n (d i) -> p n d i", d=DIAGS),
                                   c[:, :, 0:MD].unsqueeze(2).to_broadcast([P, EC * B, DIAGS, MD]),
                                   windows(c, [[MW * MH, EC * B], [1, DIAGS], [1, MD]]),
                                   ALU.mult).then_inc(kv_ready, 1)

            for h in range(KV):
                products(h, h, False)
            with pool.Fori(1, MH // KV) as i:
                for r in range(KV):
                    products(KV * i + r, r, True)

            for t in range(TILES):
                c = t % 2
                pool.wait_ge(ln3["var"], t + 1)
                pool.tensor_tensor(rs3[:, c:c + 1], ve3[:, c:c + 1], mhalf[:, 0:1], ALU.pow)\
                    .then_inc(ln3["rstd"], 1)
            pool.wait_ge(x2T_full, TILES)
            pool.memset(ones[:, :], 1.0).then_inc(tables, 1)
            pool.memset(upper[:, :], 1.0).then_inc(tables, 1)
            pool.memset(padded[:, 0:TILES, :], 0.0).then_inc(tables, 1)
            pool.wait_ge(tables, 11)
            pool.affine_select(out=upper[:, :], in_=upper[:, :], compare_op=ALU.is_gt, fill=0.0,
                               base=0, pattern=[[1, P]], channel_multiplier=-1).then_inc(tables, 1)

            pool.wait_ge(idx_ready, 1)
            for r in range(2):
                pool.wait_ge(h3_stored[r], 16 * (TILES // 2))

            def gather(j, r, free):
                if free:
                    pool.wait_ge(xT_full, j - 3)
                pool.tensor_copy(gcol[:, r:r + 1], idx[:, bass.ds(j, 1)]).then_inc(gcol_ready, 1)
                pool.wait_ge(gcol_ready, j + 1)
                carry()
                pool.indirect_dma_start(
                    out=xg[:, r, :], out_offset=None, in_=h3_d[:, :],
                    in_offset=bass.IndirectOffsetOnAxis(ap=gcol[:, r:r + 1], axis=0),
                ).then_inc(gathered[r], 16)

            for r in range(4):
                gather(r, r, False)
            with pool.Fori(1, SLOT_TILES // 4) as i:
                for r in range(4):
                    gather(4 * i + r, r, True)

            for r in range(4):
                pool.wait_ge(y_stored[r], 16 * (SLOT_TILES // 4))

            def fetch(t, r, free):
                if free:
                    pool.wait_ge(res_ready, t - 3)
                pool.tensor_copy(fcol[:, r, :], slot[:, :, bass.ds(t, 1)].squeeze(2))\
                    .then_inc(fcol_ready, 1)
                pool.wait_ge(fcol_ready, t + 1)
                carry()
                for k in range(TOPK):
                    pool.indirect_dma_start(
                        out=ga[:, r, k, :], out_offset=None, in_=y_d[:, :],
                        in_offset=bass.IndirectOffsetOnAxis(ap=fcol[:, r, k:k + 1], axis=0),
                    ).then_inc(fetched[r], 16)

            for r in range(4):
                fetch(r, r, False)
            with pool.Fori(1, TILES // 4) as i:
                for r in range(4):
                    fetch(4 * i + r, r, True)

        @block.scalar
        def _(act_e):
            def hT_hi(n, pos_n, first_unit):
                for t in range(TB):
                    act_e.wait_ge(misc_full, n + t + 1)
                    act_e.activation(hTh[:, :, P * t:P * t + P],
                                     ps[:, bank(pos_n + t), :].rearrange("p (c q) -> p c q", c=EC),
                                     ACT.Copy).then_inc(ht_hi, 1)

            def move_pT(b, h):
                act_e.wait_ge(pt_full, H * b + h + 1)
                act_e.activation(pT[:, h % NE, :], ps[:, PB[h % 2], 0:3 * P],
                                 ACT.Copy).then_inc(pt_act, 1)

            def exps(b, g):
                act_e.wait_ge(nm_ready, H // 2 * b + g + 1)
                for h in (2 * g, 2 * g + 1):
                    if h >= NE:
                        act_e.wait_ge(pt_full, H * b + h - NE + 1)
                    act_e.activation(pr[:, h % NE, 0:P], sc[:, h % NE, 0:P], ACT.Exp,
                                     bias=nm[:, h, 0:1], accum_out=sums[:, h, 0:1])
                    act_e.activation(pr[:, h % NE, P:3 * P], sc[:, h % NE, P:3 * P], ACT.Exp,
                                     bias=nm[:, h, 1:2], accum_out=sums[:, h, 1:2]).then_inc(p_ready, 1)

            def x1T(b, n, pos_n):
                for t in range(TB):
                    act_e.wait_ge(misc_full, n + t + 1)
                    act_e.activation(QX[:, :, bass.ds(S * b + P * t, P)],
                                     ps[:, bank(pos_n + t), :].rearrange("p (c q) -> p c q", c=EC),
                                     ACT.Copy).then_inc(qx_ready, 1)

            for m in range(4):
                act_e.wait_ge(w_in[m], 16)
                act_e.activation(whi[:, HI_AT[m], :, :], wraw[:, m, :, :], ACT.Copy).then_inc(wsplit_hi, 1)
                if m == 0:
                    hT_hi(0, 0, 0)

            def turn(b, first=False, last=False):
                u = units_before(b, first)
                pos = positions(first, last)
                if first:
                    act_e.wait_ge(small_in, 16 * 5)
                for g in range(H // HG):
                    n = K0 + g
                    act_e.wait_ge(misc_full, u + n + 1)
                    act_e.activation(kT[:, g, :], ps[:, bank(n), 0:S], ACT.Identity,
                                     bias=bqk_c[:, 1, g:g + 1]).then_inc(k_ready, 1)
                if not first:
                    hT_hi(u + pos["oT"], pos["oT"], 4 * b)
                for g in range(-1, H // 2):
                    if g + 1 < H // 2:
                        exps(b, g + 1)
                    for h in (2 * g, 2 * g + 1):
                        if g >= 0 and pt_on_act(h):
                            move_pT(b, h)
                    if g == 2 and not last:
                        hT_hi(u + pos["hT"], pos["hT"], 4 * b + 2)
                    if g == 4 and not first:
                        x1T(b - 1, u + pos["x1T"], pos["x1T"])

            turn(0, first=True)
            with act_e.Fori(1, B - 1) as b:
                turn(b)
            turn(B - 1, last=True)
            hT_hi(UNITS_END, 0, 4 * B - 2)
            x1T(B - 1, UNITS_END + 2 * TB, 0)


            def widen(h, r, free):
                if free:
                    act_e.wait_ge(y_read, h - 1)
                q = mixer_rows(h)
                act_e.activation(qe[:, r % 2, :, 0:MD], q, ACT.Copy)
                act_e.activation(qe[:, r % 2, :, MD:MW], q[:, :, 0:MW - MD], ACT.Copy)\
                    .then_inc(qe_ready, 1)

            act_e.wait_ge(qx_ready, TILES)
            for h in range(2):
                widen(h, h, False)
            with act_e.Fori(1, MH // 2) as i:
                for r in range(2):
                    widen(2 * i + r, r, True)

            for t in range(TILES):
                act_e.wait_ge(h3T_full, t + 1)
                if t >= 2:
                    act_e.wait_ge(logits_full, t - 1)
                act_e.activation(h3T[:, t % 2, :, :], ps[:, 2 + t % 2, :].rearrange("p (c q) -> p c q", c=EC),
                                 ACT.Copy).then_inc(h3T_ready, 1)
            act_e.wait_ge(shifted, 1)
            act_e.activation(topx[:, :, :], topx[:, :, :], ACT.Exp).then_inc(numer, 1)

            def rows_T(j, r, free):
                act_e.wait_ge(xT_full, j + 1)
                if free:
                    act_e.wait_ge(gate_full, j - 1)
                act_e.activation(xgT[:, r % 2, :, :], ps[:, 0, :].rearrange("p (c q) -> p c q", c=EC),
                                 ACT.Copy).then_inc(xT_ready, 1)

            def silu(j, r, free):
                act_e.wait_ge(up_full, j + 1)
                if free:
                    act_e.wait_ge(gu_ready, j - 1)
                act_e.activation(act[:, r % 2, :], ps[:, 1, 0:F], ACT.Silu).then_inc(act_ready, 1)

            def rows_out(j, r, free):
                act_e.wait_ge(down_full, j + 1)
                if free:
                    act_e.wait_ge(y_stored[r], 4 * (j - r))
                act_e.activation(yo[:, r, :], ps[:, 4 + r % 2, :], ACT.Copy).then_inc(yo_ready, 1)

            rows_T(0, 0, False)
            for j in range(4):
                silu(j, j, j >= 2)
                rows_T(j + 1, (j + 1) % 4, j + 1 >= 2)
                if j >= 1:
                    rows_out(j - 1, j - 1, False)
            with act_e.Fori(1, SLOT_TILES // 4 - 1) as i:
                for r in range(4):
                    silu(4 * i + r, r, True)
                    rows_T(4 * i + r + 1, (r + 1) % 4, True)
                    rows_out(4 * i + r - 1, (r - 1) % 4, True)
            for j in range(SLOT_TILES - 4, SLOT_TILES):
                silu(j, j % 4, True)
                if j + 1 < SLOT_TILES:
                    rows_T(j + 1, (j + 1) % 4, True)
                rows_out(j - 1, (j - 1) % 4, True)
            rows_out(SLOT_TILES - 1, 3, True)

        @block.vector
        def _(dve):
            def carry():
                carried[0] = (carried[0] + 1) % 48
                dve.memset(carrier[:, carried[0]:carried[0] + 1], 0.0)

            def layer_stats(ln, src, st, mv, ve, n):
                for t in range(TB):
                    dve.bn_stats(st[:, t, :], src(t)).then_inc(ln["stats"], 1)
                dve.wait_ge(ln["stats"], TB * n + TB)
                carry()
                for t in range(TB):
                    dve.bn_aggr(mv[:, t, :], st[:, t, :]).then_inc(ln["aggr"], 1)
                dve.wait_ge(ln["aggr"], TB * n + TB)
                dve.tensor_scalar(ve[:, :], mv[:, :, 1], EPS, None, ALU.add).then_inc(ln["var"], 1)

            def layer_out(ln, src, dst, mv, rs, n):
                dve.wait_ge(ln["rstd"], n + 1)
                for t in range(TB):
                    dve.tensor_scalar(dst[:, t, :], src(t), mv[:, t, 0:1], rs[:, t:t + 1],
                                      ALU.subtract, ALU.mult).then_inc(ln["out"], 1)

            def x_tile(b):
                return lambda t: X[:, bass.ds(TB * b + t, 1), :].squeeze(1)

            def hT_lo(done, pos_n):
                for t in range(TB):
                    dve.wait_ge(ht_hi, done + t + 1)
                    n = pos_n + t
                    cols = slice(P * t, P * t + P)
                    dve.tensor_tensor(hTl[:, :, cols], ps[:, bank(n), :].rearrange("p (c q) -> p c q", c=EC),
                                      hTh[:, :, cols].bitcast(F32), ALU.subtract).then_inc(ht_lo, 1)

            def scores(b, g):
                for h in (2 * g, 2 * g + 1):
                    if h >= NE:
                        dve.wait_ge(p_ready, H * b + h - NE + 1)
                    dve.wait_ge(s_full, H * b + h + 1)
                    carry()
                    bank_h = SB[h % 2]
                    dve.tensor_tensor_reduce(sc[:, h % NE, 0:P], ps[:, bank_h, 0:P],
                                             bias_tab[:, h, P:2 * P], 1.0, MASKED, ALU.add, ALU.max,
                                             mx[:, h, 0:1])
                    dve.tensor_tensor_reduce(sc[:, h % NE, P:3 * P], ps[:, bank_h, P:3 * P],
                                             bias_tab[:, h, :], 1.0, MASKED, ALU.add, ALU.max,
                                             mx[:, h, 1:2]).then_inc(s_read, 1)
                dve.wait_ge(s_read, H * b + 2 * g + 2)
                dve.tensor_scalar(nm[:, 2 * g:2 * g + 2, :], mx[:, 2 * g:2 * g + 2, :], -1.0, None,
                                  ALU.mult).then_inc(nm_ready, 1)

            def move_pT(b, h):
                dve.wait_ge(pt_full, H * b + h + 1)
                dve.tensor_copy(pT[:, h % NE, :], ps[:, PB[h % 2], 0:3 * P]).then_inc(pt_dve, 1)

            def average(b):
                dve.wait_ge(p_ready, H * b + H)
                dve.reciprocal(rsum[:, :, :], sums[:, :, :]).then_inc(rsum_ready, 1)
                dve.wait_ge(rsum_ready, b + 1)
                dve.wait_ge(av_done, H * b + H)
                for t in range(TB):
                    dve.tensor_tensor(hn[:, t, :].rearrange("p (h d) -> p h d", h=H),
                                      ps[:, OB[t], :].rearrange("p (h d) -> p h d", h=H),
                                      rsum[:, :, t:t + 1].to_broadcast([P, H, HD]),
                                      ALU.mult).then_inc(o_ready, 1)

            def add_attention(b, n, pos_n):
                dve.wait_ge(xb_ready, b + 1)
                for t in range(TB):
                    dve.wait_ge(misc_full, n + t + 1)
                    xs = X[:, bass.ds(TB * b + t, 1), :].squeeze(1)
                    dve.tensor_tensor(xs, ps[:, bank(pos_n + t), :], xs, ALU.add)\
                        .then_inc(x1_ready, 1)

            dve.wait_ge(x_in0, 16)
            layer_stats(ln1, x_tile(0), st1, mv1, ve1, 0)
            dve.wait_ge(consts, 5)
            for h in range(H):
                dve.tensor_scalar(bias_tab[:, h, :], dist[:, :], 2.0 ** (-8.0 * (h + 1) / H), None,
                                  ALU.mult).then_inc(tab_scaled, 1)
            layer_out(ln1, x_tile(0), hn, mv1, rs1, 0)
            for m in range(4):
                dve.wait_ge(wsplit_hi, m + 1)
                dve.tensor_tensor(wlo[:, m, :, :], wraw[:, m, :, :], whi[:, HI_AT[m], :, :].bitcast(F32),
                                  ALU.subtract).then_inc(wsplit_lo, 1)
                if m == 0:
                    hT_lo(0, 0)

            def turn(b, first=False, last=False):
                u = units_before(b, first)
                pos = positions(first, last)
                if first:
                    dve.wait_ge(small_in, 16 * 5)
                for g in range(H // HG):
                    dve.wait_ge(misc_full, u + Q0 + g + 1)
                    dve.tensor_scalar(qT[:, g, :], ps[:, bank(Q0 + g), 0:S], bqk_c[:, 0, g:g + 1],
                                      HD ** -0.5, ALU.add, ALU.mult).then_inc(q_ready, 1)
                for t in range(TB):
                    dve.wait_ge(misc_full, u + V0 + t + 1)
                    dve.tensor_tensor(v[:, t, :], ps[:, bank(V0 + t), :], bv_b[:, :], ALU.add)\
                        .then_inc(v_ready, 1)
                if first:
                    dve.wait_ge(tab_ready, 1)
                    dve.wait_ge(x_in, 16)
                else:
                    hT_lo(4 * b, pos["oT"])
                    add_attention(b - 1, u + pos["wo"], pos["wo"])
                for g in range(-2, H // 2):
                    if g + 2 < H // 2:
                        scores(b, g + 2)
                    for h in (2 * g, 2 * g + 1):
                        if g >= 0 and not pt_on_act(h):
                            move_pT(b, h)
                    if not last:
                        if g == -1:
                            layer_stats(ln1, x_tile(b + 1), st1, mv1, ve1, b + 1)
                        if g == 1:
                            layer_out(ln1, x_tile(b + 1), hn, mv1, rs1, b + 1)
                        if g == 3:
                            hT_lo(4 * b + 2, pos["hT"])
                    if not first:
                        if g == 0:
                            dve.wait_ge(x1_ready, TB * b)
                            carry()
                            layer_stats(ln2, x_tile(b - 1), st2, mv2, ve2, b - 1)
                        if g == 2:
                            layer_out(ln2, x_tile(b - 1), hn2, mv2, rs2, b - 1)
                average(b)

            turn(0, first=True)
            with dve.Fori(1, B - 1) as b:
                turn(b)
            turn(B - 1, last=True)
            hT_lo(4 * B - 2, 0)
            add_attention(B - 1, UNITS_END + TB, 0)
            dve.wait_ge(x1_ready, TB * B)
            layer_stats(ln2, x_tile(B - 1), st2, mv2, ve2, B - 1)
            layer_out(ln2, x_tile(B - 1), hn2, mv2, rs2, B - 1)


            def prepare(h, r):
                dve.wait_ge(strip_in[r], 16 if isinstance(h, int) and h < NS else 4 * (h - r) + 16)
                dve.scalar_tensor_tensor(out=strip[:, r, 0:P], in0=anti[:, :],
                                         scalar=d_b[:, bass.ds(h, 1)], in1=strip[:, r, 0:P],
                                         op0=ALU.mult, op1=ALU.add).then_inc(strip_fixed, 1)

            def contract(h, r):
                y = convolved(r)
                q = qe[:, r % 2, :, :]
                z = terms[:, :, :]
                dims = [[MW, EC * B]]

                def grid(a, start, pitch, rows, width):
                    return a[:, :, start:start + rows * pitch]\
                        .rearrange("p n (d i) -> p n d i", i=pitch)[:, :, :, 0:width]

                dve.wait_ge(qe_ready, h + 1)
                dve.wait_ge(y_full, h + 1)
                dve.tensor_tensor(grid(z, DIAGS * SKEW, SKEW, MIRROR, MIRROR),
                                  grid(y, 2 * MD - 1, MD - 1, MIRROR, MIRROR),
                                  windows(q, dims + [[-1, MIRROR], [1, MIRROR]], MD - 1), ALU.mult)\
                    .then_inc(wrapped, 1)
                dve.tensor_tensor(grid(z, 0, SKEW, DIAGS, MD), grid(y, 0, MD, DIAGS, MD),
                                  windows(q, dims + [[1, DIAGS], [1, MD]]), ALU.mult)
                dve.wait_ge(wrapped, h + 1)
                dve.tensor_tensor(grid(z, DIAGS * SKEW + 1, SKEW + 1, MIRROR, MD),
                                  grid(y, MD, MD, MIRROR, MD),
                                  windows(q, dims + [[0, MIRROR], [1, MD]]), ALU.mult).then_inc(y_read, 1)
                dve.wait_ge(y_read, h + 1)
                carry()
                dve.tensor_reduce(mixer_rows(h),
                                  terms[:, :, 0:MD * SKEW].rearrange("p n (r j) -> p n j r", r=MD)[:, :, 0:MD, :],
                                  AX.X, ALU.add).then_inc(mixed, 1)
                dve.wait_ge(mixed, h + 1)

            dve.wait_ge(consts, 7)
            dve.wait_ge(qx_ready, TILES)
            for h in range(NS - 1):
                prepare(h, h)
            with dve.Fori(0, MH // NS - 1) as i:
                for r in range(NS):
                    prepare(NS * i + r + NS - 1, (r + NS - 1) % NS)
                    contract(NS * i + r, r)
            for h in range(MH - NS, MH):
                if h + NS - 1 < MH:
                    prepare(h + NS - 1, (h + NS - 1) % NS)
                contract(h, h % NS)

            def normalise(t):
                dve.wait_ge(ln3["rstd"], t + 1)
                if t >= 2:
                    dve.wait_ge(h3T_full, t - 1)
                    dve.wait_ge(h3_stored[t % 2], 16 * (t // 2))
                dve.tensor_scalar(h3[:, t % 2, :], X[:, t, :], mv3[:, t % 2, 0:1],
                                  rs3[:, t % 2:t % 2 + 1], ALU.subtract, ALU.mult)\
                    .then_inc(ln3["out"], 1)

            for t in range(TILES):
                dve.wait_ge(x2T_full, t + 1)
                dve.tensor_tensor(X[:, t, :], ps[:, t % 2, :], X[:, t, :], ALU.add).then_inc(x2_ready, 1)
                if t >= 1:
                    normalise(t - 1)
                dve.wait_ge(x2_ready, t + 1)
                dve.bn_stats(st3[:, t % 2, :], X[:, t, :]).then_inc(ln3["stats"], 1)
                dve.wait_ge(ln3["stats"], t + 1)
                dve.bn_aggr(mv3[:, t % 2, :], st3[:, t % 2, :]).then_inc(ln3["aggr"], 1)
                dve.wait_ge(ln3["aggr"], t + 1)
                dve.tensor_scalar(ve3[:, t % 2:t % 2 + 1], mv3[:, t % 2, 1:2], EPS, None, ALU.add)\
                    .then_inc(ln3["var"], 1)
            normalise(TILES - 1)

            steps = 0

            def step(ins):
                nonlocal steps
                steps += 1
                ins.then_inc(route, 1)
                dve.wait_ge(route, steps)

            dve.wait_ge(logits_full, TILES)
            step(dve.tensor_copy(logits[:, :, :], ps[:, 4, 0:TILES * NX].rearrange("p (t e) -> p t e", e=NX)))
            for t in range(TILES):
                ins = dve.max(top[:, t, :], logits[:, t, :])
            step(ins)
            for t in range(TILES):
                ins = dve.max_index(topi[:, t, :], top[:, t, :], logits[:, t, :])
            step(ins)
            dve.tensor_tensor(topx[:, :, :], top[:, :, :], top[:, :, 0:1].to_broadcast([P, TILES, 8]),
                              ALU.subtract).then_inc(shifted, 1)
            step(dve.tensor_copy(idxf[:, :, :], topi[:, :, 0:TOPK].rearrange("p t k -> p k t")))
            for k in range(TOPK):
                ins = dve.tensor_tensor(hot[:, k, :, :], iota8[:, :].unsqueeze(1).to_broadcast([P, TILES, NX]),
                                        idxf[:, k, :].unsqueeze(2).to_broadcast([P, TILES, NX]),
                                        ALU.is_equal)
            step(ins)
            step(dve.tensor_tensor(picked, hot[:, 0, :, :], hot[:, 1, :, :], ALU.add))
            dve.tensor_reduce(cnt[:, :], picked.rearrange("p t e -> p e t"), AX.X, ALU.add)\
                .then_inc(picked_ready, 1)
            dve.wait_ge(numer, 1)
            step(dve.tensor_reduce(zsum[:, :], topx[:, :, :], AX.X, ALU.add))
            step(dve.reciprocal(zrec[:, :], zsum[:, :]))
            step(dve.tensor_tensor(gate[:, :, :], topx[:, :, 0:TOPK],
                                   zrec[:, :].unsqueeze(2).to_broadcast([P, TILES, TOPK]), ALU.mult))
            step(dve.tensor_reduce(psum2[:, :], gate[:, :, :], AX.X, ALU.add))
            step(dve.reciprocal(prec2[:, :], psum2[:, :]))
            step(dve.tensor_tensor(gate[:, :, :], gate[:, :, :],
                                   prec2[:, :].unsqueeze(2).to_broadcast([P, TILES, TOPK]), ALU.mult))
            dve.tensor_scalar(iota16[:, :], iota40[:, 0:TILES], float(P), None, ALU.mult)
            dve.wait_ge(ranks_full, 1)
            dve.tensor_copy(ranks[:, :, :], ps[:, 5, 0:TILES * NX].rearrange("p (t e) -> p t e", e=NX))
            step(dve.tensor_copy(count[:, :], ps[:, 6, 0:NX]))
            c3 = cmp[:, 0:NX * TILES].rearrange("p (e k) -> p e k", e=NX)
            step(dve.tensor_tensor(c3, count[:, :].unsqueeze(2).to_broadcast([P, NX, TILES]),
                                   iota16[:, :].unsqueeze(1).to_broadcast([P, NX, TILES]), ALU.is_gt))
            step(dve.tensor_reduce(ntile[:, :], c3, AX.X, ALU.add))
            c3 = cmp[:, 0:NX * NX].rearrange("p (e k) -> p e k", e=NX)
            step(dve.tensor_tensor(c3, ntile[:, :].unsqueeze(1).to_broadcast([P, NX, NX]), le8[:, :, :],
                                   ALU.mult))
            step(dve.tensor_reduce(cumt[:, :], c3, AX.X, ALU.add))
            step(dve.tensor_tensor(base[:, :], cumt[:, :], ntile[:, :], ALU.subtract))
            step(dve.scalar_tensor_tensor(out=ranks[:, :, :],
                                          in0=base[:, :].unsqueeze(1).to_broadcast([P, TILES, NX]),
                                          scalar=float(P), in1=ranks[:, :, :], op0=ALU.mult, op1=ALU.add))
            for k in range(TOPK):
                ins = dve.tensor_tensor(hot[:, k, :, :], hot[:, k, :, :], ranks[:, :, :], ALU.mult)
            step(ins)
            step(dve.tensor_reduce(slotf[:, :, :], hot[:, :, :, :], AX.X, ALU.add))
            step(dve.tensor_copy(slot[:, :, :], slotf[:, :, :]))
            dve.tensor_single_scalar(sdiv[:, :, :], slot[:, :, :], P.bit_length() - 1, ALU.arith_shift_right)
            step(dve.tensor_single_scalar(smod[:, :, :], slot[:, :, :], P - 1, ALU.bitwise_and))
            dve.tensor_copy(sdivf[:, :, :], sdiv[:, :, :])
            step(dve.tensor_copy(smodf[:, :, :], smod[:, :, :]))
            for k in range(TOPK):
                for t in range(TILES):
                    n = TILES * k + t
                    dve.tensor_scalar(hot_p[:, n, :], iota128[:, :], smodf[:, k, t:t + 1], None,
                                      ALU.is_equal)
                    dve.tensor_scalar(hot_j[:, n, :], iota40[:, :], sdivf[:, k, t:t + 1],
                                      tok[:, t:t + 1], ALU.is_equal, ALU.mult).then_inc(hot_ready, 1)
            c3 = cmp[:, :].rearrange("p (j e) -> p j e", e=NX)
            step(dve.tensor_tensor(c3, cumt[:, :].unsqueeze(1).to_broadcast([P, SLOT_TILES, NX]),
                                   iota40[:, :].unsqueeze(2).to_broadcast([P, SLOT_TILES, NX]), ALU.is_le))
            step(dve.tensor_reduce(eidf[:, :], c3, AX.X, ALU.add))
            step(dve.tensor_scalar(eid[:, :], eidf[:, :], float(NX - 1), None, ALU.min))
            dve.wait_ge(idx_full, 1)
            dve.tensor_copy(idx[:, :], ps[:, 7, 0:SLOT_TILES]).then_inc(idx_ready, 1)

            def rows_gu_T(j, r, free):
                dve.wait_ge(guT_full, j + 1)
                if free:
                    dve.wait_ge(down_full, j - 1)
                dve.tensor_copy(guT[:, r % 2, 0:FC - 1, :],
                                ps[:, 3, 0:(FC - 1) * P].rearrange("p (c q) -> p c q", q=P))
                dve.tensor_copy(guT[0:FLAST, r % 2, FC - 1, :], ps[0:FLAST, 3, (FC - 1) * P:FC * P])\
                    .then_inc(guT_ready, 1)

            def gated(j, r, free):
                dve.wait_ge(act_ready, j + 1)
                dve.wait_ge(gate_full, j + 1)
                if free:
                    dve.wait_ge(guT_full, j - 1)
                dve.tensor_tensor(gu[:, r % 2, :], ps[:, 2, 0:F], act[:, r % 2, :], ALU.mult)\
                    .then_inc(gu_ready, 1)

            for j in range(4):
                if j >= 1:
                    rows_gu_T(j - 1, j - 1, j - 1 >= 2)
                gated(j, j, j >= 2)
            with dve.Fori(1, SLOT_TILES // 4) as i:
                for r in range(4):
                    rows_gu_T(4 * i + r - 1, (r - 1) % 4, True)
                    gated(4 * i + r, r, True)
            rows_gu_T(SLOT_TILES - 1, 3, True)

            def combine(t, r, free):
                dve.wait_ge(fetched[r], 8 * (t - r) + 32)
                if free:
                    dve.wait_ge(sent[r], 4 * (t - r))
                xs = X[:, bass.ds(t, 1), :].squeeze(1)
                g = gate[:, bass.ds(t, 1), :].squeeze(1)
                dve.scalar_tensor_tensor(out=res[:, r, :], in0=ga[:, r, 0, :], scalar=g[:, 0:1],
                                         in1=xs, op0=ALU.mult, op1=ALU.add).then_inc(half_done, 1)
                dve.wait_ge(half_done, t + 1)
                dve.scalar_tensor_tensor(out=res[:, r, :], in0=ga[:, r, 1, :], scalar=g[:, 1:2],
                                         in1=res[:, r, :], op0=ALU.mult, op1=ALU.add)\
                    .then_inc(res_ready, 1)

            for r in range(4):
                combine(r, r, False)
            with dve.Fori(1, TILES // 4) as i:
                for r in range(4):
                    combine(4 * i + r, r, True)

        @block.tensor
        def _(pe):
            def three_pass(dst, parts, n):
                for c in range(n):
                    for i in range(3):
                        lhs, rhs = parts(c, i)
                        mm = pe.matmul(dst, lhs, rhs, start=(c == 0 and i == 0),
                                       stop=(c == n - 1 and i == 2))
                return mm

            H_OF = (hTh, hTl, hTh)

            def w_of(i, m, c, cols=slice(0, E)):
                return wlo[:, m, c, cols] if i == 2 else whi[:, HI_AT[m], c, cols]

            def transposes(src, t, dst):
                for c in range(EC):
                    mm = pe.transpose(dst[:, P * c:P * c + P], src[:, t, P * c:P * c + P], ident[:, :])
                mm.then_inc(misc_full, 1)

            def rows_projection(m, t, dst):
                three_pass(dst, lambda c, i: (H_OF[i][:, c, P * t:P * t + P], w_of(i, m, c)), EC)\
                    .then_inc(misc_full, 1)

            def qkv(b, first):
                if first:
                    pe.wait_ge(ht_lo, TB)
                else:
                    pe.wait_ge(ht_lo, 4 * b)
                for m in range(2):
                    if first:
                        pe.wait_ge(wsplit_lo, m + 1)
                    for g in range(H // HG):
                        n = (Q0, K0)[m] + g
                        if n in (Q0 + 2, Q0 + 3, K0, K0 + 1):
                            pe.wait_ge(q_ready, 4 * b + n - 1)
                        elif n > K0 + 1:
                            pe.wait_ge(k_ready, 4 * b + g - 1)
                        cols = slice(P * g, P * g + P)
                        three_pass(ps[:, bank(n), 0:S],
                                   lambda c, i: (w_of(i, m, c, cols), H_OF[i][:, c, :]), EC)\
                            .then_inc(misc_full, 1)
                if first:
                    pe.wait_ge(wsplit_lo, 3)
                for t in range(TB):
                    pe.wait_ge(k_ready, 4 * b + 3 + t)
                    rows_projection(2, t, ps[:, bank(V0 + t), :])

            def score(b, h, first):
                if not (first and h < 2):
                    pe.wait_ge(s_read, H * b + h - 1)
                r = slice(HD * (h % HG), HD * (h % HG) + HD)
                g = h // HG
                pe.matmul(ps[:, SB[h % 2], 0:P], qT[r, g, 0:P], kT[r, g, 0:P], start=True, stop=True)
                pe.matmul(ps[:, SB[h % 2], P:3 * P], qT[r, g, P:S], kT[r, g, :], start=True, stop=True)\
                    .then_inc(s_full, 1)

            def moved(b, h):
                if pt_on_act(h):
                    pe.wait_ge(pt_act, pt_count(b, h, True))
                else:
                    pe.wait_ge(pt_dve, pt_count(b, h, False))

            def probs_T(b, h):
                pe.wait_ge(p_ready, H * b + h + 1)
                if h >= 2:
                    moved(b, h - 2)
                for i in range(3):
                    mm = pe.transpose(ps[:, PB[h % 2], P * i:P * i + P], pr[:, h % NE, P * i:P * i + P],
                                      ident[:, :])
                mm.then_inc(pt_full, 1)

            def values(b, h):
                moved(b, h)
                if h == 0:
                    pe.wait_ge(v_ready, TB * b + TB)
                d = slice(HD * h, HD * h + HD)
                pe.matmul(ps[:, OB[0], d], pT[:, h % NE, 0:P], v[:, 0, d], start=True, stop=True)
                pe.matmul(ps[:, OB[1], d], pT[:, h % NE, P:2 * P], v[:, 0, d], start=True, stop=False)
                pe.matmul(ps[:, OB[1], d], pT[:, h % NE, 2 * P:3 * P], v[:, 1, d], start=False,
                          stop=True).then_inc(av_done, 1)

            def next_hT(b, pos_n, first):
                pe.wait_ge(ln1["out"], TB * b + 2 * TB)
                for t in range(TB):
                    if first:
                        pe.wait_ge(v_ready, t + 1)
                    else:
                        pe.wait_ge(x1_ready, TB * b - TB + t + 1)
                    transposes(hn, t, ps[:, bank(pos_n + t), :])

            def x1_T(b, pos_n, after_hT):
                pe.wait_ge(ln2["out"], TB * b + TB)
                for t in range(TB):
                    if after_hT:
                        pe.wait_ge(ht_lo, 4 * b + 4 + 2 + t + 1)
                    else:
                        pe.wait_ge(x1_ready, TB * b + t + 1)
                    transposes(hn2, t, ps[:, bank(pos_n + t), :])

            pe.wait_ge(consts, 5)
            pe.wait_ge(ln1["out"], TB)
            for t in range(TB):
                transposes(hn, t, ps[:, bank(t), :])

            def turn(b, first=False, last=False):
                pos = positions(first, last)
                qkv(b, first)
                if not first:
                    pe.wait_ge(v_ready, TB * b + TB)
                    pe.wait_ge(o_ready, TB * b)
                    for t in range(TB):
                        transposes(hn, t, ps[:, bank(pos["oT"] + t), :])
                    for t in range(TB):
                        pe.wait_ge(ht_lo, 4 * b + t + 1)
                        rows_projection(3, t, ps[:, bank(pos["wo"] + t), :])
                pe.wait_ge(q_ready, 4 * b + 4)
                pe.wait_ge(k_ready, 4 * b + 4)
                for g in range(-2, H // 2 + 1):
                    for h in (2 * g + 4, 2 * g + 5):
                        if h < H:
                            score(b, h, first)
                    for h in (2 * g, 2 * g + 1):
                        if 0 <= h < H:
                            probs_T(b, h)
                    for h in (2 * g - 2, 2 * g - 1):
                        if 0 <= h:
                            values(b, h)
                    if g == 2 and not last:
                        next_hT(b, pos["hT"], first)
                    if g == 4 and not first:
                        x1_T(b - 1, pos["x1T"], not last)
                if not first:
                    pe.wait_ge(qx_ready, TB * b)

            turn(0, first=True)
            pe.wait_ge(wsplit_lo, 4)
            with pe.Fori(1, B - 1) as b:
                turn(b)
            turn(B - 1, last=True)
            pe.wait_ge(o_ready, TB * B)
            for t in range(TB):
                transposes(hn, t, ps[:, bank(t), :])
            for t in range(TB):
                pe.wait_ge(ht_lo, 4 * B - 2 + t + 1)
                rows_projection(3, t, ps[:, bank(t), :])
            x1_T(B - 1, 0, False)

            def convolve(h, r, free):
                pe.wait_ge(strip_fixed, h + 1)
                pe.wait_ge(kv_ready, h + 1)
                if free:
                    pe.wait_ge(y_read, h - 1)
                for lo in range(EC):
                    for m in range(lo + 1):
                        mm = pe.matmul(convolved(r)[:, B * lo:B * lo + B, 0:PAIRS],
                                       strip[:, r, P * (lo - m):P * (lo - m) + P],
                                       kv[:, r, B * m:B * m + B, :],
                                       start=(m == 0), stop=(m == lo))
                mm.then_inc(y_full, 1)

            pe.wait_ge(x1_ready, TB * B)
            pe.wait_ge(qx_ready, TILES)
            for h in range(KV):
                convolve(h, h, h >= 2)
            with pe.Fori(1, MH // KV) as i:
                for r in range(KV):
                    convolve(KV * i + r, r, True)
            pe.wait_ge(mixed, MH)

            def x2_T(t):
                if t >= 2:
                    pe.wait_ge(x2_ready, t - 1)
                for c in range(EC):
                    mm = pe.transpose(ps[:, t % 2, P * c:P * c + P], QX[:, c, P * t:P * t + P], ident[:, :])
                mm.then_inc(x2T_full, 1)

            def h3_T(t):
                pe.wait_ge(ln3["out"], t + 1)
                if t >= 2:
                    pe.wait_ge(h3T_ready, t - 1)
                for c in range(EC):
                    mm = pe.transpose(ps[:, 2 + t % 2, P * c:P * c + P], h3[:, t % 2, P * c:P * c + P],
                                      ident[:, :])
                mm.then_inc(h3T_full, 1)

            def router(t):
                pe.wait_ge(h3T_ready, t + 1)
                for c in range(EC):
                    mm = pe.matmul(ps[:, 4, NX * t:NX * t + NX], h3T[:, t % 2, c, :], wr[:, c, :],
                                   start=(c == 0), stop=(c == EC - 1))
                mm.then_inc(logits_full, 1)

            for t in range(TILES + 2):
                if t < TILES:
                    x2_T(t)
                if 1 <= t <= TILES:
                    h3_T(t - 1)
                if t >= 2:
                    router(t - 2)

            pe.wait_ge(tables, 12)
            pe.wait_ge(picked_ready, 1)
            for back in range(TILES):
                pe.matmul(ps[:, 5, 0:TILES * NX], ones[:, :] if back else upper[:, :],
                          padded[:, TILES - back:2 * TILES - back, :].rearrange("p t e -> p (t e)"),
                          start=(back == 0), stop=(back == TILES - 1))
            pe.matmul(ps[:, 6, 0:NX], ones[:, :], cnt[:, :], start=True, stop=True).then_inc(ranks_full, 1)
            for n in range(TOPK * TILES):
                pe.wait_ge(hot_ready, n + 1)
                mm = pe.matmul(ps[:, 7, 0:SLOT_TILES], hot_p[:, n, :], hot_j[:, n, :],
                               start=(n == 0), stop=(n == TOPK * TILES - 1))
            mm.then_inc(idx_full, 1)

            pe.wait_ge(idx_ready, 1)
            pe.wait_ge(wx_in, 16 * (3 * NX - 2))
            pe.wait_ge(wx_late, 16)

            def expert(j):
                return pe.value_load(eid[0:1, bass.ds(j, 1)], min_val=0, max_val=NX - 1)

            def rows_T(j, r, free):
                pe.wait_ge(gathered[r], 4 * (j - r) + 16)
                if free:
                    pe.wait_ge(xT_ready, j)
                for c in range(EC):
                    mm = pe.transpose(ps[:, 0, P * c:P * c + P], xg[:, r, P * c:P * c + P], ident[:, :])
                mm.then_inc(xT_full, 1)

            def up(j, r, e, w, bank_w, full):
                for c in range(EC):
                    mm = pe.matmul(ps[:, bank_w, 0:F], xgT[:, r % 2, c, :],
                                   w[:, bass.ds(e, 1), c, :].squeeze(1), start=(c == 0), stop=(c == EC - 1))
                mm.then_inc(full, 1)

            def hidden_T(j, r, free):
                pe.wait_ge(gu_ready, j + 1)
                if free:
                    pe.wait_ge(guT_ready, j)
                for c in range(FC):
                    k = P if c < FC - 1 else FLAST
                    mm = pe.transpose(ps[0:k, 3, P * c:P * c + P], gu[:, r % 2, P * c:P * c + k], ident[:, :])
                mm.then_inc(guT_full, 1)

            def down(j, r, e, free):
                pe.wait_ge(guT_ready, j + 1)
                if free:
                    pe.wait_ge(yo_ready, j - 1)
                for c in range(FC):
                    k = P if c < FC - 1 else FLAST
                    mm = pe.matmul(ps[:, 4 + r % 2, :], guT[0:k, r % 2, c, :],
                                   wd[0:k, bass.ds(e, 1), c, :].squeeze(1), start=(c == 0), stop=(c == FC - 1))
                mm.then_inc(down_full, 1)

            def expert_tile(j, r, first=False, last=False):
                e = expert(j)
                pe.wait_ge(xT_ready, j + 1)
                if not first:
                    pe.wait_ge(act_ready, j)
                up(j, r, e, wu, 1, up_full)
                if not first:
                    hidden_T(j - 1, (r - 1) % 4, not (isinstance(j, int) and j == 1))
                    pe.wait_ge(gu_ready, j)
                up(j, r, e, wg, 2, gate_full)
                if not last:
                    rows_T(j + 1, (r + 1) % 4, True)
                if not first:
                    down(j - 1, (r - 1) % 4, expert(j - 1), not (isinstance(j, int) and j <= 2))

            rows_T(0, 0, False)
            for j in range(4):
                expert_tile(j, j, first=(j == 0))
            with pe.Fori(1, SLOT_TILES // 4 - 1) as i:
                for r in range(4):
                    expert_tile(4 * i + r, r)
            for j in range(SLOT_TILES - 4, SLOT_TILES):
                expert_tile(j, j % 4, last=(j == SLOT_TILES - 1))
            hidden_T(SLOT_TILES - 1, 3, True)
            down(SLOT_TILES - 1, 3, expert(SLOT_TILES - 1), True)

        return nc


def kernel(**inputs):
    import numpy as _np
    import concourse.bacc as _bacc
    from concourse.bass_utils import run_bass_kernel_spmd as _run

    arrays = laid_out(inputs)
    nc = _bacc.Bacc("TRN2", target_bir_lowering=False, num_devices=1)
    args = [nc.dram_tensor(n, a.shape, mybir.dt.from_np(a.dtype), kind="ExternalInput").ap()
            for n, a in arrays.items()]
    out = nc.dram_tensor("out", (B, S, E), F32, kind="ExternalOutput").ap()
    decoder_block(nc, *args, out)
    r = _run(nc, [arrays], core_ids=[0])
    return r.results[0]["out"]


def laid_out(inputs):
    import numpy as np
    g = {k: np.asarray(v) for k, v in inputs.items()}

    def chunks(w):
        return w.reshape(-1, P, w.shape[-1]).transpose(1, 0, 2)

    def experts(w):
        n = -(-w.shape[1] // P) * P
        w = np.concatenate([w, np.zeros((w.shape[0], n - w.shape[1], w.shape[2]), w.dtype)], 1)
        return w.reshape(w.shape[0], -1, P, w.shape[2]).transpose(2, 0, 1, 3)

    w_attn = np.stack([chunks(g[f"L0_attn_W{m}"].T) for m in "qkvo"])
    b_qk = np.stack([g[f"L0_attn_b{m}"].reshape(-1, P).T for m in "qk"], 1)
    c = g["ctx_2048"].transpose(2, 0, 1).reshape(EC, P, B, S)[:, ::-1]
    c = c.transpose(1, 0, 2, 3).reshape(P, EC * B, MH, MD)
    ctx_rev = np.concatenate([c, c[..., :MW - MD]], -1)
    kern = g["L0_xattn_ssm_kernel"]
    kern_pad = np.concatenate([np.zeros((MH, P - 1), kern.dtype), kern], 1)
    out = {
        "x": g["x"], "w_attn": w_attn, "b_qk": b_qk, "b_v": g["L0_attn_bv"], "b_o": g["L0_attn_bo"],
        "ctx_rev": ctx_rev, "kern_pad": kern_pad, "skip_d": g["L0_xattn_D"],
        "w_router": chunks(g["L0_ffn_w_router"].T),
        "w_up": experts(g["L0_ffn_w1"].transpose(0, 2, 1)),
        "w_gate": experts(g["L0_ffn_w3"].transpose(0, 2, 1)),
        "w_down": experts(g["L0_ffn_w2"].transpose(0, 2, 1)),
    }
    return {k: np.ascontiguousarray(a) for k, a in out.items()}
```

```python
from contextlib import ExitStack

import concourse.bass as bass
from concourse import mybir

P = 128
B, S, E = 8, 256, 512
TILES = B * S // P
TB = S // P
EC = E // P
H, HD = 16, 32
HG = P // HD
MH, MD = 32, 8
DIAGS = MD // 2 + 1
PAIRS = DIAGS * MD
MW = MD + DIAGS - 1
MIRROR = DIAGS - 2
SKEW = MD + MIRROR
TERMS = MD * SKEW + MIRROR + 1
NX, F = 8, 352
FC = (F + P - 1) // P
FLAST = F - (FC - 1) * P
TOPK = 2
SLOT_TILES = TILES * TOPK + NX - 1
SLOT_COLS = SLOT_TILES + SLOT_TILES % 2
ROUNDS = (SLOT_TILES - 1) // 4
SLOTS = SLOT_TILES * P
EPS = 1e-5
KPAD = P - 1 + E
MASKED = -1e30

F32 = mybir.dt.float32
F32R = mybir.dt.float32r
I32 = mybir.dt.int32
U32 = mybir.dt.uint32
ALU = mybir.AluOpType
ACT = mybir.ActivationFunctionType
AX = mybir.AxisListType
KB = 1024


def decoder_block(nc, x, w_attn, b_qkv, b_o, ctx_rev, kern_pad, skip_d, w_router, w_up, w_gate,
                  w_down, out):
    ctx = ExitStack()
    with ctx:
        arena = (nc.sbuf_base + 63) // 64 * 64

        def at(name, shape, kb, dt=F32):
            return nc.alloc_sbuf_tensor_at(name, shape, dt, offset=arena + int(kb * KB))

        def sem(name):
            return ctx.enter_context(nc.semaphore(name))

        X = at("X", [P, TILES, E], 0)
        QX = at("QX", [P, EC, B * S], 32)
        ident = at("ident", [P, P], 200)
        mhalf = at("mhalf", [P, TB], 200.5)
        carrier = at("carrier", [P, 64], 200.75)
        carried = [0, 0]
        wraw = at("wraw", [P, 4, EC, E], 32)
        whi = at("whi", [P, 4, EC, E], 64, F32R)
        wlo = at("wlo", [P, 4, EC, E], 96, F32R)
        HI_AT = (1, 2, 3, 0)
        bias_tab = at("bias_tab", [P, H, S], 128)
        hn = at("hn", [P, TB, E], 144)
        oTh = at("oTh", [P, EC, S], 148, F32R)
        oTl = at("oTl", [P, EC, S], 192, F32R)
        hTh = at("hTh", [P, EC, S], 152, F32R)
        hTl = at("hTl", [P, EC, S], 156, F32R)
        qT = at("qT", [P, H // HG, S], 160)
        kT = at("kT", [P, H // HG, S], 164)
        v = at("v", [P, TB, E], 168)
        NE = 4
        sc = at("sc", [P, NE, 3 * P], 172)
        pr = at("pr", [P, NE, 3 * P], 178)
        pT = at("pT", [P, NE, 3 * P], 184)
        bo_b = at("bo_b", [P, E], 190)
        dist = at("dist", [P, S], 194)
        dist_i = at("dist_i", [P, S], 195, I32)
        bqkv_c = at("bqkv_c", [P, 3, H // HG], 196)
        mx = at("mx", [P, H, TB], 196.25)
        nm = at("nm", [P, H, TB], 196.5)
        sums = at("sums", [P, H, TB], 196.75)
        rsum = at("rsum", [P, H, TB], 197)
        st1 = at("st1", [P, TB, 6], 197.25)
        mv1 = at("mv1", [P, TB, 2], 197.375)
        ve1 = at("ve1", [P, TB], 197.5)
        rs1 = at("rs1", [P, TB], 197.625)
        st2 = at("st2", [P, TB, 6], 197.75)
        mv2 = at("mv2", [P, TB, 2], 197.875)
        ve2 = at("ve2", [P, TB], 198)
        rs2 = at("rs2", [P, TB], 198.125)
        cx = at("cx", [P, EC * B, MH, MW], 72)
        NS = 4
        strip = at("strip", [P, NS, E], 120)
        KV = 4
        kv = at("kv", [P, KV, EC * B, PAIRS], 128)
        qe = at("qe", [P, 2, EC * B, MW], 64)
        terms = at("terms", [P, EC * B, TERMS], 148)
        anti = at("anti", [P, P], 201)
        d_b = at("d_b", [P, MH], 201.5)
        wd = at("wd", [P, NX, FC, E], 64)
        wg = at("wg", [P, NX, EC, F], 112)
        wu = at("wu", [P, NX, EC, F], 156)
        CB = 64
        h3 = at("h3", [P, 2, E], CB)
        h3T = at("h3T", [P, 2, EC, P], CB + 4)
        logits = at("logits", [P, TILES, NX], CB + 8)
        top = at("top", [P, TILES, 8], CB + 8.5)
        topi = at("topi", [P, TILES, 8], CB + 9, U32)
        topx = at("topx", [P, TILES, 8], CB + 9.5)
        padded = at("padded", [P, 2 * TILES, NX], CB + 10, F32R)
        picked = padded[:, TILES:2 * TILES, :]
        hot = at("hot", [P, TOPK, TILES, NX], CB + 11)
        zsum = at("zsum", [P, TILES], 202)
        zrec = at("zrec", [P, TILES], 202.0625)
        psum2 = at("psum2", [P, TILES], 202.125)
        prec2 = at("prec2", [P, TILES], 202.1875)
        gate = at("gate", [P, TILES, TOPK], 202.25)
        idxf = at("idxf", [P, TOPK, TILES], 202.375)
        slotf = at("slotf", [P, TOPK, TILES], 202.5)
        slot = at("slot", [P, TOPK, TILES], 202.625, I32)
        sdiv = at("sdiv", [P, TOPK, TILES], 202.75, I32)
        smod = at("smod", [P, TOPK, TILES], 202.875, I32)
        sdivf = at("sdivf", [P, TOPK, TILES], 203)
        smodf = at("smodf", [P, TOPK, TILES], 203.125)
        cnt = at("cnt", [P, NX], 203.25)
        count = at("count", [P, NX], 203.28125)
        ntile = at("ntile", [P, NX], 203.3125)
        cumt = at("cumt", [P, NX], 203.34375)
        base = at("base", [P, NX], 203.375)
        eidf = at("eidf", [P, SLOT_TILES], 203.5)
        eid = at("eid", [P, SLOT_TILES], 203.75, I32)
        idx = at("idx", [P, SLOT_COLS], 204, I32)
        tok = at("tok", [P, TILES], 204.25)
        iota8 = at("iota8", [P, NX], 204.3125)
        iota16 = at("iota16", [P, TILES], 204.34375)
        iota_j = at("iota_j", [P, SLOT_COLS], 204.5)
        le8 = at("le8", [P, NX, NX], 204.75)
        st3 = at("st3", [P, 2, 6], 205)
        mv3 = at("mv3", [P, 2, 2], 205.0625)
        ve3 = at("ve3", [P, 2], 205.125)
        rs3 = at("rs3", [P, 2], 205.15625)
        gcol = at("gcol", [P, 4], 205.1875, U32)
        fcol = at("fcol", [P, 2, 4, TOPK], 205.25, U32)
        tok_i = at("tok_i", [P, TILES], 205.3125, I32)
        iota_ji = at("iota_ji", [P, SLOT_COLS], 205.5, I32)
        wr = at("wr", [P, EC, NX], 205.75)
        iota128 = at("iota128", [P, P], 206.25)
        ranks = at("ranks", [P, TILES, NX], 206.75)
        ones = at("ones", [P, P], 32, F32R)
        upper = at("upper", [P, P], 32.5, F32R)
        upper_f = at("upper_f", [P, P], 35)
        cmp = at("cmp", [P, SLOT_TILES * NX], 33)
        hot_p = at("hot_p", [P, TOPK * TILES, P], 35, F32R)
        hot_j = at("hot_j", [P, TOPK * TILES, SLOT_COLS], 51, F32R)
        NG = 4
        xg = at("xg", [P, NG, E], 32)
        xgT = at("xgT", [P, 2, EC, P], 40)
        act = at("act", [P, 2, F], 44)
        gu = at("gu", [P, 2, F], 47)
        guT = at("guT", [P, 2, FC, P], 50)
        yo = at("yo", [P, 4, E], 53)
        ga = at("ga", [P, 4, TOPK, E], 64)
        res = at("res", [P, 4, E], 80)

        ps = ctx.enter_context(nc.psum_tensor("ps", [P, 8, 512], F32))

        h3_d = nc.dram_tensor("h3_rows", [B * S, E], F32, kind="Internal").ap()
        y_d = nc.dram_tensor("expert_rows", [SLOTS, E], F32, kind="Internal").ap()

        x_t = x.rearrange("b (t p) e -> p (b t) e", p=P)
        out_t = out.rearrange("b (t p) e -> p (b t) e", p=P)
        h3_t = h3_d.rearrange("(t p) e -> p t e", p=P)
        y_t = y_d.rearrange("(t p) e -> p t e", p=P)

        x_in0, x_in = sem("x_in0"), sem("x_in")
        w_in = [sem(f"w_in{m}") for m in range(4)]
        small_in = sem("small_in")
        wsplit_hi, wsplit_lo = sem("wsplit_hi"), sem("wsplit_lo")
        consts = sem("consts")
        tab_scaled, tab_ready = sem("tab_scaled"), sem("tab_ready")
        ln1 = {k: sem(f"ln1_{k}") for k in ("stats", "aggr", "var", "rstd", "out")}
        ln2 = {k: sem(f"ln2_{k}") for k in ("stats", "aggr", "var", "rstd", "out")}
        misc_full = sem("misc_full")
        ht_hi, ht_lo = sem("ht_hi"), sem("ht_lo")
        q_ready, k_ready, v_ready = sem("q_ready"), sem("k_ready"), sem("v_ready")
        s_full, s_read = sem("s_full"), sem("s_read")
        nm_ready, p_ready = sem("nm_ready"), sem("p_ready")
        pt_full, pt_dve, pt_act = sem("pt_full"), sem("pt_dve"), sem("pt_act")
        rsum_ready, pn_ready, av_done = sem("rsum_ready"), sem("pn_ready"), sem("av_done")
        ot_hi, ot_lo = sem("ot_hi"), sem("ot_lo")
        xb_ready, x1_ready, qx_ready = sem("xb_ready"), sem("x1_ready"), sem("qx_ready")
        cx_in = sem("cx_in")
        strip_in = [sem(f"strip_in{r}") for r in range(NS)]
        strip_fixed, kv_ready, qe_ready = sem("strip_fixed"), sem("kv_ready"), sem("qe_ready")
        wrapped = sem("wrapped")
        y_full, y_read, mixed = sem("y_full"), sem("y_read"), sem("mixed")
        x2T_full, x2_ready = sem("x2T_full"), sem("x2_ready")
        ln3 = {k: sem(f"ln3_{k}") for k in ("stats", "aggr", "var", "rstd", "out")}
        h3_stored = [sem("h3_stored0"), sem("h3_stored1")]
        h3T_full, h3T_ready, logits_full = sem("h3T_full"), sem("h3T_ready"), sem("logits_full")
        tables = sem("tables")
        route, shifted, numer = sem("route"), sem("shifted"), sem("numer")
        picked_ready, ranks_full = sem("picked_ready"), sem("ranks_full")
        hot_ready, idx_full, idx_ready = sem("hot_ready"), sem("idx_full"), sem("idx_ready")
        wx_in, wx_late = sem("wx_in"), sem("wx_late")
        gcol_ready = sem("gcol_ready")
        gathered = [sem(f"gathered{r}") for r in range(4)]
        xT_full, xT_ready = sem("xT_full"), sem("xT_ready")
        up_full, gate_full = sem("up_full"), sem("gate_full")
        act_ready, gu_ready = sem("act_ready"), sem("gu_ready")
        guT_full, guT_ready = sem("guT_full"), sem("guT_ready")
        down_full, yo_ready = sem("down_full"), sem("yo_ready")
        y_stored = [sem(f"y_stored{r}") for r in range(4)]
        fcol_ready = sem("fcol_ready")
        fetched = [sem(f"fetched{r}") for r in range(4)]
        half_done, res_ready = sem("half_done"), sem("res_ready")
        sent = [sem(f"sent{r}") for r in range(4)]
        block = ctx.enter_context(nc.Block())

        MISC = (0, 1)
        SB = (2, 3)
        PB = (4, 5)
        OB = (6, 7)
        HB = 2 * HG
        Q0, K0 = 0, H // HG
        FIRST_UNITS, TURN_UNITS = 2 * (H // HG) + 2 * TB, 2 * (H // HG) + 4 * TB

        def units_before(b, first):
            return TB if first else TB + FIRST_UNITS + (b - 1) * TURN_UNITS

        UNITS_END = TB + FIRST_UNITS + (B - 1) * TURN_UNITS - TB

        def positions(first, last):
            n = K0 + H // HG
            pos = {}
            if not first:
                pos["wo"] = n
                n += TB
            pos["v"] = n
            n += TB
            if not last:
                pos["hT"] = n
                n += TB
            if not first:
                pos["x1T"] = n
            return pos

        def bank(n):
            return MISC[n % 2]

        def pt_on_act(h):
            return h % 4 == 3

        def pt_count(b, h, act_engine):
            n = (h + 1) // 4 if act_engine else h + 1 - (h + 1) // 4
            return (H // 4 if act_engine else H - H // 4) * b + n

        def windows(a, dims, start=0):
            return bass.AP(tensor=a.tensor, offset=a.offset + start, ap=[list(a.ap[0])] + dims)

        def mixer_rows(h):
            q = QX[:, :, :].rearrange("p c (b h i) -> p (c b) h i", b=B, h=MH)
            return q[:, :, bass.ds(h, 1), :].squeeze(2)

        def convolved(r):
            return ps[:, 4 * (r % 2):4 * (r % 2) + 4, :].rearrange("p c (b k) -> p (c b) k", b=B)

        @block.sync
        def _(sp):
            sp.dma_start(X[:, 0:TB, :], x_t[:, 0:TB, :]).then_inc(x_in0, 16)
            for m in range(4):
                sp.dma_start(wraw[:, m, :, :], w_attn[m]).then_inc(w_in[m], 16)
                if m == 0:
                    sp.dma_start(bqkv_c[:, :, :], b_qkv).then_inc(small_in, 16)
                    sp.dma_start(bo_b[:, :], b_o.partition_broadcast(P)).then_inc(small_in, 16)
                    sp.dma_start(d_b[:, :], skip_d.partition_broadcast(P)).then_inc(small_in, 16)
                    sp.dma_start(wr[:, :, :], w_router).then_inc(small_in, 16)
            sp.dma_start(X[:, TB:TILES, :], x_t[:, TB:TILES, :]).then_inc(x_in, 16)

            sp.wait_ge(q_ready, 4 * B)
            sp.wait_ge(k_ready, 4 * B)
            sp.wait_ge(v_ready, TB * B)
            sp.dma_start(cx[:, :, :, :], ctx_rev).then_inc(cx_in, 16)

            def load_strip(h, r, first=False):
                if not first:
                    sp.wait_ge(y_full, h - NS + 1)
                src = kern_pad[bass.ds(h, 1), :]
                src = bass.AP(tensor=src.tensor, offset=src.offset, ap=[[1, P], [1, E]])
                sp.dma_start(strip[:, r, :], src).then_inc(strip_in[r], 16)

            sp.wait_ge(x1_ready, TB * B)
            for h in range(NS):
                load_strip(h, h, first=True)
            sp.wait_ge(qx_ready, TILES)
            with sp.Fori(1, MH // NS) as i:
                for r in range(NS):
                    load_strip(NS * i + r, r)
                sp.dma_start(wu[:, bass.ds(i, 1), :, :], w_up[:, bass.ds(i, 1), :, :]).then_inc(wx_in, 16)

            LATE = 2
            sp.wait_ge(mixed, MH)
            sp.dma_start(wu[:, 0, :, :], w_up[:, 0, :, :]).then_inc(wx_in, 16)
            for t in range(TILES):
                if t % 2:
                    sp.dma_start(wg[:, t // 2, :, :], w_gate[:, t // 2, :, :]).then_inc(wx_in, 16)
                elif t // 2 >= LATE:
                    sp.dma_start(wd[:, t // 2, :, :], w_down[:, t // 2, :, :]).then_inc(wx_in, 16)
                sp.wait_ge(ln3["out"], t + 1)
                sp.dma_start(h3_t[:, t, :], h3[:, t % 2, :]).then_inc(h3_stored[t % 2], 16)
            sp.wait_ge(idx_ready, 1)
            sp.dma_start(wd[:, 0:LATE, :, :], w_down[:, 0:LATE, :, :]).then_inc(wx_late, 16)

            def store_rows(j, r):
                sp.wait_ge(yo_ready, j + 1)
                sp.dma_start(y_t[:, bass.ds(j, 1), :], yo[:, r:r + 1, :]).then_inc(y_stored[r], 16)

            with sp.Fori(0, ROUNDS) as i:
                for r in range(4):
                    store_rows(4 * i + r, r)
            for j in range(4 * ROUNDS, SLOT_TILES):
                store_rows(j, j % 4)
            with sp.Fori(0, TILES // 4) as i:
                for r in range(4):
                    sp.wait_ge(res_ready, 4 * i + r + 1)
                    sp.dma_start(out_t[:, bass.ds(4 * i + r, 1), :], res[:, r:r + 1, :])\
                        .then_inc(sent[r], 16)
            for r in range(4):
                sp.wait_ge(sent[r], 16 * (TILES // 4))

        @block.gpsimd
        def _(pool):
            pool.memset(ident[:, :], 0.0).then_inc(consts, 1)
            pool.memset(mhalf[:, :], -0.5).then_inc(consts, 1)
            pool.iota(dist_i[:, :], pattern=[[1, S]], base=-P, channel_multiplier=-1).then_inc(consts, 1)
            pool.wait_ge(consts, 3)
            pool.affine_select(out=ident[:, :], in_=ident[:, :], compare_op=ALU.not_equal, fill=1.0,
                               base=0, pattern=[[-1, P]], channel_multiplier=1).then_inc(consts, 1)
            pool.tensor_copy(dist[:, :], dist_i[:, :]).then_inc(consts, 1)

            def carry():
                carried[1] = (carried[1] + 1) % 16
                pool.tensor_tensor(carrier[:, 48 + carried[1]:49 + carried[1]], mhalf[:, 0:1], mhalf[:, 0:1], ALU.add)

            def rstd(ln, var, dst, n):
                pool.wait_ge(ln["var"], n + 1)
                pool.tensor_tensor(dst[:, :], var[:, :], mhalf[:, :], ALU.pow).then_inc(ln["rstd"], 1)

            def add_bo(b):
                pool.wait_ge(ln1["out"], TB * b + TB)
                xs = X[:, bass.ds(TB * b, TB), :]
                pool.tensor_tensor(xs, xs, bo_b[:, :].unsqueeze(1).to_broadcast([P, TB, E]),
                                   ALU.add).then_inc(xb_ready, 1)

            rstd(ln1, ve1, rs1, 0)
            pool.iota(tok_i[:, :], pattern=[[P, TILES]], base=0, channel_multiplier=1).then_inc(tables, 1)
            pool.iota(iota_ji[:, :], pattern=[[1, SLOT_COLS]], base=0, channel_multiplier=0)\
                .then_inc(tables, 1)
            pool.iota(iota128[:, :], pattern=[[1, P]], base=0, channel_multiplier=0,
                      allow_small_or_imprecise_dtypes=True).then_inc(tables, 1)
            pool.memset(le8[:, :, :], 1.0).then_inc(tables, 1)
            pool.wait_ge(tables, 4)
            pool.tensor_copy(tok[:, :], tok_i[:, :]).then_inc(tables, 1)
            pool.tensor_copy(iota_j[:, :], iota_ji[:, :]).then_inc(tables, 1)
            pool.tensor_copy(iota8[:, :], iota_ji[:, 0:NX]).then_inc(tables, 1)
            pool.affine_select(out=le8[:, :, :], in_=le8[:, :, :], compare_op=ALU.is_ge, fill=0.0,
                               base=0, pattern=[[1, NX], [-1, NX]], channel_multiplier=0)\
                .then_inc(tables, 1)
            pool.wait_ge(tab_scaled, H)
            pool.affine_select(out=bias_tab[:, :, :], in_=bias_tab[:, :, :], compare_op=ALU.is_ge,
                               fill=MASKED, base=P, pattern=[[0, H], [-1, S]],
                               channel_multiplier=1).then_inc(tab_ready, 1)
            pool.wait_ge(small_in, 16 * 4)
            add_bo(0)

            def turn(b, first=False, last=False):
                if not last:
                    rstd(ln1, ve1, rs1, b + 1)
                    add_bo(b + 1)
                if not first:
                    rstd(ln2, ve2, rs2, b - 1)

            turn(0, first=True)
            with pool.Fori(1, B - 1) as b:
                turn(b)
            turn(B - 1, last=True)
            rstd(ln2, ve2, rs2, B - 1)


            pool.wait_ge(x1_ready, TB * B)
            pool.wait_ge(av_done, H * B)
            pool.memset(anti[:, :], 0.0).then_inc(consts, 1)
            pool.wait_ge(consts, 6)
            pool.affine_select(out=anti[:, :], in_=anti[:, :], compare_op=ALU.not_equal, fill=1.0,
                               base=-(P - 1), pattern=[[1, P]], channel_multiplier=1).then_inc(consts, 1)
            pool.wait_ge(cx_in, 16)

            def products(h, r, free):
                if free:
                    pool.wait_ge(y_full, h - KV + 1)
                c = cx[:, :, bass.ds(h, 1), :].squeeze(2)
                pool.tensor_tensor(kv[:, r, :, :].rearrange("p n (d i) -> p n d i", d=DIAGS),
                                   c[:, :, 0:MD].unsqueeze(2).to_broadcast([P, EC * B, DIAGS, MD]),
                                   windows(c, [[MW * MH, EC * B], [1, DIAGS], [1, MD]]),
                                   ALU.mult).then_inc(kv_ready, 1)

            for h in range(KV):
                if h == KV - 1:
                    pool.wait_ge(qx_ready, TILES)
                products(h, h, False)
            with pool.Fori(1, MH // KV) as i:
                for r in range(KV):
                    products(KV * i + r, r, True)

            for t in range(TILES):
                c = t % 2
                pool.wait_ge(ln3["var"], t + 1)
                pool.tensor_tensor(rs3[:, c:c + 1], ve3[:, c:c + 1], mhalf[:, 0:1], ALU.pow)\
                    .then_inc(ln3["rstd"], 1)
            pool.wait_ge(x2T_full, TILES)
            pool.memset(ones[:, :].bitcast(F32), 1.0).then_inc(tables, 1)
            pool.memset(upper_f[:, :], 1.0).then_inc(tables, 1)
            pool.memset(padded[:, 0:TILES, :].bitcast(F32), 0.0).then_inc(tables, 1)
            pool.wait_ge(tables, 11)
            pool.affine_select(out=upper_f[:, :], in_=upper_f[:, :], compare_op=ALU.is_gt, fill=0.0,
                               base=0, pattern=[[1, P]], channel_multiplier=-1).then_inc(tables, 1)
            pool.wait_ge(tables, 12)
            pool.tensor_copy(upper[:, :], upper_f[:, :]).then_inc(tables, 1)

            pool.wait_ge(idx_ready, 1)
            for r in range(2):
                pool.wait_ge(h3_stored[r], 16 * (TILES // 2))

            def gather(j, r, free):
                if free:
                    pool.wait_ge(xT_full, j - 3)
                pool.tensor_copy(gcol[:, r:r + 1], idx[:, bass.ds(j, 1)]).then_inc(gcol_ready, 1)
                pool.wait_ge(gcol_ready, j + 1)
                carry()
                pool.indirect_dma_start(
                    out=xg[:, r, :], out_offset=None, in_=h3_d[:, :],
                    in_offset=bass.IndirectOffsetOnAxis(ap=gcol[:, r:r + 1], axis=0),
                ).then_inc(gathered[r], 16)

            for r in range(4):
                gather(r, r, False)
            with pool.Fori(1, ROUNDS) as i:
                for r in range(4):
                    gather(4 * i + r, r, True)
            for j in range(4 * ROUNDS, SLOT_TILES):
                gather(j, j % 4, True)

            def fetch(i, half, free):
                pool.tensor_copy(fcol[:, half, :, :],
                                 slot[:, :, bass.ds(4 * i, 4)].rearrange("p k t -> p t k"))\
                    .then_inc(fcol_ready, 1)
                pool.wait_ge(fcol_ready, i + 1)
                carry()
                for r in range(4):
                    if free:
                        pool.wait_ge(res_ready, 4 * i + r - 3)
                        carry()
                    for k in range(TOPK):
                        pool.indirect_dma_start(
                            out=ga[:, r, k, :], out_offset=None, in_=y_d[:, :],
                            in_offset=bass.IndirectOffsetOnAxis(ap=fcol[:, half, r, k:k + 1], axis=0),
                        ).then_inc(fetched[r], 16)

            for r in range(4):
                pool.wait_ge(y_stored[r], 16 * ((SLOT_TILES - r + 3) // 4))
            for i in range(TILES // 4):
                fetch(i, i % 2, i >= 1)

        @block.scalar
        def _(act_e):
            def hT_hi(n, pos_n):
                for t in range(TB):
                    act_e.wait_ge(misc_full, n + t + 1)
                    act_e.activation(hTh[:, :, P * t:P * t + P],
                                     ps[:, bank(pos_n + t), :].rearrange("p (c q) -> p c q", c=EC),
                                     ACT.Copy).then_inc(ht_hi, 1)

            def oT_hi(b, k):
                act_e.wait_ge(av_done, H * b + HB * k + HB)
                for g in (2 * k, 2 * k + 1):
                    act_e.activation(oTh[:, g, :], ps[:, OB[k], S * (g % 2):S * (g % 2) + S],
                                     ACT.Identity, bias=bqkv_c[:, 2, g:g + 1]).then_inc(ot_hi, 1)

            def move_pT(b, h):
                act_e.wait_ge(pt_full, H * b + h + 1)
                act_e.activation(pT[:, h % NE, :], ps[:, PB[h % 2], 0:3 * P],
                                 ACT.Copy).then_inc(pt_act, 1)

            def exps(b, g):
                act_e.wait_ge(nm_ready, H // 2 * b + g + 1)
                for h in (2 * g, 2 * g + 1):
                    if h >= NE:
                        act_e.wait_ge(pt_full, H * b + h - NE + 1)
                    act_e.activation(pr[:, h % NE, 0:P], sc[:, h % NE, 0:P], ACT.Exp,
                                     bias=nm[:, h, 0:1], accum_out=sums[:, h, 0:1])
                    act_e.activation(pr[:, h % NE, P:3 * P], sc[:, h % NE, P:3 * P], ACT.Exp,
                                     bias=nm[:, h, 1:2], accum_out=sums[:, h, 1:2]).then_inc(p_ready, 1)

            def x1T(b, n, pos_n):
                for t in range(TB):
                    act_e.wait_ge(misc_full, n + t + 1)
                    act_e.activation(QX[:, :, bass.ds(S * b + P * t, P)],
                                     ps[:, bank(pos_n + t), :].rearrange("p (c q) -> p c q", c=EC),
                                     ACT.Copy).then_inc(qx_ready, 1)

            for m in range(4):
                act_e.wait_ge(w_in[m], 16)
                act_e.activation(whi[:, HI_AT[m], :, :], wraw[:, m, :, :], ACT.Copy).then_inc(wsplit_hi, 1)
                if m == 0:
                    hT_hi(0, 0)

            def turn(b, first=False, last=False):
                u = units_before(b, first)
                pos = positions(first, last)
                if first:
                    act_e.wait_ge(small_in, 16 * 4)
                for g in range(H // HG):
                    n = K0 + g
                    act_e.wait_ge(misc_full, u + n + 1)
                    act_e.activation(kT[:, g, :], ps[:, bank(n), 0:S], ACT.Identity,
                                     bias=bqkv_c[:, 1, g:g + 1]).then_inc(k_ready, 1)
                for t in range(TB):
                    act_e.wait_ge(misc_full, u + pos["v"] + t + 1)
                    act_e.activation(v[:, t, :], ps[:, bank(pos["v"] + t), :], ACT.Copy)\
                        .then_inc(v_ready, 1)
                for g in range(-1, H // 2):
                    if g + 1 < H // 2:
                        exps(b, g + 1)
                    for h in (2 * g, 2 * g + 1):
                        if g >= 0 and pt_on_act(h):
                            move_pT(b, h)
                    if g == 2 and not last:
                        hT_hi(u + pos["hT"], pos["hT"])
                    if g == 5:
                        oT_hi(b, 0)
                    if g == 6 and not first:
                        x1T(b - 1, u + pos["x1T"], pos["x1T"])
                oT_hi(b, 1)

            turn(0, first=True)
            with act_e.Fori(1, B - 1) as b:
                turn(b)
            turn(B - 1, last=True)
            x1T(B - 1, UNITS_END + TB, 0)


            def widen(h, r, free):
                if free:
                    act_e.wait_ge(y_read, h - 1)
                q = mixer_rows(h)
                act_e.activation(qe[:, r % 2, :, 0:MD], q, ACT.Copy)
                act_e.activation(qe[:, r % 2, :, MD:MW], q[:, :, 0:MW - MD], ACT.Copy)\
                    .then_inc(qe_ready, 1)

            act_e.wait_ge(qx_ready, TILES)
            for h in range(2):
                widen(h, h, False)
            with act_e.Fori(1, MH // 2) as i:
                for r in range(2):
                    widen(2 * i + r, r, True)

            for t in range(TILES):
                act_e.wait_ge(h3T_full, t + 1)
                if t >= 2:
                    act_e.wait_ge(logits_full, t - 1)
                act_e.activation(h3T[:, t % 2, :, :], ps[:, 2 + t % 2, :].rearrange("p (c q) -> p c q", c=EC),
                                 ACT.Copy).then_inc(h3T_ready, 1)
            act_e.wait_ge(shifted, 1)
            act_e.activation(topx[:, :, :], topx[:, :, :], ACT.Exp).then_inc(numer, 1)

            def rows_T(j, r, free):
                act_e.wait_ge(xT_full, j + 1)
                if free:
                    act_e.wait_ge(gate_full, j - 1)
                act_e.activation(xgT[:, r % 2, :, :], ps[:, 0, :].rearrange("p (c q) -> p c q", c=EC),
                                 ACT.Copy).then_inc(xT_ready, 1)

            def silu(j, r, free):
                act_e.wait_ge(up_full, j + 1)
                if free:
                    act_e.wait_ge(gu_ready, j - 1)
                act_e.activation(act[:, r % 2, :], ps[:, 1, 0:F], ACT.Silu).then_inc(act_ready, 1)

            def rows_out(j, r, free):
                act_e.wait_ge(down_full, j + 1)
                if free:
                    act_e.wait_ge(y_stored[r], 4 * (j - r))
                act_e.activation(yo[:, r, :], ps[:, 4 + r % 2, :], ACT.Copy).then_inc(yo_ready, 1)

            rows_T(0, 0, False)
            for j in range(4):
                silu(j, j, j >= 2)
                rows_T(j + 1, (j + 1) % 4, j + 1 >= 2)
                if j >= 1:
                    rows_out(j - 1, j - 1, False)
            with act_e.Fori(1, ROUNDS) as i:
                for r in range(4):
                    silu(4 * i + r, r, True)
                    rows_T(4 * i + r + 1, (r + 1) % 4, True)
                    rows_out(4 * i + r - 1, (r - 1) % 4, True)
            for j in range(4 * ROUNDS, SLOT_TILES):
                silu(j, j % 4, True)
                if j + 1 < SLOT_TILES:
                    rows_T(j + 1, (j + 1) % 4, True)
                rows_out(j - 1, (j - 1) % 4, True)
            rows_out(SLOT_TILES - 1, (SLOT_TILES - 1) % 4, True)

        @block.vector
        def _(dve):
            def carry():
                carried[0] = (carried[0] + 1) % 48
                dve.memset(carrier[:, carried[0]:carried[0] + 1], 0.0)

            def layer_stats(ln, src, st, mv, ve, n):
                for t in range(TB):
                    dve.bn_stats(st[:, t, :], src(t)).then_inc(ln["stats"], 1)
                dve.wait_ge(ln["stats"], TB * n + TB)
                carry()
                for t in range(TB):
                    dve.bn_aggr(mv[:, t, :], st[:, t, :]).then_inc(ln["aggr"], 1)
                dve.wait_ge(ln["aggr"], TB * n + TB)
                dve.tensor_scalar(ve[:, :], mv[:, :, 1], EPS, None, ALU.add).then_inc(ln["var"], 1)

            def layer_out(ln, src, dst, mv, rs, n):
                dve.wait_ge(ln["rstd"], n + 1)
                for t in range(TB):
                    dve.tensor_scalar(dst[:, t, :], src(t), mv[:, t, 0:1], rs[:, t:t + 1],
                                      ALU.subtract, ALU.mult).then_inc(ln["out"], 1)

            def x_tile(b):
                return lambda t: X[:, bass.ds(TB * b + t, 1), :].squeeze(1)

            def hT_lo(done, pos_n):
                for t in range(TB):
                    dve.wait_ge(ht_hi, done + t + 1)
                    n = pos_n + t
                    cols = slice(P * t, P * t + P)
                    dve.tensor_tensor(hTl[:, :, cols], ps[:, bank(n), :].rearrange("p (c q) -> p c q", c=EC),
                                      hTh[:, :, cols].bitcast(F32), ALU.subtract).then_inc(ht_lo, 1)

            def scores(b, g):
                for h in (2 * g, 2 * g + 1):
                    if h >= NE:
                        dve.wait_ge(p_ready, H * b + h - NE + 1)
                    dve.wait_ge(s_full, H * b + h + 1)
                    carry()
                    bank_h = SB[h % 2]
                    dve.tensor_tensor_reduce(sc[:, h % NE, 0:P], ps[:, bank_h, 0:P],
                                             bias_tab[:, h, P:2 * P], 1.0, MASKED, ALU.add, ALU.max,
                                             mx[:, h, 0:1])
                    dve.tensor_tensor_reduce(sc[:, h % NE, P:3 * P], ps[:, bank_h, P:3 * P],
                                             bias_tab[:, h, :], 1.0, MASKED, ALU.add, ALU.max,
                                             mx[:, h, 1:2]).then_inc(s_read, 1)
                dve.wait_ge(s_read, H * b + 2 * g + 2)
                dve.tensor_scalar(nm[:, 2 * g:2 * g + 2, :], mx[:, 2 * g:2 * g + 2, :], -1.0, None,
                                  ALU.mult).then_inc(nm_ready, 1)

            def move_pT(b, h):
                dve.wait_ge(pt_full, H * b + h + 1)
                dve.tensor_copy(pT[:, h % NE, :], ps[:, PB[h % 2], 0:3 * P]).then_inc(pt_dve, 1)

            def divide(b, g):
                dve.wait_ge(p_ready, H * b + 2 * g + 2)
                dve.reciprocal(rsum[:, 2 * g:2 * g + 2, :], sums[:, 2 * g:2 * g + 2, :])\
                    .then_inc(rsum_ready, 1)
                dve.wait_ge(rsum_ready, H // 2 * b + g + 1)
                for h in (2 * g, 2 * g + 1):
                    for t in range(TB):
                        p_t = pr[:, h % NE, P * t:P + 2 * P * t]
                        ins = dve.tensor_scalar(p_t, p_t, rsum[:, h, t:t + 1], None, ALU.mult)
                    ins.then_inc(pn_ready, 1)

            def oT_lo(b, k):
                dve.wait_ge(ot_hi, 4 * b + 2 * k + 2)
                for g in (2 * k, 2 * k + 1):
                    dve.scalar_tensor_tensor(out=oTl[:, g, :], in0=ps[:, OB[k], S * (g % 2):S * (g % 2) + S],
                                             scalar=bqkv_c[:, 2, g:g + 1], in1=oTh[:, g, :].bitcast(F32),
                                             op0=ALU.add, op1=ALU.subtract).then_inc(ot_lo, 1)

            def add_attention(b, n, pos_n):
                dve.wait_ge(xb_ready, b + 1)
                for t in range(TB):
                    dve.wait_ge(misc_full, n + t + 1)
                    xs = X[:, bass.ds(TB * b + t, 1), :].squeeze(1)
                    dve.tensor_tensor(xs, ps[:, bank(pos_n + t), :], xs, ALU.add)\
                        .then_inc(x1_ready, 1)

            dve.wait_ge(x_in0, 16)
            layer_stats(ln1, x_tile(0), st1, mv1, ve1, 0)
            dve.wait_ge(consts, 5)
            for h in range(H):
                dve.tensor_scalar(bias_tab[:, h, :], dist[:, :], 2.0 ** (-8.0 * (h + 1) / H), None,
                                  ALU.mult).then_inc(tab_scaled, 1)
            layer_out(ln1, x_tile(0), hn, mv1, rs1, 0)
            for m in range(4):
                dve.wait_ge(wsplit_hi, m + 1)
                dve.tensor_tensor(wlo[:, m, :, :], wraw[:, m, :, :], whi[:, HI_AT[m], :, :].bitcast(F32),
                                  ALU.subtract).then_inc(wsplit_lo, 1)
                if m == 0:
                    hT_lo(0, 0)

            def turn(b, first=False, last=False):
                u = units_before(b, first)
                pos = positions(first, last)
                if first:
                    dve.wait_ge(small_in, 16 * 4)
                for g in range(H // HG):
                    dve.wait_ge(misc_full, u + Q0 + g + 1)
                    dve.tensor_scalar(qT[:, g, :], ps[:, bank(Q0 + g), 0:S], bqkv_c[:, 0, g:g + 1],
                                      HD ** -0.5, ALU.add, ALU.mult).then_inc(q_ready, 1)
                if first:
                    dve.wait_ge(tab_ready, 1)
                    dve.wait_ge(x_in, 16)
                else:
                    add_attention(b - 1, u + pos["wo"], pos["wo"])
                for g in range(-2, H // 2):
                    if g + 2 < H // 2:
                        scores(b, g + 2)
                    if 0 <= g + 1 < H // 2:
                        divide(b, g + 1)
                    for h in (2 * g, 2 * g + 1):
                        if g >= 0 and not pt_on_act(h):
                            move_pT(b, h)
                    if not last:
                        if g == -1:
                            layer_stats(ln1, x_tile(b + 1), st1, mv1, ve1, b + 1)
                        if g == 1:
                            layer_out(ln1, x_tile(b + 1), hn, mv1, rs1, b + 1)
                        if g == 3:
                            hT_lo(TB * b + TB, pos["hT"])
                    if not first:
                        if g == 0:
                            dve.wait_ge(x1_ready, TB * b)
                            carry()
                            layer_stats(ln2, x_tile(b - 1), st2, mv2, ve2, b - 1)
                        if g == 4:
                            layer_out(ln2, x_tile(b - 1), hn, mv2, rs2, b - 1)
                    if g == 6:
                        oT_lo(b, 0)
                oT_lo(b, 1)

            turn(0, first=True)
            with dve.Fori(1, B - 1) as b:
                turn(b)
            turn(B - 1, last=True)
            add_attention(B - 1, UNITS_END, 0)
            dve.wait_ge(x1_ready, TB * B)
            layer_stats(ln2, x_tile(B - 1), st2, mv2, ve2, B - 1)
            layer_out(ln2, x_tile(B - 1), hn, mv2, rs2, B - 1)


            def prepare(h, r):
                dve.wait_ge(strip_in[r], 16 if isinstance(h, int) and h < NS else 4 * (h - r) + 16)
                dve.scalar_tensor_tensor(out=strip[:, r, 0:P], in0=anti[:, :],
                                         scalar=d_b[:, bass.ds(h, 1)], in1=strip[:, r, 0:P],
                                         op0=ALU.mult, op1=ALU.add).then_inc(strip_fixed, 1)

            def contract(h, r):
                y = convolved(r)
                q = qe[:, r % 2, :, :]
                z = terms[:, :, :]
                dims = [[MW, EC * B]]

                def grid(a, start, pitch, rows, width):
                    return a[:, :, start:start + rows * pitch]\
                        .rearrange("p n (d i) -> p n d i", i=pitch)[:, :, :, 0:width]

                dve.wait_ge(qe_ready, h + 1)
                dve.wait_ge(y_full, h + 1)
                dve.tensor_tensor(grid(z, DIAGS * SKEW, SKEW, MIRROR, MIRROR),
                                  grid(y, 2 * MD - 1, MD - 1, MIRROR, MIRROR),
                                  windows(q, dims + [[-1, MIRROR], [1, MIRROR]], MD - 1), ALU.mult)\
                    .then_inc(wrapped, 1)
                dve.tensor_tensor(grid(z, 0, SKEW, DIAGS, MD), grid(y, 0, MD, DIAGS, MD),
                                  windows(q, dims + [[1, DIAGS], [1, MD]]), ALU.mult)
                dve.wait_ge(wrapped, h + 1)
                dve.tensor_tensor(grid(z, DIAGS * SKEW + 1, SKEW + 1, MIRROR, MD),
                                  grid(y, MD, MD, MIRROR, MD),
                                  windows(q, dims + [[0, MIRROR], [1, MD]]), ALU.mult).then_inc(y_read, 1)
                dve.wait_ge(y_read, h + 1)
                carry()
                dve.tensor_reduce(mixer_rows(h),
                                  terms[:, :, 0:MD * SKEW].rearrange("p n (r j) -> p n j r", r=MD)[:, :, 0:MD, :],
                                  AX.X, ALU.add).then_inc(mixed, 1)
                dve.wait_ge(mixed, h + 1)

            dve.wait_ge(consts, 7)
            dve.wait_ge(qx_ready, TILES)
            for h in range(NS - 1):
                prepare(h, h)
            with dve.Fori(0, MH // NS - 1) as i:
                for r in range(NS):
                    prepare(NS * i + r + NS - 1, (r + NS - 1) % NS)
                    contract(NS * i + r, r)
            for h in range(MH - NS, MH):
                if h + NS - 1 < MH:
                    prepare(h + NS - 1, (h + NS - 1) % NS)
                contract(h, h % NS)

            def normalise(t):
                dve.wait_ge(ln3["rstd"], t + 1)
                if t >= 2:
                    dve.wait_ge(h3T_full, t - 1)
                    dve.wait_ge(h3_stored[t % 2], 16 * (t // 2))
                dve.tensor_scalar(h3[:, t % 2, :], X[:, t, :], mv3[:, t % 2, 0:1],
                                  rs3[:, t % 2:t % 2 + 1], ALU.subtract, ALU.mult)\
                    .then_inc(ln3["out"], 1)

            for t in range(TILES):
                dve.wait_ge(x2T_full, t + 1)
                dve.tensor_tensor(X[:, t, :], ps[:, t % 2, :], X[:, t, :], ALU.add).then_inc(x2_ready, 1)
                if t >= 1:
                    normalise(t - 1)
                dve.wait_ge(x2_ready, t + 1)
                dve.bn_stats(st3[:, t % 2, :], X[:, t, :]).then_inc(ln3["stats"], 1)
                dve.wait_ge(ln3["stats"], t + 1)
                dve.bn_aggr(mv3[:, t % 2, :], st3[:, t % 2, :]).then_inc(ln3["aggr"], 1)
                dve.wait_ge(ln3["aggr"], t + 1)
                dve.tensor_scalar(ve3[:, t % 2:t % 2 + 1], mv3[:, t % 2, 1:2], EPS, None, ALU.add)\
                    .then_inc(ln3["var"], 1)
            normalise(TILES - 1)

            steps = 0

            def step(ins):
                nonlocal steps
                steps += 1
                ins.then_inc(route, 1)
                dve.wait_ge(route, steps)

            dve.wait_ge(logits_full, TILES)
            step(dve.tensor_copy(logits[:, :, :], ps[:, 4, 0:TILES * NX].rearrange("p (t e) -> p t e", e=NX)))
            for t in range(TILES):
                ins = dve.max(top[:, t, :], logits[:, t, :])
            step(ins)
            for t in range(TILES):
                ins = dve.max_index(topi[:, t, :], top[:, t, :], logits[:, t, :])
            step(ins)
            dve.tensor_tensor(topx[:, :, :], top[:, :, :], top[:, :, 0:1].to_broadcast([P, TILES, 8]),
                              ALU.subtract).then_inc(shifted, 1)
            step(dve.tensor_copy(idxf[:, :, :], topi[:, :, 0:TOPK].rearrange("p t k -> p k t")))
            for k in range(TOPK):
                ins = dve.tensor_tensor(hot[:, k, :, :], iota8[:, :].unsqueeze(1).to_broadcast([P, TILES, NX]),
                                        idxf[:, k, :].unsqueeze(2).to_broadcast([P, TILES, NX]),
                                        ALU.is_equal)
            step(ins)
            step(dve.tensor_tensor(picked, hot[:, 0, :, :], hot[:, 1, :, :], ALU.add))
            dve.tensor_reduce(cnt[:, :], picked.bitcast(F32).rearrange("p t e -> p e t"), AX.X, ALU.add)\
                .then_inc(picked_ready, 1)
            dve.wait_ge(numer, 1)
            step(dve.tensor_reduce(zsum[:, :], topx[:, :, :], AX.X, ALU.add))
            step(dve.reciprocal(zrec[:, :], zsum[:, :]))
            step(dve.tensor_tensor(gate[:, :, :], topx[:, :, 0:TOPK],
                                   zrec[:, :].unsqueeze(2).to_broadcast([P, TILES, TOPK]), ALU.mult))
            step(dve.tensor_reduce(psum2[:, :], gate[:, :, :], AX.X, ALU.add))
            step(dve.reciprocal(prec2[:, :], psum2[:, :]))
            step(dve.tensor_tensor(gate[:, :, :], gate[:, :, :],
                                   prec2[:, :].unsqueeze(2).to_broadcast([P, TILES, TOPK]), ALU.mult))
            dve.tensor_scalar(iota16[:, :], iota_j[:, 0:TILES], float(P), None, ALU.mult)
            dve.wait_ge(ranks_full, 1)
            dve.tensor_copy(ranks[:, :, :], ps[:, 5, 0:TILES * NX].rearrange("p (t e) -> p t e", e=NX))
            step(dve.tensor_copy(count[:, :], ps[:, 6, 0:NX]))
            c3 = cmp[:, 0:NX * TILES].rearrange("p (e k) -> p e k", e=NX)
            step(dve.tensor_tensor(c3, count[:, :].unsqueeze(2).to_broadcast([P, NX, TILES]),
                                   iota16[:, :].unsqueeze(1).to_broadcast([P, NX, TILES]), ALU.is_gt))
            step(dve.tensor_reduce(ntile[:, :], c3, AX.X, ALU.add))
            c3 = cmp[:, 0:NX * NX].rearrange("p (e k) -> p e k", e=NX)
            step(dve.tensor_tensor(c3, ntile[:, :].unsqueeze(1).to_broadcast([P, NX, NX]), le8[:, :, :],
                                   ALU.mult))
            step(dve.tensor_reduce(cumt[:, :], c3, AX.X, ALU.add))
            step(dve.tensor_tensor(base[:, :], cumt[:, :], ntile[:, :], ALU.subtract))
            step(dve.scalar_tensor_tensor(out=ranks[:, :, :],
                                          in0=base[:, :].unsqueeze(1).to_broadcast([P, TILES, NX]),
                                          scalar=float(P), in1=ranks[:, :, :], op0=ALU.mult, op1=ALU.add))
            for k in range(TOPK):
                ins = dve.tensor_tensor(hot[:, k, :, :], hot[:, k, :, :], ranks[:, :, :], ALU.mult)
            step(ins)
            step(dve.tensor_reduce(slotf[:, :, :], hot[:, :, :, :], AX.X, ALU.add))
            step(dve.tensor_copy(slot[:, :, :], slotf[:, :, :]))
            dve.tensor_single_scalar(sdiv[:, :, :], slot[:, :, :], P.bit_length() - 1, ALU.arith_shift_right)
            step(dve.tensor_single_scalar(smod[:, :, :], slot[:, :, :], P - 1, ALU.bitwise_and))
            dve.tensor_copy(sdivf[:, :, :], sdiv[:, :, :])
            step(dve.tensor_copy(smodf[:, :, :], smod[:, :, :]))
            for k in range(TOPK):
                for t in range(TILES):
                    n = TILES * k + t
                    dve.tensor_scalar(hot_p[:, n, :], iota128[:, :], smodf[:, k, t:t + 1], None,
                                      ALU.is_equal)
                    dve.tensor_scalar(hot_j[:, n, :], iota_j[:, :], sdivf[:, k, t:t + 1],
                                      tok[:, t:t + 1], ALU.is_equal, ALU.mult).then_inc(hot_ready, 1)
            c3 = cmp[:, :].rearrange("p (j e) -> p j e", e=NX)
            step(dve.tensor_tensor(c3, cumt[:, :].unsqueeze(1).to_broadcast([P, SLOT_TILES, NX]),
                                   iota_j[:, 0:SLOT_TILES].unsqueeze(2).to_broadcast([P, SLOT_TILES, NX]), ALU.is_le))
            step(dve.tensor_reduce(eidf[:, :], c3, AX.X, ALU.add))
            step(dve.tensor_scalar(eid[:, :], eidf[:, :], float(NX - 1), None, ALU.min))
            dve.wait_ge(idx_full, 1)
            dve.tensor_copy(idx[:, :], ps[:, 7, 0:SLOT_COLS]).then_inc(idx_ready, 1)

            def rows_gu_T(j, r, free):
                dve.wait_ge(guT_full, j + 1)
                if free:
                    dve.wait_ge(down_full, j - 1)
                dve.tensor_copy(guT[:, r % 2, 0:FC - 1, :],
                                ps[:, 3, 0:(FC - 1) * P].rearrange("p (c q) -> p c q", q=P))
                dve.tensor_copy(guT[0:FLAST, r % 2, FC - 1, :], ps[0:FLAST, 3, (FC - 1) * P:FC * P])\
                    .then_inc(guT_ready, 1)

            def gated(j, r, free):
                dve.wait_ge(act_ready, j + 1)
                dve.wait_ge(gate_full, j + 1)
                if free:
                    dve.wait_ge(guT_full, j - 1)
                dve.tensor_tensor(gu[:, r % 2, :], ps[:, 2, 0:F], act[:, r % 2, :], ALU.mult)\
                    .then_inc(gu_ready, 1)

            for j in range(4):
                if j >= 1:
                    rows_gu_T(j - 1, j - 1, j - 1 >= 2)
                gated(j, j, j >= 2)
            with dve.Fori(1, ROUNDS) as i:
                for r in range(4):
                    rows_gu_T(4 * i + r - 1, (r - 1) % 4, True)
                    gated(4 * i + r, r, True)
            for j in range(4 * ROUNDS, SLOT_TILES):
                rows_gu_T(j - 1, (j - 1) % 4, True)
                gated(j, j % 4, True)
            rows_gu_T(SLOT_TILES - 1, (SLOT_TILES - 1) % 4, True)

            def combine(t, r, free):
                dve.wait_ge(fetched[r], 8 * (t - r) + 32)
                if free:
                    dve.wait_ge(sent[r], 4 * (t - r))
                xs = X[:, bass.ds(t, 1), :].squeeze(1)
                g = gate[:, bass.ds(t, 1), :].squeeze(1)
                dve.scalar_tensor_tensor(out=res[:, r, :], in0=ga[:, r, 0, :], scalar=g[:, 0:1],
                                         in1=xs, op0=ALU.mult, op1=ALU.add).then_inc(half_done, 1)
                dve.wait_ge(half_done, t + 1)
                dve.scalar_tensor_tensor(out=res[:, r, :], in0=ga[:, r, 1, :], scalar=g[:, 1:2],
                                         in1=res[:, r, :], op0=ALU.mult, op1=ALU.add)\
                    .then_inc(res_ready, 1)

            for r in range(4):
                combine(r, r, False)
            with dve.Fori(1, TILES // 4) as i:
                for r in range(4):
                    combine(4 * i + r, r, True)

        @block.tensor
        def _(pe):
            def three_pass(dst, parts, n):
                for c in range(n):
                    for i in range(3):
                        lhs, rhs = parts(c, i)
                        mm = pe.matmul(dst, lhs, rhs, start=(c == 0 and i == 0),
                                       stop=(c == n - 1 and i == 2))
                return mm

            H_OF = (hTh, hTl, hTh)
            O_OF = (oTh, oTl, oTh)

            def w_of(i, m, c, cols=slice(0, E)):
                return wlo[:, m, c, cols] if i == 2 else whi[:, HI_AT[m], c, cols]

            def transposes(src, t, dst):
                for c in range(EC):
                    mm = pe.transpose(dst[:, P * c:P * c + P], src[:, t, P * c:P * c + P], ident[:, :])
                mm.then_inc(misc_full, 1)

            def rows_projection(parts, m, t, dst):
                three_pass(dst, lambda c, i: (parts[i][:, c, P * t:P * t + P], w_of(i, m, c)), EC)\
                    .then_inc(misc_full, 1)

            def project(b, pos, first):
                pe.wait_ge(ht_lo, TB * b + TB)
                for m in range(2):
                    if first:
                        pe.wait_ge(wsplit_lo, m + 1)
                    for g in range(H // HG):
                        n = (Q0, K0)[m] + g
                        if n in (Q0 + 2, Q0 + 3, K0, K0 + 1):
                            pe.wait_ge(q_ready, 4 * b + n - 1)
                        elif n > K0 + 1:
                            pe.wait_ge(k_ready, 4 * b + g - 1)
                        cols = slice(P * g, P * g + P)
                        three_pass(ps[:, bank(n), 0:S],
                                   lambda c, i: (w_of(i, m, c, cols), H_OF[i][:, c, :]), EC)\
                            .then_inc(misc_full, 1)
                if first:
                    pe.wait_ge(wsplit_lo, 3)
                else:
                    pe.wait_ge(ot_lo, 4 * b)
                    for t in range(TB):
                        pe.wait_ge(k_ready, 4 * b + 3 + t)
                        rows_projection(O_OF, 3, t, ps[:, bank(pos["wo"] + t), :])
                for t in range(TB):
                    if first:
                        pe.wait_ge(k_ready, 4 * b + 3 + t)
                    else:
                        pe.wait_ge(x1_ready, TB * b - TB + t + 1)
                    rows_projection(H_OF, 2, t, ps[:, bank(pos["v"] + t), :])

            def score(b, h, first):
                if not (first and h < 2):
                    pe.wait_ge(s_read, H * b + h - 1)
                r = slice(HD * (h % HG), HD * (h % HG) + HD)
                g = h // HG
                pe.matmul(ps[:, SB[h % 2], 0:P], qT[r, g, 0:P], kT[r, g, 0:P], start=True, stop=True)
                pe.matmul(ps[:, SB[h % 2], P:3 * P], qT[r, g, P:S], kT[r, g, :], start=True, stop=True)\
                    .then_inc(s_full, 1)

            def moved(b, h):
                if pt_on_act(h):
                    pe.wait_ge(pt_act, pt_count(b, h, True))
                else:
                    pe.wait_ge(pt_dve, pt_count(b, h, False))

            def probs_T(b, h):
                pe.wait_ge(pn_ready, H * b + h + 1)
                if h >= 2:
                    moved(b, h - 2)
                for i in range(3):
                    mm = pe.transpose(ps[:, PB[h % 2], P * i:P * i + P], pr[:, h % NE, P * i:P * i + P],
                                      ident[:, :])
                mm.then_inc(pt_full, 1)

            def values(b, h):
                moved(b, h)
                if h == 0:
                    pe.wait_ge(v_ready, TB * b + TB)
                d = slice(HD * h, HD * h + HD)
                o = ps[HD * (h % HG):HD * (h % HG) + HD, OB[h // HB], :]
                q0 = S * (h // HG % 2)
                pe.matmul(o[:, q0:q0 + S], v[:, 0, d], pT[:, h % NE, 0:2 * P], start=True, stop=False)
                pe.matmul(o[:, q0 + P:q0 + S], v[:, 1, d], pT[:, h % NE, 2 * P:3 * P], start=False,
                          stop=True).then_inc(av_done, 1)

            def next_hT(b, pos_n):
                pe.wait_ge(ln1["out"], TB * b + 2 * TB)
                for t in range(TB):
                    pe.wait_ge(v_ready, TB * b + t + 1)
                    transposes(hn, t, ps[:, bank(pos_n + t), :])

            def x1_T(b, pos_n, emptied, count):
                pe.wait_ge(ln2["out"], TB * b + TB)
                for t in range(TB):
                    pe.wait_ge(emptied, count + t + 1)
                    transposes(hn, t, ps[:, bank(pos_n + t), :])

            pe.wait_ge(consts, 5)
            pe.wait_ge(ln1["out"], TB)
            for t in range(TB):
                transposes(hn, t, ps[:, bank(t), :])

            def turn(b, first=False, last=False):
                pos = positions(first, last)
                project(b, pos, first)
                pe.wait_ge(q_ready, 4 * b + 4)
                pe.wait_ge(k_ready, 4 * b + 4)
                for g in range(-2, H // 2 + 1):
                    for h in (2 * g + 4, 2 * g + 5):
                        if h < H:
                            score(b, h, first)
                    for h in (2 * g, 2 * g + 1):
                        if 0 <= h < H:
                            probs_T(b, h)
                    for h in (2 * g - 2, 2 * g - 1):
                        if 0 <= h:
                            values(b, h)
                    if g == 2 and not last:
                        next_hT(b, pos["hT"])
                    if g == 6 and not first:
                        if last:
                            x1_T(b - 1, pos["x1T"], v_ready, TB * b)
                        else:
                            x1_T(b - 1, pos["x1T"], ht_lo, TB * b + TB)
                if not first:
                    pe.wait_ge(qx_ready, TB * b)

            turn(0, first=True)
            pe.wait_ge(wsplit_lo, 4)
            with pe.Fori(1, B - 1) as b:
                turn(b)
            turn(B - 1, last=True)
            pe.wait_ge(ot_lo, 4 * B)
            for t in range(TB):
                rows_projection(O_OF, 3, t, ps[:, bank(t), :])
            x1_T(B - 1, 0, x1_ready, TB * B - TB)

            def convolve(h, r, free):
                pe.wait_ge(strip_fixed, h + 1)
                pe.wait_ge(kv_ready, h + 1)
                if free:
                    pe.wait_ge(y_read, h - 1)
                for lo in range(EC):
                    for m in range(lo + 1):
                        mm = pe.matmul(convolved(r)[:, B * lo:B * lo + B, 0:PAIRS],
                                       strip[:, r, P * (lo - m):P * (lo - m) + P],
                                       kv[:, r, B * m:B * m + B, :],
                                       start=(m == 0), stop=(m == lo))
                mm.then_inc(y_full, 1)

            pe.wait_ge(x1_ready, TB * B)
            pe.wait_ge(qx_ready, TILES)
            for h in range(KV):
                convolve(h, h, h >= 2)
            with pe.Fori(1, MH // KV) as i:
                for r in range(KV):
                    convolve(KV * i + r, r, True)
            pe.wait_ge(mixed, MH)

            def x2_T(t):
                if t >= 2:
                    pe.wait_ge(x2_ready, t - 1)
                for c in range(EC):
                    mm = pe.transpose(ps[:, t % 2, P * c:P * c + P], QX[:, c, P * t:P * t + P], ident[:, :])
                mm.then_inc(x2T_full, 1)

            def h3_T(t):
                pe.wait_ge(ln3["out"], t + 1)
                if t >= 2:
                    pe.wait_ge(h3T_ready, t - 1)
                for c in range(EC):
                    mm = pe.transpose(ps[:, 2 + t % 2, P * c:P * c + P], h3[:, t % 2, P * c:P * c + P],
                                      ident[:, :])
                mm.then_inc(h3T_full, 1)

            def router(t):
                pe.wait_ge(h3T_ready, t + 1)
                for c in range(EC):
                    mm = pe.matmul(ps[:, 4, NX * t:NX * t + NX], h3T[:, t % 2, c, :], wr[:, c, :],
                                   start=(c == 0), stop=(c == EC - 1))
                mm.then_inc(logits_full, 1)

            for t in range(TILES + 3):
                if t < TILES:
                    x2_T(t)
                if 2 <= t < TILES + 2:
                    h3_T(t - 2)
                if t >= 3:
                    router(t - 3)

            pe.wait_ge(tables, 13)
            pe.wait_ge(picked_ready, 1)
            for back in range(TILES):
                pe.matmul(ps[:, 5, 0:TILES * NX], ones[:, :] if back else upper[:, :],
                          padded[:, TILES - back:2 * TILES - back, :].rearrange("p t e -> p (t e)"),
                          start=(back == 0), stop=(back == TILES - 1))
            pe.matmul(ps[:, 6, 0:NX], ones[:, :].bitcast(F32), cnt[:, :], start=True, stop=True).then_inc(ranks_full, 1)
            for n in range(TOPK * TILES):
                pe.wait_ge(hot_ready, n + 1)
                mm = pe.matmul(ps[:, 7, 0:SLOT_COLS], hot_p[:, n, :], hot_j[:, n, :],
                               start=(n == 0), stop=(n == TOPK * TILES - 1))
            mm.then_inc(idx_full, 1)

            pe.wait_ge(idx_ready, 1)
            pe.wait_ge(wx_in, 16 * (3 * NX - 2))
            pe.wait_ge(wx_late, 16)

            def expert(j):
                return pe.value_load(eid[0:1, bass.ds(j, 1)], min_val=0, max_val=NX - 1)

            def rows_T(j, r, free):
                pe.wait_ge(gathered[r], 4 * (j - r) + 16)
                if free:
                    pe.wait_ge(xT_ready, j)
                for c in range(EC):
                    mm = pe.transpose(ps[:, 0, P * c:P * c + P], xg[:, r, P * c:P * c + P], ident[:, :])
                mm.then_inc(xT_full, 1)

            def up(j, r, e, w, bank_w, full):
                for c in range(EC):
                    mm = pe.matmul(ps[:, bank_w, 0:F], xgT[:, r % 2, c, :],
                                   w[:, bass.ds(e, 1), c, :].squeeze(1), start=(c == 0), stop=(c == EC - 1))
                mm.then_inc(full, 1)

            def hidden_T(j, r, free):
                pe.wait_ge(gu_ready, j + 1)
                if free:
                    pe.wait_ge(guT_ready, j)
                for c in range(FC):
                    k = P if c < FC - 1 else FLAST
                    mm = pe.transpose(ps[0:k, 3, P * c:P * c + P], gu[:, r % 2, P * c:P * c + k], ident[:, :])
                mm.then_inc(guT_full, 1)

            def down(j, r, e, free):
                pe.wait_ge(guT_ready, j + 1)
                if free:
                    pe.wait_ge(yo_ready, j - 1)
                for c in range(FC):
                    k = P if c < FC - 1 else FLAST
                    mm = pe.matmul(ps[:, 4 + r % 2, :], guT[0:k, r % 2, c, :],
                                   wd[0:k, bass.ds(e, 1), c, :].squeeze(1), start=(c == 0), stop=(c == FC - 1))
                mm.then_inc(down_full, 1)

            def expert_tile(j, r, first=False, last=False):
                e = expert(j)
                pe.wait_ge(xT_ready, j + 1)
                if not first:
                    pe.wait_ge(act_ready, j)
                up(j, r, e, wu, 1, up_full)
                if not first:
                    hidden_T(j - 1, (r - 1) % 4, not (isinstance(j, int) and j == 1))
                    pe.wait_ge(gu_ready, j)
                up(j, r, e, wg, 2, gate_full)
                if not last:
                    rows_T(j + 1, (r + 1) % 4, True)
                if not first:
                    down(j - 1, (r - 1) % 4, expert(j - 1), not (isinstance(j, int) and j <= 2))

            rows_T(0, 0, False)
            for j in range(4):
                expert_tile(j, j, first=(j == 0))
            with pe.Fori(1, ROUNDS) as i:
                for r in range(4):
                    expert_tile(4 * i + r, r)
            for j in range(4 * ROUNDS, SLOT_TILES):
                expert_tile(j, j % 4, last=(j == SLOT_TILES - 1))
            hidden_T(SLOT_TILES - 1, (SLOT_TILES - 1) % 4, True)
            down(SLOT_TILES - 1, (SLOT_TILES - 1) % 4, expert(SLOT_TILES - 1), True)

        return nc


def kernel(**inputs):
    import numpy as _np
    import concourse.bacc as _bacc
    from concourse.bass_utils import run_bass_kernel_spmd as _run

    arrays = laid_out(inputs)
    nc = _bacc.Bacc("TRN2", target_bir_lowering=False, num_devices=1)
    args = [nc.dram_tensor(n, a.shape, mybir.dt.from_np(a.dtype), kind="ExternalInput").ap()
            for n, a in arrays.items()]
    out = nc.dram_tensor("out", (B, S, E), F32, kind="ExternalOutput").ap()
    decoder_block(nc, *args, out)
    r = _run(nc, [arrays], core_ids=[0])
    return r.results[0]["out"]


def laid_out(inputs):
    import numpy as np
    g = {k: np.asarray(v) for k, v in inputs.items()}

    def chunks(w):
        return w.reshape(-1, P, w.shape[-1]).transpose(1, 0, 2)

    def experts(w):
        n = -(-w.shape[1] // P) * P
        w = np.concatenate([w, np.zeros((w.shape[0], n - w.shape[1], w.shape[2]), w.dtype)], 1)
        return w.reshape(w.shape[0], -1, P, w.shape[2]).transpose(2, 0, 1, 3)

    w_attn = np.stack([chunks(g[f"L0_attn_W{m}"].T) for m in "qkvo"])
    b_qkv = np.stack([g[f"L0_attn_b{m}"].reshape(-1, P).T for m in "qkv"], 1)
    c = g["ctx_2048"].transpose(2, 0, 1).reshape(EC, P, B, S)[:, ::-1]
    c = c.transpose(1, 0, 2, 3).reshape(P, EC * B, MH, MD)
    ctx_rev = np.concatenate([c, c[..., :MW - MD]], -1)
    kern = g["L0_xattn_ssm_kernel"]
    kern_pad = np.concatenate([np.zeros((MH, P - 1), kern.dtype), kern], 1)
    out = {
        "x": g["x"], "w_attn": w_attn, "b_qkv": b_qkv, "b_o": g["L0_attn_bo"],
        "ctx_rev": ctx_rev, "kern_pad": kern_pad, "skip_d": g["L0_xattn_D"],
        "w_router": chunks(g["L0_ffn_w_router"].T),
        "w_up": experts(g["L0_ffn_w1"].transpose(0, 2, 1)),
        "w_gate": experts(g["L0_ffn_w3"].transpose(0, 2, 1)),
        "w_down": experts(g["L0_ffn_w2"].transpose(0, 2, 1)),
    }
    return {k: np.ascontiguousarray(a) for k, a in out.items()}
```

```python
from contextlib import ExitStack

import concourse.bass as bass
from concourse import mybir

P = 128
B, S, E = 8, 256, 512
TILES = B * S // P
TB = S // P
EC = E // P
H, HD = 16, 32
HG = P // HD
MH, MD = 32, 8
DIAGS = MD // 2 + 1
PAIRS = DIAGS * MD
MW = MD + DIAGS - 1
MIRROR = DIAGS - 2
SKEW = MD + MIRROR
TERMS = MD * SKEW + MIRROR + 1
NX, F = 8, 352
FC = (F + P - 1) // P
FLAST = F - (FC - 1) * P
TOPK = 2
SLOT_TILES = TILES * TOPK + NX - 1
SLOT_COLS = SLOT_TILES + SLOT_TILES % 2
ROUNDS = (SLOT_TILES - 1) // 4
EPS = 1e-5
KPAD = P - 1 + E
MASKED = -1e30

F32 = mybir.dt.float32
F32R = mybir.dt.float32r
I32 = mybir.dt.int32
U32 = mybir.dt.uint32
ALU = mybir.AluOpType
ACT = mybir.ActivationFunctionType
AX = mybir.AxisListType
KB = 1024


def decoder_block(nc, x, w_attn, b_qkv, b_o, ctx_rev, kern_pad, skip_d, w_router, w_up, w_gate,
                  w_down, out):
    ctx = ExitStack()
    with ctx:
        arena = (nc.sbuf_base + 63) // 64 * 64

        def at(name, shape, kb, dt=F32):
            return nc.alloc_sbuf_tensor_at(name, shape, dt, offset=arena + int(kb * KB))

        def sem(name):
            return ctx.enter_context(nc.semaphore(name))

        X = at("X", [P, TILES, E], 0)
        QX = at("QX", [P, EC, B * S], 32)
        ident = at("ident", [P, P], 200)
        mhalf = at("mhalf", [P, TB], 200.5)
        carrier = at("carrier", [P, 64], 200.75)
        carried = [0, 0]
        V_, Q_, K_, O_ = range(4)
        wraw = at("wraw", [P, 4, EC, E], 32)
        whi = at("whi", [P, 4, EC, E], 64, F32R)
        wlo = at("wlo", [P, 4, EC, E], 96, F32R)
        HI_AT = (1, 2, 3, 0)
        bias_tab = at("bias_tab", [P, H, S], 128)
        hn = at("hn", [P, TB, E], 144)
        hTh = at("hTh", [P, EC, S], 148, F32R)
        hTl = at("hTl", [P, EC, S], 152, F32R)
        qT, kT, oTh, oTl, v = [], [], [], [], []
        for n in range(2):
            qT.append(at(f"qT{n}", [P, H // HG, S], 156 + 8 * n))
            kT.append(at(f"kT{n}", [P, H // HG, S], 160 + 8 * n))
            oTh.append(at(f"oTh{n}", [P, EC, S], 156 + 8 * n, F32R))
            oTl.append(at(f"oTl{n}", [P, EC, S], 160 + 8 * n, F32R))
            v.append(at(f"v{n}", [P, TB, E], 172 + 4 * n))
        NE = 6
        sc = at("sc", [P, NE, 3 * P], 180)
        pT = at("pT", [P, NE, 3 * P], 189)
        dist = at("dist", [P, S], 189)
        dist_i = at("dist_i", [P, S], 190, I32)
        bo_b = at("bo_b", [P, E], 198)
        mx = at("mx", [P, H, TB], 201)
        nm = at("nm", [P, H, TB], 201.125)
        sums = at("sums", [P, H, TB], 201.25)
        rsum = at("rsum", [P, H, TB], 201.375)
        bqkv_c = at("bqkv_c", [P, 3, H // HG], 201.625)
        st1 = at("st1", [P, TB, 6], 201.75)
        st2 = at("st2", [P, TB, 6], 201.8125)
        mv1 = at("mv1", [P, TB, 2], 201.875)
        mv2 = at("mv2", [P, TB, 2], 201.9375)
        ve1 = at("ve1", [P, TB], 207.25)
        rs1 = at("rs1", [P, TB], 207.3125)
        ve2 = at("ve2", [P, TB], 207.375)
        rs2 = at("rs2", [P, TB], 207.4375)
        cx = at("cx", [P, EC * B, MH, MW], 72)
        NS = 4
        strip = at("strip", [P, NS, E], 120)
        KV = 4
        kv = at("kv", [P, KV, EC * B, PAIRS], 128)
        qe = at("qe", [P, 2, EC * B, MW], 64)
        terms = at("terms", [P, EC * B, TERMS], 148)
        anti = at("anti", [P, P], 201)
        d_b = at("d_b", [P, MH], 201.5)
        xraw = at("xraw", [P, 2, EC * F], 160)
        xlo = at("xlo", [P, 2, EC * F], 160, F32R)
        xhi = at("xhi", [P, 2, EC * F], 171, F32R)
        NW = 4
        PIECES = 5
        whl = at("whl", [P, NW, 2, 2, EC * F], 64, F32R)
        wd = at("wd", [P, NW, FC, E], 152)
        CB = 176
        NH = 4
        h3 = at("h3", [P, NH, E], CB)
        h3T = at("h3T", [P, 2, EC, P], CB + 12)
        lgT = at("lgT", [NX, 2, 4 * P], CB + 16)
        logits = at("logits", [P, TILES, NX], CB + 8)
        top = at("top", [P, TILES, 8], CB + 8.5)
        topi = at("topi", [P, TILES, 8], CB + 9, U32)
        topx = at("topx", [P, TILES, 8], CB + 9.5)
        padded = at("padded", [P, 2 * TILES, NX], CB + 10, F32R)
        picked = padded[:, TILES:2 * TILES, :]
        hot = at("hot", [P, TOPK, TILES, NX], CB + 11)
        zsum = at("zsum", [P, TILES], 202)
        zrec = at("zrec", [P, TILES], 202.0625)
        psum2 = at("psum2", [P, TILES], 202.125)
        prec2 = at("prec2", [P, TILES], 202.1875)
        gate = at("gate", [P, TILES, TOPK], 202.25)
        idxf = at("idxf", [P, TOPK, TILES], 202.375)
        slotf = at("slotf", [P, TOPK, TILES], 202.5)
        slot = at("slot", [P, TOPK, TILES], 202.625, I32)
        sdiv = at("sdiv", [P, TOPK, TILES], 202.75, I32)
        smod = at("smod", [P, TOPK, TILES], 202.875, I32)
        sdivf = at("sdivf", [P, TOPK, TILES], 203)
        smodf = at("smodf", [P, TOPK, TILES], 203.125)
        cnt = at("cnt", [P, NX], 203.25)
        count = at("count", [P, NX], 203.28125)
        ntile = at("ntile", [P, NX], 203.3125)
        cumt = at("cumt", [P, NX], 203.34375)
        base = at("base", [P, NX], 203.375)
        eidf = at("eidf", [P, SLOT_TILES], 203.5)
        eid = at("eid", [P, SLOT_TILES], 203.75, I32)
        cum_i = at("cum_i", [P, NX], 203.6875, I32)
        place = at("place", [P, SLOT_TILES], 205.5, I32)
        idx = at("idx", [P, SLOT_COLS], 204, I32)
        tok = at("tok", [P, TILES], 204.25)
        iota8 = at("iota8", [P, NX], 204.3125)
        dummy = at("dummy", [P, 1], 200.53125)
        padm = at("padm", [P, SLOT_COLS], 201)
        destf = at("destf", [P, SLOT_COLS], 201.25)
        dest = at("dest", [P, SLOT_COLS], 207.25, I32)
        iota16 = at("iota16", [P, TILES], 204.34375)
        iota_j = at("iota_j", [P, SLOT_COLS], 204.5)
        le8 = at("le8", [P, NX, NX], 204.75)
        st3 = at("st3", [P, 2, 6], 205)
        mv3 = at("mv3", [P, 2, 2], 205.0625)
        ve3 = at("ve3", [P, 2], 205.125)
        rs3 = at("rs3", [P, 2], 205.15625)
        gcol = at("gcol", [P, 4], 205.1875, U32)
        dcol = at("dcol", [P, 4], 205.25, U32)
        tok_i = at("tok_i", [P, TILES], 205.3125, I32)
        iota_ji = at("iota_ji", [P, SLOT_COLS], 205.5, I32)
        wr = at("wr", [P, EC, NX], 205.75)
        iota128 = at("iota128", [P, P], 206.25)
        gsplit = at("gsplit", [P, 2, TOPK, TILES], 201.625, F32R)
        glo = at("glo", [P, SLOT_COLS], 201)
        gslot = at("gslot", [P, SLOT_COLS], 207.5)
        ranks = at("ranks", [P, TILES, NX], 206.75)
        ones = at("ones", [P, P], 32, F32R)
        upper = at("upper", [P, P], 32.5, F32R)
        upper_f = at("upper_f", [P, P], 35)
        cmp = at("cmp", [P, SLOT_TILES * NX], 33)
        hot_p = at("hot_p", [P, TOPK * TILES, P], 35, F32R)
        hot_j = at("hot_j", [P, TOPK * TILES, SLOT_COLS], 51, F32R)
        hot_f = at("hot_f", [P, TOPK * TILES, SLOT_COLS], 56)
        HOT_TILES = 4
        HOT_PARTS = TILES // HOT_TILES
        hot_g = at("hot_g", [P, TOPK * TILES, 2, SLOT_COLS], 19, F32R)
        NG = 4
        xg = at("xg", [P, NG, E], 0)
        xgTh = at("xgTh", [P, 2, EC, P], 8, F32R)
        xgTl = at("xgTl", [P, 2, EC, P], 12, F32R)
        act = at("act", [P, 2, F], 16)
        gu = at("gu", [P, 2, F], 19)
        guT = at("guT", [P, 2, FC, P], 22)
        yo = at("yo", [P, 4, E], 25)

        ps = ctx.enter_context(nc.psum_tensor("ps", [P, 8, 512], F32))

        h3_d = nc.dram_tensor("h3_rows", [B * S, E], F32, kind="Internal").ap()
        split_d = nc.dram_tensor("split_weights", [P, NX, 2, 2, EC * F], F32, kind="Internal").ap()
        sum_d = nc.dram_tensor("sum_rows", [B * S + P, E], F32, kind="Internal").ap()

        x_t = x.rearrange("b (t p) e -> p (b t) e", p=P)
        out_rows = out.rearrange("b s e -> (b s) e")
        h3_t = h3_d.rearrange("(t p) e -> p t e", p=P)
        sum_t = sum_d.rearrange("(t p) e -> p t e", p=P)

        x_in0, x_in1, x_in = sem("x_in0"), sem("x_in1"), sem("x_in")
        w_in = [sem(f"w_in{m}") for m in range(4)]
        small_in = sem("small_in")
        wsplit_hi, wsplit_lo = sem("wsplit_hi"), sem("wsplit_lo")
        consts = sem("consts")
        tab_scaled, tab_ready = sem("tab_scaled"), sem("tab_ready")
        ln1 = {k: sem(f"ln1_{k}") for k in ("stats", "aggr", "var", "rstd", "out")}
        ln2 = {k: sem(f"ln2_{k}") for k in ("stats", "aggr", "var", "rstd", "out")}
        misc_full = sem("misc_full")
        ht_hi, ht_lo = sem("ht_hi"), sem("ht_lo")
        q_ready, k_ready, v_ready = sem("q_ready"), sem("k_ready"), sem("v_ready")
        s_full, s_read = sem("s_full"), sem("s_read")
        nm_ready, p_ready = sem("nm_ready"), sem("p_ready")
        pt_full, pt_dve, pt_act = sem("pt_full"), sem("pt_dve"), sem("pt_act")
        rsum_ready, pn_ready, av_done = sem("rsum_ready"), sem("pn_ready"), sem("av_done")
        ot_hi, ot_lo = sem("ot_hi"), sem("ot_lo")
        xb_ready, x1_ready, qx_ready = sem("xb_ready"), sem("x1_ready"), sem("qx_ready")
        cx_in = sem("cx_in")
        strip_in = [sem(f"strip_in{r}") for r in range(NS)]
        strip_fixed, kv_ready, qe_ready = sem("strip_fixed"), sem("kv_ready"), sem("qe_ready")
        wrapped = sem("wrapped")
        y_full, y_read, mixed = sem("y_full"), sem("y_read"), sem("mixed")
        x2T_full, x2_ready = sem("x2T_full"), sem("x2_ready")
        ln3 = {k: sem(f"ln3_{k}") for k in ("stats", "aggr", "var", "rstd", "out")}
        h3_stored = [sem(f"h3_stored{r}") for r in range(NH)]
        h3T_full, h3T_ready = sem("h3T_full"), sem("h3T_ready")
        lgT_full, lgT_ready, logits_full = sem("lgT_full"), sem("lgT_ready"), sem("logits_full")
        tables = sem("tables")
        route, shifted, numer = sem("route"), sem("shifted"), sem("numer")
        picked_ready, ranks_full = sem("picked_ready"), sem("ranks_full")
        hot_ready, idx_full, idx_ready = sem("hot_ready"), sem("idx_full"), sem("idx_ready")
        xraw_in = [sem("xraw_in0"), sem("xraw_in1")]
        xhi_ready = [sem("xhi_ready0"), sem("xhi_ready1")]
        xlo_ready = [sem("xlo_ready0"), sem("xlo_ready1")]
        xsplit_stored = [sem("xsplit_stored0"), sem("xsplit_stored1")]
        w_loaded = sem("w_loaded")
        gcol_ready = sem("gcol_ready")
        gathered = [sem(f"gathered{r}") for r in range(4)]
        xT_full, xT_hi, xT_lo = sem("xT_full"), sem("xT_hi"), sem("xT_lo")
        up_full, gate_full = sem("up_full"), sem("gate_full")
        act_ready, gu_ready = sem("act_ready"), sem("gu_ready")
        guT_full, guT_ready = sem("guT_full"), sem("guT_ready")
        down_full, yo_ready = sem("down_full"), sem("yo_ready")
        x2_stored, added, sent = sem("x2_stored"), sem("added"), sem("sent")
        dcol_ready, hot_g_ready = sem("dcol_ready"), sem("hot_g_ready")
        gates_full, gates_ready = sem("gates_full"), sem("gates_ready")
        block = ctx.enter_context(nc.Block())

        MISC = (0, 1)
        SB = (2, 3)
        PB = (4, 5)
        OB = (6, 7)
        HB = 2 * HG
        GROUPS = H // HG
        BEFORE_TURNS = 3 * TB + 2 * GROUPS
        FIRST_UNITS, TURN_UNITS = 2 * TB + 2 * GROUPS, 4 * TB + 2 * GROUPS
        UNITS_END = BEFORE_TURNS + FIRST_UNITS + (B - 3) * TURN_UNITS + (TURN_UNITS - TB) + 2 * TB

        def units_before(b, wo, proj):
            if not wo:
                return BEFORE_TURNS
            return BEFORE_TURNS + FIRST_UNITS + (b - 1) * TURN_UNITS - (0 if proj else TB)

        def positions(wo, proj, hT):
            pos, n = {}, 0
            units = [(f"qk{g}", step, proj) for step, g in QK_IN.items()] + [("x1T", X1T_IN, wo)]
            for name, _, there in ([("v", -1, proj), ("wo", 0, wo)] + sorted(units, key=lambda u: u[1])
                                   + [("hT", HT_IN, hT)]):
                if there:
                    pos[name] = n
                    n += 2
            return pos

        QK_IN = {1: 0, 3: 1, 5: 2, 6: 3}
        LN2_IN, LN2_OUT_IN = 1, 2
        X1T_IN = 4
        LN1_OUT_IN, HT_IN = 5, 7
        OT_HI_IN, OT_LO_IN = 6, 7

        AFTER_X1T = min(g for step, g in QK_IN.items() if step > X1T_IN)

        def run_turns(engine, turn):
            turn(0, 0, wo=False)
            with engine.Fori(0, (B - 4) // 2) as i:
                turn(2 * i + 1, 1)
                turn(2 * i + 2, 0)
            turn(B - 3, 1)
            turn(B - 2, 0, hT=False)
            turn(B - 1, 1, proj=False, hT=False)

        def pt_on_act(h):
            return h % 2 == 1

        def pt_count(b, h, act_engine):
            return H // 2 * b + ((h + 1) // 2 if act_engine else h // 2 + 1)

        def windows(a, dims, start=0):
            return bass.AP(tensor=a.tensor, offset=a.offset + start, ap=[list(a.ap[0])] + dims)

        def mixer_rows(h):
            q = QX[:, :, :].rearrange("p c (b h i) -> p (c b) h i", b=B, h=MH)
            return q[:, :, bass.ds(h, 1), :].squeeze(2)

        def convolved(r):
            return ps[:, 4 * (r % 2):4 * (r % 2) + 4, :].rearrange("p c (b k) -> p (c b) k", b=B)

        @block.sync
        def _(sp):
            sp.dma_start(X[:, 0:TB, :], x_t[:, 0:TB, :]).then_inc(x_in0, 16)
            for m in range(4):
                if m == O_:
                    sp.dma_start(X[:, TB:2 * TB, :], x_t[:, TB:2 * TB, :]).then_inc(x_in1, 16)
                sp.dma_start(wraw[:, m, :, :], w_attn[m]).then_inc(w_in[m], 16)
                if m == 0:
                    sp.dma_start(bqkv_c[:, :, :], b_qkv).then_inc(small_in, 16)
                    sp.dma_start(bo_b[:, :], b_o.partition_broadcast(P)).then_inc(small_in, 16)
                    sp.dma_start(d_b[:, :], skip_d.partition_broadcast(P)).then_inc(small_in, 16)
                    sp.dma_start(wr[:, :, :], w_router).then_inc(small_in, 16)
            sp.dma_start(X[:, 2 * TB:TILES, :], x_t[:, 2 * TB:TILES, :]).then_inc(x_in, 16)

            sp.wait_ge(q_ready, GROUPS * B)
            sp.wait_ge(k_ready, GROUPS * B)
            sp.dma_start(cx[:, :, :, :], ctx_rev).then_inc(cx_in, 16)

            def load_strip(h, r, first=False):
                if not first:
                    sp.wait_ge(y_full, h - NS + 1)
                src = kern_pad[bass.ds(h, 1), :]
                src = bass.AP(tensor=src.tensor, offset=src.offset, ap=[[1, P], [1, E]])
                sp.dma_start(strip[:, r, :], src).then_inc(strip_in[r], 16)

            sp.wait_ge(x1_ready, TB * B)
            for h in range(NS):
                load_strip(h, h, first=True)
            def load_raw(e, m):
                if not (isinstance(e, int) and e == 0):
                    sp.wait_ge(xsplit_stored[m], 32 * e)
                sp.dma_start(xraw[:, m, :].unsqueeze(1), (w_up, w_gate)[m][:, bass.ds(e, 1), :, :]
                             .rearrange("p e c f -> p e (c f)")).then_inc(xraw_in[m], 16)

            def store_split(e, m):
                sp.wait_ge(xlo_ready[m], e + 1)
                for i, part in enumerate((xhi, xlo)):
                    sp.dma_start(split_d[:, bass.ds(e, 1), m, i, :], part[:, m, :].bitcast(F32).unsqueeze(1))\
                        .then_inc(xsplit_stored[m], 16)

            sp.wait_ge(qx_ready, TILES)
            for m in range(2):
                load_raw(0, m)
            with sp.Fori(1, MH // NS) as i:
                for r in range(NS):
                    load_strip(NS * i + r, r)
                    (store_split, load_raw)[r % 2](i - (r + 1) % 2, r // 2)
            for m in range(2):
                store_split(NX - 1, m)

            def load_piece(e, n):
                if n < 4:
                    sp.dma_start(whl[:, e % NW, n // 2, n % 2, :].bitcast(F32),
                                 split_d[:, e, n // 2, n % 2, :]).then_inc(w_loaded, 16)
                else:
                    sp.dma_start(wd[:, e % NW, :, :], w_down[:, e, :, :]).then_inc(w_loaded, 16)

            def load_expert(e):
                sp.wait_ge(w_loaded, 16 * PIECES * e)
                for n in range(PIECES):
                    load_piece(e, n)

            for m in range(2):
                sp.wait_ge(xsplit_stored[m], 32 * NX)
            sp.wait_ge(mixed, MH)
            for t in range(TILES):
                sp.wait_ge(ln3["out"], t + 1)
                sp.dma_start(h3_t[:, t, :], h3[:, t % NH, :]).then_inc(h3_stored[t % NH], 16)
                sp.dma_start(sum_t[:, t, :], X[:, t, :]).then_inc(x2_stored, 16)
                if t % 3 == 2:
                    load_piece(0, t // 3)
            for e in range(1, NW):
                load_expert(e)
            sp.wait_ge(idx_ready, 1)
            for e in range(NW, NX):
                before = sp.value_load(cum_i[0:1, e - NW:e - NW + 1], min_val=0, max_val=SLOT_TILES)
                sp.wait_ge(yo_ready, before + 1)
                load_expert(e)
            sp.wait_ge(added, 16 * SLOT_TILES)
            COPIES = 4
            for n in range(COPIES):
                rows = slice(B * S // COPIES * n, B * S // COPIES * (n + 1))
                sp.dma_start(out_rows[rows, :], sum_d[rows, :]).then_inc(sent, 16)
            sp.wait_ge(sent, 16 * COPIES)

        @block.gpsimd
        def _(pool):
            pool.memset(ident[:, :], 0.0).then_inc(consts, 1)
            pool.memset(mhalf[:, :], -0.5).then_inc(consts, 1)
            pool.iota(dist_i[:, :], pattern=[[1, S]], base=-P, channel_multiplier=-1).then_inc(consts, 1)
            pool.wait_ge(consts, 3)
            pool.affine_select(out=ident[:, :], in_=ident[:, :], compare_op=ALU.not_equal, fill=1.0,
                               base=0, pattern=[[-1, P]], channel_multiplier=1).then_inc(consts, 1)
            pool.tensor_copy(dist[:, :], dist_i[:, :]).then_inc(consts, 1)

            def carry():
                carried[1] = (carried[1] + 1) % 16
                pool.tensor_tensor(carrier[:, 48 + carried[1]:49 + carried[1]], mhalf[:, 0:1], mhalf[:, 0:1], ALU.add)

            def rstd(ln, var, dst, n):
                pool.wait_ge(ln["var"], n + 1)
                pool.tensor_tensor(dst[:, :], var[:, :], mhalf[:, :], ALU.pow).then_inc(ln["rstd"], 1)

            def add_bo(b):
                pool.wait_ge(ln1["out"], TB * b + TB)
                xs = X[:, bass.ds(TB * b, TB), :]
                pool.tensor_tensor(xs, xs, bo_b[:, :].unsqueeze(1).to_broadcast([P, TB, E]),
                                   ALU.add).then_inc(xb_ready, 1)

            rstd(ln1, ve1, rs1, 0)
            pool.iota(tok_i[:, :], pattern=[[P, TILES]], base=1, channel_multiplier=1).then_inc(tables, 1)
            pool.iota(iota_ji[:, :], pattern=[[1, SLOT_COLS]], base=0, channel_multiplier=0)\
                .then_inc(tables, 1)
            pool.iota(iota128[:, :], pattern=[[1, P]], base=0, channel_multiplier=0,
                      allow_small_or_imprecise_dtypes=True).then_inc(tables, 1)
            pool.memset(le8[:, :, :], 1.0).then_inc(tables, 1)
            pool.wait_ge(tables, 4)
            pool.tensor_copy(tok[:, :], tok_i[:, :]).then_inc(tables, 1)
            pool.tensor_copy(iota_j[:, :], iota_ji[:, :]).then_inc(tables, 1)
            pool.tensor_copy(iota8[:, :], iota_ji[:, 0:NX]).then_inc(tables, 1)
            pool.affine_select(out=le8[:, :, :], in_=le8[:, :, :], compare_op=ALU.is_ge, fill=0.0,
                               base=0, pattern=[[1, NX], [-1, NX]], channel_multiplier=0)\
                .then_inc(tables, 1)
            pool.wait_ge(tab_scaled, H)
            pool.affine_select(out=bias_tab[:, :, :], in_=bias_tab[:, :, :], compare_op=ALU.is_ge,
                               fill=MASKED, base=P, pattern=[[0, H], [-1, S]],
                               channel_multiplier=1).then_inc(tab_ready, 1)
            pool.wait_ge(small_in, 16 * 4)
            add_bo(0)

            def turn(b, par, wo=True, proj=True, hT=True):
                if hT:
                    rstd(ln1, ve1, rs1, b + 2)
                if wo:
                    rstd(ln2, ve2, rs2, b - 1)
                if hT:
                    add_bo(b + 2)

            rstd(ln1, ve1, rs1, 1)
            add_bo(1)
            run_turns(pool, turn)
            rstd(ln2, ve2, rs2, B - 1)


            pool.wait_ge(x1_ready, TB * B)
            pool.wait_ge(av_done, GROUPS * B)
            pool.memset(anti[:, :], 0.0).then_inc(consts, 1)
            pool.wait_ge(consts, 6)
            pool.affine_select(out=anti[:, :], in_=anti[:, :], compare_op=ALU.not_equal, fill=1.0,
                               base=-(P - 1), pattern=[[1, P]], channel_multiplier=1).then_inc(consts, 1)
            pool.wait_ge(cx_in, 16)

            def products(h, r, free):
                if free:
                    pool.wait_ge(y_full, h - KV + 1)
                c = cx[:, :, bass.ds(h, 1), :].squeeze(2)
                pool.tensor_tensor(kv[:, r, :, :].rearrange("p n (d i) -> p n d i", d=DIAGS),
                                   c[:, :, 0:MD].unsqueeze(2).to_broadcast([P, EC * B, DIAGS, MD]),
                                   windows(c, [[MW * MH, EC * B], [1, DIAGS], [1, MD]]),
                                   ALU.mult).then_inc(kv_ready, 1)

            def low_parts(e, m):
                pool.wait_ge(xhi_ready[m], e + 1)
                pool.tensor_tensor(xlo[:, m, :], xraw[:, m, :], xhi[:, m, :].bitcast(F32),
                                   ALU.subtract).then_inc(xlo_ready[m], 1)

            for h in range(KV):
                if h == KV - 1:
                    pool.wait_ge(qx_ready, TILES)
                products(h, h, False)
            with pool.Fori(1, MH // KV) as i:
                for r in range(KV):
                    products(KV * i + r, r, True)
                    if r % 2 == 0:
                        low_parts(i - 1, r // 2)
            for m in range(2):
                low_parts(NX - 1, m)

            for t in range(TILES):
                c = t % 2
                pool.wait_ge(ln3["var"], t + 1)
                pool.tensor_tensor(rs3[:, c:c + 1], ve3[:, c:c + 1], mhalf[:, 0:1], ALU.pow)\
                    .then_inc(ln3["rstd"], 1)
            pool.wait_ge(x2T_full, TILES)
            pool.memset(ones[:, :].bitcast(F32), 1.0).then_inc(tables, 1)
            pool.memset(upper_f[:, :], 1.0).then_inc(tables, 1)
            pool.memset(padded[:, 0:TILES, :].bitcast(F32), 0.0).then_inc(tables, 1)
            pool.wait_ge(tables, 11)
            pool.affine_select(out=upper_f[:, :], in_=upper_f[:, :], compare_op=ALU.is_gt, fill=0.0,
                               base=0, pattern=[[1, P]], channel_multiplier=-1).then_inc(tables, 1)
            pool.wait_ge(tables, 12)
            pool.tensor_copy(upper[:, :], upper_f[:, :]).then_inc(tables, 1)

            pool.wait_ge(idx_ready, 1)
            for r in range(NH):
                pool.wait_ge(h3_stored[r], 16 * (TILES // NH))

            pool.wait_ge(x2_stored, 16 * TILES)
            LAG = 6

            def gather(j, r, free):
                if free:
                    pool.wait_ge(xT_full, j - 3)
                pool.tensor_copy(gcol[:, r:r + 1], idx[:, bass.ds(j, 1)]).then_inc(gcol_ready, 1)
                pool.wait_ge(gcol_ready, j + 1)
                carry()
                pool.indirect_dma_start(
                    out=xg[:, r, :], out_offset=None, in_=h3_d[:, :],
                    in_offset=bass.IndirectOffsetOnAxis(ap=gcol[:, r:r + 1], axis=0),
                ).then_inc(gathered[r], 16)

            def scatter(j, r):
                pool.tensor_copy(dcol[:, r:r + 1], dest[:, bass.ds(j, 1)]).then_inc(dcol_ready, 1)
                pool.wait_ge(dcol_ready, j + 1)
                pool.wait_ge(yo_ready, j + 2)
                if not (isinstance(j, int) and j == 0):
                    pool.wait_ge(added, 16 * j)
                carry()
                pool.indirect_dma_start(
                    out=sum_d[:, :], out_offset=bass.IndirectOffsetOnAxis(ap=dcol[:, r:r + 1], axis=0),
                    in_=yo[:, r, :], in_offset=None, compute_op=ALU.add,
                ).then_inc(added, 16)

            for r in range(4):
                gather(r, r, False)
            for j in range(4, LAG + 4):
                gather(j, j % 4, True)
                if j >= LAG:
                    scatter(j - LAG, (j - LAG) % 4)
            with pool.Fori(0, (SLOT_TILES - LAG - 4) // 4) as i:
                for r in range(4):
                    gather(4 * i + r + LAG + 4, (r + LAG) % 4, True)
                    scatter(4 * i + r + 4, r)
            for j in range((SLOT_TILES - LAG) // 4 * 4, SLOT_TILES):
                if j + LAG < SLOT_TILES:
                    gather(j + LAG, (j + LAG) % 4, True)
                scatter(j, j % 4)

        @block.scalar
        def _(act_e):
            def emptied(n, i, dst, signal, **kw):
                act_e.wait_ge(misc_full, n + 1)
                src = ps[:, MISC[i], :]
                if len(dst.shape) == 3:
                    src = src.rearrange("p (c q) -> p c q", c=EC)
                act_e.activation(dst, src, ACT.Copy).then_inc(signal, 1)

            def hT_hi(n):
                for t in range(TB):
                    emptied(n + t, t, hTh[:, :, P * t:P * t + P], ht_hi)

            def v_out(n, par):
                for t in range(TB):
                    emptied(n + t, t, v[par][:, t, :], v_ready)

            def x1T_out(b, n):
                for t in range(TB):
                    emptied(n + t, t, QX[:, :, bass.ds(S * b + P * t, P)], qx_ready)

            def k_out(n, g, par):
                act_e.wait_ge(misc_full, n + 2)
                act_e.activation(kT[par][:, g, :], ps[:, MISC[1], 0:S], ACT.Identity,
                                 bias=bqkv_c[:, 1, g:g + 1]).then_inc(k_ready, 1)

            def oT_hi(b, k, par):
                act_e.wait_ge(av_done, GROUPS * b + 2 * k + 2)
                for g in (2 * k, 2 * k + 1):
                    act_e.activation(oTh[par][:, g, :], ps[:, OB[k], S * (g % 2):S * (g % 2) + S],
                                     ACT.Identity, bias=bqkv_c[:, 2, g:g + 1]).then_inc(ot_hi, 1)

            def move_pT(b, h):
                act_e.wait_ge(pt_full, H * b + h + 1)
                act_e.activation(pT[:, h % NE, :], ps[:, PB[h % 2], 0:3 * P],
                                 ACT.Copy).then_inc(pt_act, 1)

            def exps(b, g):
                act_e.wait_ge(nm_ready, H // 2 * b + g + 1)
                for h in (2 * g, 2 * g + 1):
                    for t in range(TB):
                        s_t = sc[:, h % NE, P * t:P + 2 * P * t]
                        ins = act_e.activation(s_t, s_t, ACT.Exp, bias=nm[:, h, t:t + 1],
                                               accum_out=sums[:, h, t:t + 1])
                    ins.then_inc(p_ready, 1)

            def weights_hi(m):
                act_e.wait_ge(w_in[m], 16)
                act_e.activation(whi[:, HI_AT[m], :, :], wraw[:, m, :, :], ACT.Copy).then_inc(wsplit_hi, 1)

            weights_hi(V_)
            hT_hi(0)
            weights_hi(Q_)
            weights_hi(K_)
            v_out(TB, 0)
            act_e.wait_ge(small_in, 16 * 4)
            for g in range(GROUPS):
                if g == GROUPS - 2:
                    weights_hi(O_)
                k_out(2 * TB + 2 * g, g, 0)
            hT_hi(2 * TB + 2 * GROUPS)

            def turn(b, par, wo=True, proj=True, hT=True):
                u = units_before(b, wo, proj)
                pos = positions(wo, proj, hT)
                for g in range(-1, H // 2):
                    if g + 1 < H // 2:
                        exps(b, g + 1)
                    for h in (2 * g, 2 * g + 1):
                        if g >= 0 and pt_on_act(h):
                            move_pT(b, h)
                    if g == -1 and proj:
                        v_out(u + pos["v"], 1 - par)
                    if g in QK_IN and proj:
                        k_out(u + pos[f"qk{QK_IN[g]}"], QK_IN[g], 1 - par)
                    if g == X1T_IN and wo:
                        x1T_out(b - 1, u + pos["x1T"])
                    if g == OT_HI_IN:
                        oT_hi(b, 0, par)
                    if g == HT_IN and hT:
                        hT_hi(u + pos["hT"])
                oT_hi(b, 1, par)

            run_turns(act_e, turn)
            x1T_out(B - 1, UNITS_END + TB)

            def widen(h, r, free):
                if free:
                    act_e.wait_ge(y_read, h - 1)
                q = mixer_rows(h)
                act_e.activation(qe[:, r % 2, :, 0:MD], q, ACT.Copy)
                act_e.activation(qe[:, r % 2, :, MD:MW], q[:, :, 0:MW - MD], ACT.Copy)\
                    .then_inc(qe_ready, 1)

            act_e.wait_ge(qx_ready, TILES)
            def high_parts(e, m):
                act_e.wait_ge(xraw_in[m], 16 * e + 16)
                act_e.activation(xhi[:, m, :], xraw[:, m, :], ACT.Copy).then_inc(xhi_ready[m], 1)

            def widen_4(i, first=False):
                for r in range(4):
                    widen(4 * i + r, r, not (first and r < 2))
                    if r >= 2:
                        high_parts(i, r - 2)

            widen_4(0, first=True)
            with act_e.Fori(1, NX) as i:
                widen_4(i)

            def lgT_out(q):
                act_e.wait_ge(lgT_full, 4 * q + 4)
                if q >= 2:
                    act_e.wait_ge(logits_full, 4 * q - 4)
                act_e.activation(lgT[:, q % 2, :], ps[0:NX, 5 + q % 2, :], ACT.Copy).then_inc(lgT_ready, 1)

            for t in range(TILES):
                act_e.wait_ge(h3T_full, t + 1)
                if t >= 2:
                    act_e.wait_ge(lgT_full, t - 1)
                act_e.activation(h3T[:, t % 2, :, :], ps[:, 2 + t % 2, :].rearrange("p (c q) -> p c q", c=EC),
                                 ACT.Copy).then_inc(h3T_ready, 1)
                if t % 4 == 0 and t >= 4:
                    lgT_out(t // 4 - 1)
            lgT_out(TILES // 4 - 1)
            act_e.wait_ge(shifted, 1)
            act_e.activation(topx[:, :, :], topx[:, :, :], ACT.Exp).then_inc(numer, 1)

            def rows_T(j, r, free):
                act_e.wait_ge(xT_full, j + 1)
                if free:
                    act_e.wait_ge(gate_full, j - 1)
                act_e.activation(xgTh[:, r % 2, :, :], ps[:, 0, :].rearrange("p (c q) -> p c q", c=EC),
                                 ACT.Copy).then_inc(xT_hi, 1)

            def silu(j, r, free):
                act_e.wait_ge(up_full, j + 1)
                if free:
                    act_e.wait_ge(gu_ready, j - 1)
                act_e.activation(act[:, r % 2, :], ps[:, 1, 0:F], ACT.Silu).then_inc(act_ready, 1)

            def rows_out(j, r, free):
                act_e.wait_ge(down_full, j + 1)
                if free:
                    act_e.wait_ge(added, 16 * (j - 3))
                act_e.activation(yo[:, r, :], ps[:, 4 + r % 2, :], ACT.Copy,
                                 scale=gslot[:, bass.ds(j, 1)]).then_inc(yo_ready, 1)

            rows_T(0, 0, False)
            for j in range(4):
                silu(j, j, j >= 2)
                rows_T(j + 1, (j + 1) % 4, j + 1 >= 2)
                if j == 1:
                    act_e.wait_ge(gates_ready, 1)
                if j >= 1:
                    rows_out(j - 1, j - 1, False)
            with act_e.Fori(1, ROUNDS) as i:
                for r in range(4):
                    silu(4 * i + r, r, True)
                    rows_T(4 * i + r + 1, (r + 1) % 4, True)
                    rows_out(4 * i + r - 1, (r - 1) % 4, True)
            for j in range(4 * ROUNDS, SLOT_TILES):
                silu(j, j % 4, True)
                if j + 1 < SLOT_TILES:
                    rows_T(j + 1, (j + 1) % 4, True)
                rows_out(j - 1, (j - 1) % 4, True)
            rows_out(SLOT_TILES - 1, (SLOT_TILES - 1) % 4, True)

        @block.vector
        def _(dve):
            def carry():
                carried[0] = (carried[0] + 1) % 48
                dve.memset(carrier[:, carried[0]:carried[0] + 1], 0.0)

            def layer_stats(ln, src, st, mv, ve, n):
                for t in range(TB):
                    dve.bn_stats(st[:, t, :], src(t)).then_inc(ln["stats"], 1)
                dve.wait_ge(ln["stats"], TB * n + TB)
                carry()
                for t in range(TB):
                    dve.bn_aggr(mv[:, t, :], st[:, t, :]).then_inc(ln["aggr"], 1)
                dve.wait_ge(ln["aggr"], TB * n + TB)
                dve.tensor_scalar(ve[:, :], mv[:, :, 1], EPS, None, ALU.add).then_inc(ln["var"], 1)

            def layer_out(ln, src, dst, mv, rs, n):
                dve.wait_ge(ln["rstd"], n + 1)
                for t in range(TB):
                    dve.tensor_scalar(dst[:, t, :], src(t), mv[:, t, 0:1], rs[:, t:t + 1],
                                      ALU.subtract, ALU.mult).then_inc(ln["out"], 1)

            def x_tile(b):
                return lambda t: X[:, bass.ds(TB * b + t, 1), :].squeeze(1)

            def hT_lo(b):
                for t in range(TB):
                    dve.wait_ge(ht_hi, TB * b + t + 1)
                    cols = slice(P * t, P * t + P)
                    dve.tensor_tensor(hTl[:, :, cols], ps[:, MISC[t], :].rearrange("p (c q) -> p c q", c=EC),
                                      hTh[:, :, cols].bitcast(F32), ALU.subtract).then_inc(ht_lo, 1)

            def q_out(n, g, par):
                dve.wait_ge(misc_full, n + 1)
                dve.tensor_scalar(qT[par][:, g, :], ps[:, MISC[0], 0:S], bqkv_c[:, 0, g:g + 1],
                                  HD ** -0.5, ALU.add, ALU.mult).then_inc(q_ready, 1)

            def scores(b, g):
                for h in (2 * g, 2 * g + 1):
                    dve.wait_ge(s_full, H * b + h + 1)
                    carry()
                    bank_h = SB[h % 2]
                    dve.tensor_tensor_reduce(sc[:, h % NE, 0:P], ps[:, bank_h, 0:P],
                                             bias_tab[:, h, P:2 * P], 1.0, MASKED, ALU.add, ALU.max,
                                             mx[:, h, 0:1])
                    dve.tensor_tensor_reduce(sc[:, h % NE, P:3 * P], ps[:, bank_h, P:3 * P],
                                             bias_tab[:, h, :], 1.0, MASKED, ALU.add, ALU.max,
                                             mx[:, h, 1:2]).then_inc(s_read, 1)
                dve.wait_ge(s_read, H * b + 2 * g + 2)
                dve.tensor_scalar(nm[:, 2 * g:2 * g + 2, :], mx[:, 2 * g:2 * g + 2, :], -1.0, None,
                                  ALU.mult).then_inc(nm_ready, 1)

            def divide(b, g):
                dve.wait_ge(p_ready, H * b + 2 * g + 2)
                dve.reciprocal(rsum[:, 2 * g:2 * g + 2, :], sums[:, 2 * g:2 * g + 2, :])\
                    .then_inc(rsum_ready, 1)
                dve.wait_ge(rsum_ready, H // 2 * b + g + 1)
                for h in (2 * g, 2 * g + 1):
                    for t in range(TB):
                        p_t = sc[:, h % NE, P * t:P + 2 * P * t]
                        ins = dve.tensor_scalar(p_t, p_t, rsum[:, h, t:t + 1], None, ALU.mult)
                    ins.then_inc(pn_ready, 1)

            def move_pT(b, h):
                dve.wait_ge(pt_full, H * b + h + 1)
                dve.tensor_copy(pT[:, h % NE, :], ps[:, PB[h % 2], 0:3 * P]).then_inc(pt_dve, 1)

            def oT_lo(b, k, par):
                dve.wait_ge(ot_hi, GROUPS * b + 2 * k + 2)
                for g in (2 * k, 2 * k + 1):
                    dve.scalar_tensor_tensor(out=oTl[par][:, g, :],
                                             in0=ps[:, OB[k], S * (g % 2):S * (g % 2) + S],
                                             scalar=bqkv_c[:, 2, g:g + 1],
                                             in1=oTh[par][:, g, :].bitcast(F32),
                                             op0=ALU.add, op1=ALU.subtract).then_inc(ot_lo, 1)

            def add_attention(b, t, n):
                dve.wait_ge(xb_ready, b + 1)
                dve.wait_ge(misc_full, n + 1)
                xs = X[:, bass.ds(TB * b + t, 1), :].squeeze(1)
                dve.tensor_tensor(xs, ps[:, MISC[t], :], xs, ALU.add).then_inc(x1_ready, 1)

            dve.wait_ge(x_in0, 16)
            layer_stats(ln1, x_tile(0), st1, mv1, ve1, 0)
            dve.wait_ge(consts, 5)
            for h in range(H):
                dve.tensor_scalar(bias_tab[:, h, :], dist[:, :], 2.0 ** (-8.0 * (h + 1) / H), None,
                                  ALU.mult).then_inc(tab_scaled, 1)
            layer_out(ln1, x_tile(0), hn, mv1, rs1, 0)
            def weights_lo(m):
                dve.wait_ge(wsplit_hi, m + 1)
                dve.tensor_tensor(wlo[:, m, :, :], wraw[:, m, :, :], whi[:, HI_AT[m], :, :].bitcast(F32),
                                  ALU.subtract).then_inc(wsplit_lo, 1)

            weights_lo(V_)
            hT_lo(0)
            weights_lo(Q_)
            weights_lo(K_)
            dve.wait_ge(small_in, 16 * 4)
            q_out(2 * TB, 0, 0)
            dve.wait_ge(x_in1, 16)
            layer_stats(ln1, x_tile(1), st1, mv1, ve1, 1)
            q_out(2 * TB + 2, 1, 0)
            layer_out(ln1, x_tile(1), hn, mv1, rs1, 1)
            q_out(2 * TB + 4, 2, 0)
            weights_lo(O_)
            q_out(2 * TB + 6, 3, 0)
            hT_lo(1)
            dve.wait_ge(tab_ready, 1)
            dve.wait_ge(x_in, 16)

            def turn(b, par, wo=True, proj=True, hT=True):
                u = units_before(b, wo, proj)
                pos = positions(wo, proj, hT)
                for g in range(-2, H // 2):
                    if g + 2 < H // 2:
                        scores(b, g + 2)
                    if 0 <= g + 1 < H // 2:
                        divide(b, g + 1)
                    for h in (2 * g, 2 * g + 1):
                        if g >= 0 and not pt_on_act(h):
                            move_pT(b, h)
                    if g == -1 and hT:
                        layer_stats(ln1, x_tile(b + 2), st1, mv1, ve1, b + 2)
                    if wo:
                        if g in (0, 1):
                            add_attention(b - 1, g, u + pos["wo"] + g)
                        if g == LN2_IN:
                            dve.wait_ge(x1_ready, TB * b)
                            carry()
                            layer_stats(ln2, x_tile(b - 1), st2, mv2, ve2, b - 1)
                        if g == LN2_OUT_IN:
                            layer_out(ln2, x_tile(b - 1), hn, mv2, rs2, b - 1)
                    if g in QK_IN and proj:
                        q_out(u + pos[f"qk{QK_IN[g]}"], QK_IN[g], 1 - par)
                    if g == LN1_OUT_IN and hT:
                        if wo:
                            dve.wait_ge(misc_full, u + pos["x1T"] + TB)
                        layer_out(ln1, x_tile(b + 2), hn, mv1, rs1, b + 2)
                    if g == OT_LO_IN:
                        oT_lo(b, 0, par)
                    if g == HT_IN and hT:
                        hT_lo(b + 2)
                oT_lo(b, 1, par)

            run_turns(dve, turn)
            for t in range(TB):
                add_attention(B - 1, t, UNITS_END + t)
            dve.wait_ge(x1_ready, TB * B)
            layer_stats(ln2, x_tile(B - 1), st2, mv2, ve2, B - 1)
            layer_out(ln2, x_tile(B - 1), hn, mv2, rs2, B - 1)

            def prepare(h, r):
                dve.wait_ge(strip_in[r], 16 if isinstance(h, int) and h < NS else 4 * (h - r) + 16)
                dve.scalar_tensor_tensor(out=strip[:, r, 0:P], in0=anti[:, :],
                                         scalar=d_b[:, bass.ds(h, 1)], in1=strip[:, r, 0:P],
                                         op0=ALU.mult, op1=ALU.add).then_inc(strip_fixed, 1)

            def contract(h, r):
                y = convolved(r)
                q = qe[:, r % 2, :, :]
                z = terms[:, :, :]
                dims = [[MW, EC * B]]

                def grid(a, start, pitch, rows, width):
                    return a[:, :, start:start + rows * pitch]\
                        .rearrange("p n (d i) -> p n d i", i=pitch)[:, :, :, 0:width]

                dve.wait_ge(qe_ready, h + 1)
                dve.wait_ge(y_full, h + 1)
                dve.tensor_tensor(grid(z, DIAGS * SKEW, SKEW, MIRROR, MIRROR),
                                  grid(y, 2 * MD - 1, MD - 1, MIRROR, MIRROR),
                                  windows(q, dims + [[-1, MIRROR], [1, MIRROR]], MD - 1), ALU.mult)\
                    .then_inc(wrapped, 1)
                dve.tensor_tensor(grid(z, 0, SKEW, DIAGS, MD), grid(y, 0, MD, DIAGS, MD),
                                  windows(q, dims + [[1, DIAGS], [1, MD]]), ALU.mult)
                dve.wait_ge(wrapped, h + 1)
                dve.tensor_tensor(grid(z, DIAGS * SKEW + 1, SKEW + 1, MIRROR, MD),
                                  grid(y, MD, MD, MIRROR, MD),
                                  windows(q, dims + [[0, MIRROR], [1, MD]]), ALU.mult).then_inc(y_read, 1)
                dve.wait_ge(y_read, h + 1)
                carry()
                dve.tensor_reduce(mixer_rows(h),
                                  terms[:, :, 0:MD * SKEW].rearrange("p n (r j) -> p n j r", r=MD)[:, :, 0:MD, :],
                                  AX.X, ALU.add).then_inc(mixed, 1)
                dve.wait_ge(mixed, h + 1)

            dve.wait_ge(consts, 7)
            dve.wait_ge(qx_ready, TILES)
            LEAD = 2
            for h in range(LEAD):
                prepare(h, h)
            with dve.Fori(0, MH // NS - 1) as i:
                for r in range(NS):
                    prepare(NS * i + r + LEAD, (r + LEAD) % NS)
                    contract(NS * i + r, r)
            for h in range(MH - NS, MH):
                if h + LEAD < MH:
                    prepare(h + LEAD, (h + LEAD) % NS)
                contract(h, h % NS)

            def normalise(t):
                if t == 0:
                    for m in range(2):
                        dve.wait_ge(xsplit_stored[m], 32 * NX)
                dve.wait_ge(ln3["rstd"], t + 1)
                if t >= NH:
                    dve.wait_ge(h3T_full, t - NH + 1)
                    dve.wait_ge(h3_stored[t % NH], 16 * (t // NH))
                dve.tensor_scalar(h3[:, t % NH, :], X[:, t, :], mv3[:, t % 2, 0:1],
                                  rs3[:, t % 2:t % 2 + 1], ALU.subtract, ALU.mult)\
                    .then_inc(ln3["out"], 1)

            for t in range(TILES):
                dve.wait_ge(x2T_full, t + 1)
                dve.tensor_tensor(X[:, t, :], ps[:, t % 2, :], X[:, t, :], ALU.add).then_inc(x2_ready, 1)
                if t >= 1:
                    normalise(t - 1)
                dve.wait_ge(x2_ready, t + 1)
                dve.bn_stats(st3[:, t % 2, :], X[:, t, :]).then_inc(ln3["stats"], 1)
                dve.wait_ge(ln3["stats"], t + 1)
                dve.bn_aggr(mv3[:, t % 2, :], st3[:, t % 2, :]).then_inc(ln3["aggr"], 1)
                dve.wait_ge(ln3["aggr"], t + 1)
                dve.tensor_scalar(ve3[:, t % 2:t % 2 + 1], mv3[:, t % 2, 1:2], EPS, None, ALU.add)\
                    .then_inc(ln3["var"], 1)
            normalise(TILES - 1)

            steps = 0

            def step(ins):
                nonlocal steps
                steps += 1
                ins.then_inc(route, 1)
                dve.wait_ge(route, steps)

            dve.wait_ge(logits_full, TILES)
            step(dve.tensor_copy(logits[:, :, :], ps[:, 4, 0:TILES * NX].rearrange("p (t e) -> p t e", e=NX)))
            for t in range(TILES):
                ins = dve.max(top[:, t, :], logits[:, t, :])
            step(ins)
            for t in range(TILES):
                ins = dve.max_index(topi[:, t, :], top[:, t, :], logits[:, t, :])
            step(ins)
            dve.tensor_tensor(topx[:, :, :], top[:, :, :], top[:, :, 0:1].to_broadcast([P, TILES, 8]),
                              ALU.subtract).then_inc(shifted, 1)
            step(dve.tensor_copy(idxf[:, :, :], topi[:, :, 0:TOPK].rearrange("p t k -> p k t")))
            for k in range(TOPK):
                ins = dve.tensor_tensor(hot[:, k, :, :], iota8[:, :].unsqueeze(1).to_broadcast([P, TILES, NX]),
                                        idxf[:, k, :].unsqueeze(2).to_broadcast([P, TILES, NX]),
                                        ALU.is_equal)
            step(ins)
            step(dve.tensor_tensor(picked, hot[:, 0, :, :], hot[:, 1, :, :], ALU.add))
            dve.tensor_reduce(cnt[:, :], picked.bitcast(F32).rearrange("p t e -> p e t"), AX.X, ALU.add)\
                .then_inc(picked_ready, 1)
            dve.wait_ge(numer, 1)
            step(dve.tensor_reduce(zsum[:, :], topx[:, :, :], AX.X, ALU.add))
            step(dve.reciprocal(zrec[:, :], zsum[:, :]))
            step(dve.tensor_tensor(gate[:, :, :], topx[:, :, 0:TOPK],
                                   zrec[:, :].unsqueeze(2).to_broadcast([P, TILES, TOPK]), ALU.mult))
            step(dve.tensor_reduce(psum2[:, :], gate[:, :, :], AX.X, ALU.add))
            step(dve.reciprocal(prec2[:, :], psum2[:, :]))
            step(dve.tensor_tensor(gate[:, :, :], gate[:, :, :],
                                   prec2[:, :].unsqueeze(2).to_broadcast([P, TILES, TOPK]), ALU.mult))
            dve.tensor_scalar(dummy[:, :], tok[:, 0:1], float(B * S), None, ALU.add)
            dve.tensor_copy(gsplit[:, 0, :, :], gate[:, :, :].rearrange("p t k -> p k t"))
            dve.tensor_scalar(iota16[:, :], iota_j[:, 0:TILES], float(P), None, ALU.mult)
            dve.wait_ge(ranks_full, 1)
            dve.tensor_copy(ranks[:, :, :], ps[:, 5, 0:TILES * NX].rearrange("p (t e) -> p t e", e=NX))
            step(dve.tensor_copy(count[:, :], ps[:, 6, 0:NX]))
            c3 = cmp[:, 0:NX * TILES].rearrange("p (e k) -> p e k", e=NX)
            step(dve.tensor_tensor(c3, count[:, :].unsqueeze(2).to_broadcast([P, NX, TILES]),
                                   iota16[:, :].unsqueeze(1).to_broadcast([P, NX, TILES]), ALU.is_gt))
            step(dve.tensor_reduce(ntile[:, :], c3, AX.X, ALU.add))
            step(dve.tensor_scalar(ntile[:, :], ntile[:, :], 1.0, None, ALU.max))
            c3 = cmp[:, 0:NX * NX].rearrange("p (e k) -> p e k", e=NX)
            step(dve.tensor_tensor(c3, ntile[:, :].unsqueeze(1).to_broadcast([P, NX, NX]), le8[:, :, :],
                                   ALU.mult))
            step(dve.tensor_reduce(cumt[:, :], c3, AX.X, ALU.add))
            step(dve.tensor_tensor(base[:, :], cumt[:, :], ntile[:, :], ALU.subtract))
            step(dve.scalar_tensor_tensor(out=ranks[:, :, :],
                                          in0=base[:, :].unsqueeze(1).to_broadcast([P, TILES, NX]),
                                          scalar=float(P), in1=ranks[:, :, :], op0=ALU.mult, op1=ALU.add))
            for k in range(TOPK):
                ins = dve.tensor_tensor(hot[:, k, :, :], hot[:, k, :, :], ranks[:, :, :], ALU.mult)
            step(ins)
            step(dve.tensor_reduce(slotf[:, :, :], hot[:, :, :, :], AX.X, ALU.add))
            step(dve.tensor_copy(slot[:, :, :], slotf[:, :, :]))
            dve.tensor_single_scalar(sdiv[:, :, :], slot[:, :, :], P.bit_length() - 1, ALU.arith_shift_right)
            step(dve.tensor_single_scalar(smod[:, :, :], slot[:, :, :], P - 1, ALU.bitwise_and))
            dve.tensor_copy(sdivf[:, :, :], sdiv[:, :, :])
            step(dve.tensor_copy(smodf[:, :, :], smod[:, :, :]))
            for k in range(TOPK):
                pairs = slice(TILES * k, TILES * k + TILES)
                step(dve.tensor_tensor(hot_f[:, pairs, :],
                                       iota_j[:, :].unsqueeze(1).to_broadcast([P, TILES, SLOT_COLS]),
                                       sdivf[:, k, :].unsqueeze(2).to_broadcast([P, TILES, SLOT_COLS]),
                                       ALU.is_equal))
                dve.tensor_tensor(hot_j[:, pairs, :], hot_f[:, pairs, :],
                                  tok[:, :].unsqueeze(2).to_broadcast([P, TILES, SLOT_COLS]), ALU.mult)
                for q in range(HOT_PARTS):
                    t = slice(HOT_TILES * q, HOT_TILES * q + HOT_TILES)
                    dve.tensor_tensor(hot_p[:, TILES * k + HOT_TILES * q:TILES * k + HOT_TILES * (q + 1), :],
                                      iota128[:, :].unsqueeze(1).to_broadcast([P, HOT_TILES, P]),
                                      smodf[:, k, t].unsqueeze(2).to_broadcast([P, HOT_TILES, P]),
                                      ALU.is_equal).then_inc(hot_ready, 1)
            c3 = cmp[:, :].rearrange("p (j e) -> p j e", e=NX)
            step(dve.tensor_tensor(c3, cumt[:, :].unsqueeze(1).to_broadcast([P, SLOT_TILES, NX]),
                                   iota_j[:, 0:SLOT_TILES].unsqueeze(2).to_broadcast([P, SLOT_TILES, NX]), ALU.is_le))
            step(dve.tensor_reduce(eidf[:, :], c3, AX.X, ALU.add))
            step(dve.tensor_scalar(eid[:, :], eidf[:, :], float(NX - 1), None, ALU.min))
            dve.tensor_single_scalar(place[:, :], eid[:, :], NW - 1, ALU.bitwise_and)
            dve.tensor_copy(cum_i[:, :], cumt[:, :])
            dve.wait_ge(idx_full, 1)
            step(dve.tensor_scalar(padm[:, :], ps[:, 7, 0:SLOT_COLS], 0.0, None, ALU.is_equal))
            step(dve.scalar_tensor_tensor(out=destf[:, :], in0=padm[:, :], scalar=dummy[:, 0:1],
                                          in1=ps[:, 7, 0:SLOT_COLS], op0=ALU.mult, op1=ALU.add))
            step(dve.tensor_scalar(dest[:, :], destf[:, :], -1.0, None, ALU.add))
            dve.tensor_single_scalar(idx[:, :], dest[:, :], B * S - 1, ALU.bitwise_and).then_inc(idx_ready, 1)
            step(dve.tensor_tensor(gsplit[:, 1, :, :], gate[:, :, :].rearrange("p t k -> p k t"),
                                   gsplit[:, 0, :, :].bitcast(F32), ALU.subtract))
            dve.wait_ge(x2_stored, 16 * TILES)
            for k in range(TOPK):
                pairs = slice(TILES * k, TILES * k + TILES)
                for i in range(2):
                    dve.tensor_tensor(hot_g[:, pairs, i, :], hot_f[:, pairs, :],
                                      gsplit[:, i, k, :].bitcast(F32).unsqueeze(2)
                                      .to_broadcast([P, TILES, SLOT_COLS]),
                                      ALU.mult).then_inc(hot_g_ready, 1)
            dve.wait_ge(gates_full, 1)
            step(dve.tensor_copy(glo[:, :], ps[:, 6, SLOT_COLS:2 * SLOT_COLS]))
            dve.tensor_tensor(gslot[:, :], ps[:, 6, 0:SLOT_COLS], glo[:, :], ALU.add).then_inc(gates_ready, 1)
            dve.wait_ge(gates_ready, 1)
            dve.memset(carrier[:, 0:1], 0.0).then_inc(yo_ready, 1)

            def rows_lo(j, r):
                dve.wait_ge(xT_hi, j + 1)
                dve.tensor_tensor(xgTl[:, r % 2, :, :], ps[:, 0, :].rearrange("p (c q) -> p c q", c=EC),
                                  xgTh[:, r % 2, :, :].bitcast(F32), ALU.subtract).then_inc(xT_lo, 1)

            def rows_gu_T(j, r, free):
                dve.wait_ge(guT_full, j + 1)
                if free:
                    dve.wait_ge(down_full, j - 1)
                dve.tensor_copy(guT[:, r % 2, 0:FC - 1, :],
                                ps[:, 3, 0:(FC - 1) * P].rearrange("p (c q) -> p c q", q=P))
                dve.tensor_copy(guT[0:FLAST, r % 2, FC - 1, :], ps[0:FLAST, 3, (FC - 1) * P:FC * P])\
                    .then_inc(guT_ready, 1)

            def gated(j, r, free):
                dve.wait_ge(act_ready, j + 1)
                dve.wait_ge(gate_full, j + 1)
                if free:
                    dve.wait_ge(guT_full, j - 1)
                dve.tensor_tensor(gu[:, r % 2, :], ps[:, 2, 0:F], act[:, r % 2, :], ALU.mult)\
                    .then_inc(gu_ready, 1)

            rows_lo(0, 0)
            for j in range(4):
                if j >= 1:
                    rows_gu_T(j - 1, j - 1, j - 1 >= 2)
                gated(j, j, j >= 2)
                rows_lo(j + 1, (j + 1) % 4)
            with dve.Fori(1, ROUNDS) as i:
                for r in range(4):
                    rows_gu_T(4 * i + r - 1, (r - 1) % 4, True)
                    gated(4 * i + r, r, True)
                    rows_lo(4 * i + r + 1, (r + 1) % 4)
            for j in range(4 * ROUNDS, SLOT_TILES):
                rows_gu_T(j - 1, (j - 1) % 4, True)
                gated(j, j % 4, True)
                if j + 1 < SLOT_TILES:
                    rows_lo(j + 1, (j + 1) % 4)
            rows_gu_T(SLOT_TILES - 1, (SLOT_TILES - 1) % 4, True)

        @block.tensor
        def _(pe):
            def three_pass(dst, parts, n):
                for c in range(n):
                    for i in range(3):
                        lhs, rhs = parts(c, i)
                        mm = pe.matmul(dst, lhs, rhs, start=(c == 0 and i == 0),
                                       stop=(c == n - 1 and i == 2))
                return mm

            def w_of(i, m, c, cols=slice(0, E)):
                return wlo[:, m, c, cols] if i == 2 else whi[:, HI_AT[m], c, cols]

            def transposes(t):
                for c in range(EC):
                    mm = pe.transpose(ps[:, MISC[t], P * c:P * c + P], hn[:, t, P * c:P * c + P], ident[:, :])
                mm.then_inc(misc_full, 1)

            def rows_projection(hi, lo, m, t):
                three_pass(ps[:, MISC[t], :],
                           lambda c, i: ((hi, lo, hi)[i][:, c, P * t:P * t + P], w_of(i, m, c)), EC)\
                    .then_inc(misc_full, 1)

            def project_v(b):
                pe.wait_ge(ht_lo, TB * b + TB)
                for t in range(TB):
                    rows_projection(hTh, hTl, V_, t)

            def project_qk(b, g, emptied):
                for n, m in enumerate((Q_, K_)):
                    if isinstance(b, int) and b == 0 and g == 0:
                        pe.wait_ge(wsplit_lo, m + 1)
                    pe.wait_ge(*emptied[n])
                    cols = slice(P * g, P * g + P)
                    three_pass(ps[:, MISC[n], 0:S],
                               lambda c, i: (w_of(i, m, c, cols), (hTh, hTl, hTh)[i][:, c, :]), EC)\
                        .then_inc(misc_full, 1)

            def project_out(b, t, par):
                if t == 0:
                    pe.wait_ge(ot_lo, GROUPS * b + GROUPS)
                rows_projection(oTh[par], oTl[par], O_, t)

            def qk_read(b, g):
                return (q_ready, GROUPS * b + g + 1), (k_ready, GROUPS * b + g + 1)

            def both(signal, n):
                return (signal, n + 1), (signal, n + 2)

            def score(b, h, par, first):
                g = h // HG
                if h % HG == 0:
                    pe.wait_ge(q_ready, GROUPS * b + g + 1)
                    pe.wait_ge(k_ready, GROUPS * b + g + 1)
                if not (first and h < 2):
                    pe.wait_ge(s_read, H * b + h - 1)
                rows = slice(HD * (h % HG), HD * (h % HG) + HD)
                for t in range(TB):
                    mm = pe.matmul(ps[:, SB[h % 2], P * t:P + 2 * P * t], qT[par][rows, g, P * t:P * t + P],
                                   kT[par][rows, g, 0:P + P * t], start=True, stop=True)
                mm.then_inc(s_full, 1)

            def moved(b, h):
                pe.wait_ge(pt_act if pt_on_act(h) else pt_dve, pt_count(b, h, pt_on_act(h)))

            def probs_T(b, h):
                pe.wait_ge(pn_ready, H * b + h + 1)
                if h >= 2:
                    moved(b, h - 2)
                for i in range(3):
                    mm = pe.transpose(ps[:, PB[h % 2], P * i:P * i + P], sc[:, h % NE, P * i:P * i + P],
                                      ident[:, :])
                mm.then_inc(pt_full, 1)

            def values(b, g, par):
                for h in (HG * g + HG - 2, HG * g + HG - 1):
                    moved(b, h)
                if g == 0:
                    pe.wait_ge(v_ready, TB * b + TB)
                for t in range(TB):
                    for h in range(HG * g, HG * g + HG):
                        o = ps[HD * (h % HG):HD * (h % HG) + HD, OB[h // HB], :]
                        q0 = S * (g % 2)
                        mm = pe.matmul(o[:, q0 + P * t:q0 + S], v[par][:, t, HD * h:HD * h + HD],
                                       pT[:, h % NE, 2 * P * t:2 * P + P * t], start=(t == 0),
                                       stop=(t == TB - 1))
                mm.then_inc(av_done, 1)

            def next_hT(b, emptied):
                pe.wait_ge(ln1["out"], TB * b + TB)
                for t in range(TB):
                    pe.wait_ge(*emptied[t])
                    transposes(t)

            def x1_T(b, emptied):
                pe.wait_ge(ln2["out"], TB * b + TB)
                for t in range(TB):
                    pe.wait_ge(*emptied[t])
                    transposes(t)

            pe.wait_ge(consts, 5)
            pe.wait_ge(ln1["out"], TB)
            for t in range(TB):
                transposes(t)
            pe.wait_ge(wsplit_lo, V_ + 1)
            project_v(0)
            for g in range(GROUPS):
                project_qk(0, g, qk_read(0, g - 1) if g else both(v_ready, 0))
            next_hT(1, qk_read(0, GROUPS - 1))
            pe.wait_ge(wsplit_lo, O_ + 1)

            def turn(b, par, wo=True, proj=True, hT=True):
                for g in range(-2, H // 2 + 1):
                    for h in (2 * g + 4, 2 * g + 5):
                        if h < H:
                            score(b, h, par, not wo)
                    for h in (2 * g, 2 * g + 1):
                        if 0 <= h < H:
                            probs_T(b, h)
                    if g == -1 and proj:
                        project_v(b + 1)
                    if g in (0, 1) and wo:
                        if proj:
                            pe.wait_ge(v_ready, TB * b + TB + g + 1)
                        else:
                            pe.wait_ge(qx_ready, TB * b - 2 * TB + g + 1)
                        project_out(b - 1, g, 1 - par)
                    if g in QK_IN and proj:
                        n = QK_IN[g]
                        if n == 0:
                            emptied = both(x1_ready, TB * b - TB) if wo else both(v_ready, TB * b + TB)
                        elif n == AFTER_X1T and wo:
                            emptied = both(qx_ready, TB * b - TB)
                        else:
                            emptied = qk_read(b + 1, n - 1)
                        project_qk(b + 1, n, emptied)
                    if g == X1T_IN and wo:
                        x1_T(b - 1, qk_read(b + 1, AFTER_X1T - 1) if proj else both(x1_ready, TB * b - TB))
                    if g == HT_IN and hT:
                        next_hT(b + 2, qk_read(b + 1, 3))
                    if g >= 2 and g % 2 == 0:
                        values(b, g // 2 - 1, par)

            run_turns(pe, turn)
            for t in range(TB):
                pe.wait_ge(qx_ready, TB * (B - 2) + t + 1)
                project_out(B - 1, t, 1)
            x1_T(B - 1, both(x1_ready, TB * B - TB))

            def convolve(h, r, free):
                pe.wait_ge(strip_fixed, h + 1)
                pe.wait_ge(kv_ready, h + 1)
                if free:
                    pe.wait_ge(y_read, h - 1)
                for lo in range(EC):
                    for m in range(lo + 1):
                        mm = pe.matmul(convolved(r)[:, B * lo:B * lo + B, 0:PAIRS],
                                       strip[:, r, P * (lo - m):P * (lo - m) + P],
                                       kv[:, r, B * m:B * m + B, :],
                                       start=(m == 0), stop=(m == lo))
                mm.then_inc(y_full, 1)

            pe.wait_ge(x1_ready, TB * B)
            pe.wait_ge(qx_ready, TILES)
            for h in range(KV):
                convolve(h, h, h >= 2)
            with pe.Fori(1, MH // KV) as i:
                for r in range(KV):
                    convolve(KV * i + r, r, True)
            pe.wait_ge(mixed, MH)

            def x2_T(t):
                if t >= 2:
                    pe.wait_ge(x2_ready, t - 1)
                for c in range(EC):
                    mm = pe.transpose(ps[:, t % 2, P * c:P * c + P], QX[:, c, P * t:P * t + P], ident[:, :])
                mm.then_inc(x2T_full, 1)

            def h3_T(t):
                pe.wait_ge(ln3["out"], t + 1)
                if t >= 2:
                    pe.wait_ge(h3T_ready, t - 1)
                for c in range(EC):
                    mm = pe.transpose(ps[:, 2 + t % 2, P * c:P * c + P], h3[:, t % NH, P * c:P * c + P],
                                      ident[:, :])
                mm.then_inc(h3T_full, 1)

            def router(t):
                pe.wait_ge(h3T_ready, t + 1)
                if t % 4 == 0 and t >= 8:
                    pe.wait_ge(lgT_ready, t // 4 - 1)
                q = P * (t % 4)
                for c in range(EC):
                    mm = pe.matmul(ps[0:NX, 5 + t // 4 % 2, q:q + P], wr[:, c, :], h3T[:, t % 2, c, :],
                                   start=(c == 0), stop=(c == EC - 1))
                mm.then_inc(lgT_full, 1)

            def logits_back(q):
                pe.wait_ge(lgT_ready, q + 1)
                for t in range(4 * q, 4 * q + 4):
                    pe.transpose(ps[:, 4, NX * t:NX * t + NX], lgT[:, q % 2, P * (t % 4):P * (t % 4) + P],
                                 ident[0:NX, 0:NX]).then_inc(logits_full, 1)

            for t in range(TILES + 3):
                if t < TILES:
                    x2_T(t)
                if 2 <= t < TILES + 2:
                    h3_T(t - 2)
                if t >= 3:
                    router(t - 3)
                if t % 4 == 0 and t >= 8:
                    logits_back(t // 4 - 2)
            logits_back(TILES // 4 - 1)

            pe.wait_ge(tables, 13)
            pe.wait_ge(picked_ready, 1)
            for back in range(TILES):
                pe.matmul(ps[:, 5, 0:TILES * NX], ones[:, :] if back else upper[:, :],
                          padded[:, TILES - back:2 * TILES - back, :].rearrange("p t e -> p (t e)"),
                          start=(back == 0), stop=(back == TILES - 1))
            pe.matmul(ps[:, 6, 0:NX], ones[:, :].bitcast(F32), cnt[:, :], start=True, stop=True).then_inc(ranks_full, 1)
            for n in range(TOPK * TILES):
                if n % HOT_TILES == 0:
                    pe.wait_ge(hot_ready, n // HOT_TILES + 1)
                mm = pe.matmul(ps[:, 7, 0:SLOT_COLS], hot_p[:, n, :], hot_j[:, n, :],
                               start=(n == 0), stop=(n == TOPK * TILES - 1))
            mm.then_inc(idx_full, 1)
            for n in range(TOPK * TILES):
                if n % TILES == 0:
                    pe.wait_ge(hot_g_ready, 2 * (n // TILES) + 2)
                mm = pe.matmul(ps[:, 6, 0:2 * SLOT_COLS], hot_p[:, n, :],
                               hot_g[:, n, :, :].rearrange("p i j -> p (i j)"),
                               start=(n == 0), stop=(n == TOPK * TILES - 1))
            mm.then_inc(gates_full, 1)

            pe.wait_ge(idx_ready, 1)
            def ring_place(j):
                return pe.value_load(place[0:1, bass.ds(j, 1)], min_val=0, max_val=NW - 1)

            def rows_T(j, r, free):
                pe.wait_ge(gathered[r], 4 * (j - r) + 16)
                if free:
                    pe.wait_ge(xT_lo, j)
                for c in range(EC):
                    mm = pe.transpose(ps[:, 0, P * c:P * c + P], xg[:, r, P * c:P * c + P], ident[:, :])
                mm.then_inc(xT_full, 1)

            def up(r, e, m, bank_w, full):
                for c in range(EC):
                    for i, (rows, part) in enumerate(((xgTh, 0), (xgTh, 1), (xgTl, 0))):
                        mm = pe.matmul(ps[:, bank_w, 0:F], rows[:, r % 2, c, :],
                                       whl[:, bass.ds(e, 1), m, part, F * c:F * c + F].squeeze(1),
                                       start=(c == 0 and i == 0), stop=(c == EC - 1 and i == 2))
                mm.then_inc(full, 1)

            def hidden_T(j, r, free):
                pe.wait_ge(gu_ready, j + 1)
                if free:
                    pe.wait_ge(guT_ready, j)
                for c in range(FC):
                    k = P if c < FC - 1 else FLAST
                    mm = pe.transpose(ps[0:k, 3, P * c:P * c + P], gu[:, r % 2, P * c:P * c + k], ident[:, :])
                mm.then_inc(guT_full, 1)

            def down(j, r, e, free):
                pe.wait_ge(guT_ready, j + 1)
                if free:
                    pe.wait_ge(yo_ready, j - 1)
                for c in range(FC):
                    k = P if c < FC - 1 else FLAST
                    mm = pe.matmul(ps[:, 4 + r % 2, :], guT[0:k, r % 2, c, :],
                                   wd[0:k, bass.ds(e, 1), c, :].squeeze(1), start=(c == 0), stop=(c == FC - 1))
                mm.then_inc(down_full, 1)

            def expert_tile(j, r, first=False, last=False):
                expert = pe.value_load(eid[0:1, bass.ds(j, 1)], min_val=0, max_val=NX - 1)
                e = ring_place(j)
                pe.wait_ge(w_loaded, 16 * PIECES * expert + 16 * PIECES)
                pe.wait_ge(xT_lo, j + 1)
                if not first:
                    pe.wait_ge(act_ready, j)
                up(r, e, 0, 1, up_full)
                if not first:
                    hidden_T(j - 1, (r - 1) % 4, not (isinstance(j, int) and j == 1))
                    pe.wait_ge(gu_ready, j)
                up(r, e, 1, 2, gate_full)
                if not last:
                    rows_T(j + 1, (r + 1) % 4, True)
                if not first:
                    down(j - 1, (r - 1) % 4, ring_place(j - 1), not (isinstance(j, int) and j <= 2))

            rows_T(0, 0, False)
            for j in range(4):
                expert_tile(j, j, first=(j == 0))
            with pe.Fori(1, ROUNDS) as i:
                for r in range(4):
                    expert_tile(4 * i + r, r)
            for j in range(4 * ROUNDS, SLOT_TILES):
                expert_tile(j, j % 4, last=(j == SLOT_TILES - 1))
            hidden_T(SLOT_TILES - 1, (SLOT_TILES - 1) % 4, True)
            down(SLOT_TILES - 1, (SLOT_TILES - 1) % 4, ring_place(SLOT_TILES - 1), True)

        return nc


def kernel(**inputs):
    import numpy as _np
    import concourse.bacc as _bacc
    from concourse.bass_utils import run_bass_kernel_spmd as _run

    arrays = laid_out(inputs)
    nc = _bacc.Bacc("TRN2", target_bir_lowering=False, num_devices=1)
    args = [nc.dram_tensor(n, a.shape, mybir.dt.from_np(a.dtype), kind="ExternalInput").ap()
            for n, a in arrays.items()]
    out = nc.dram_tensor("out", (B, S, E), F32, kind="ExternalOutput").ap()
    decoder_block(nc, *args, out)
    r = _run(nc, [arrays], core_ids=[0])
    return r.results[0]["out"]


def laid_out(inputs):
    import numpy as np
    g = {k: np.asarray(v) for k, v in inputs.items()}

    def chunks(w):
        return w.reshape(-1, P, w.shape[-1]).transpose(1, 0, 2)

    def experts(w):
        n = -(-w.shape[1] // P) * P
        w = np.concatenate([w, np.zeros((w.shape[0], n - w.shape[1], w.shape[2]), w.dtype)], 1)
        return w.reshape(w.shape[0], -1, P, w.shape[2]).transpose(2, 0, 1, 3)

    w_attn = np.stack([chunks(g[f"L0_attn_W{m}"].T) for m in "vqko"])
    b_qkv = np.stack([g[f"L0_attn_b{m}"].reshape(-1, P).T for m in "qkv"], 1)
    c = g["ctx_2048"].transpose(2, 0, 1).reshape(EC, P, B, S)[:, ::-1]
    c = c.transpose(1, 0, 2, 3).reshape(P, EC * B, MH, MD)
    ctx_rev = np.concatenate([c, c[..., :MW - MD]], -1)
    kern = g["L0_xattn_ssm_kernel"]
    kern_pad = np.concatenate([np.zeros((MH, P - 1), kern.dtype), kern], 1)
    out = {
        "x": g["x"], "w_attn": w_attn, "b_qkv": b_qkv, "b_o": g["L0_attn_bo"],
        "ctx_rev": ctx_rev, "kern_pad": kern_pad, "skip_d": g["L0_xattn_D"],
        "w_router": chunks(g["L0_ffn_w_router"].T),
        "w_up": experts(g["L0_ffn_w1"].transpose(0, 2, 1)),
        "w_gate": experts(g["L0_ffn_w3"].transpose(0, 2, 1)),
        "w_down": experts(g["L0_ffn_w2"].transpose(0, 2, 1)),
    }
    return {k: np.ascontiguousarray(a) for k, a in out.items()}
```
